# Optimizing a Trainium2 kernel written in Bass

```python
import numpy as np
import jax
import jax.numpy as jnp

def _softmax(x, axis=-1):
    return jax.nn.softmax(x, axis=axis)

def _gelu(x):
    return jax.nn.gelu(x, approximate=True)

def _silu(x):
    return jax.nn.silu(x)

def _sigmoid(x):
    return jax.nn.sigmoid(x)

def _layernorm(x, axis=-1, eps=1e-05):
    m = jnp.mean(x, axis=axis, keepdims=True)
    v = jnp.var(x, axis=axis, keepdims=True)
    return (x - m) / jnp.sqrt(v + eps)

def _scatter_add(tgt, idx, src, axis=0):
    return tgt.at[idx].add(src)

def _segment_sum(src, seg, n):
    return jax.ops.segment_sum(src, seg, n)
kernel_name = 'mk_gnn_ffn_d1_gnn_r8_402da1'

def setup_inputs(seed: int=0):
    np.random.seed(seed)
    _w = jnp.asarray

    def _rec_inputs():
        import jax
        import jax.numpy as jnp
        _gk = jax.random.key(seed)
        x = -0.0002117 + 1 * jax.random.normal(jax.random.fold_in(_gk, 1), (12500, 256), jnp.float32)
        src = jax.random.randint(jax.random.fold_in(_gk, 2), (200000,), 0, 12500, jnp.int32)
        dst = jnp.minimum((12500 * jax.random.uniform(jax.random.fold_in(_gk, 3), (200000,)) ** 2.0).astype(jnp.int32), 99999)
        _o = jnp.argsort(dst, stable=True)
        src = src[_o]
        dst = dst[_o]
        return (x, src, dst)
    x, src, dst = _rec_inputs()

    def _L0_gnn_setup():
        import jax, jax.numpy as jnp
        import numpy as np
        MEM_LEN = 12500
        Z_DIM = 256
        K = 7
        NUM_EDGES = 62500
        key = jax.random.key(seed)
        k1, k2, k3, k4, k5 = jax.random.split(key, 5)
        mems = jax.random.normal(k1, (MEM_LEN, Z_DIM), dtype=jnp.float32)
        r = jax.random.normal(k2, (1, Z_DIM), dtype=jnp.float32)
        W = jax.random.normal(k3, (Z_DIM, Z_DIM), dtype=jnp.float32) / np.sqrt(Z_DIM)
        y = jax.random.randint(k4, (1,), 0, MEM_LEN, dtype=jnp.int32)
        edge_index = jax.random.randint(k5, (2, NUM_EDGES), 0, MEM_LEN, dtype=jnp.int32)
        return {'mems': mems, 'r': r, 'W': W, 'y': y, 'edge_index': edge_index}
    _L0_gnn_all = _L0_gnn_setup()
    _L0_gnn_in = {k: v for k, v in _L0_gnn_all.items() if k in ('r', 'W', 'y')}
    del _L0_gnn_all

    def _L0_ffn_setup():
        import math
        import jax, jax.numpy as jnp
        import numpy as np
        CAPACITY_FACTOR = 1.25
        key = jax.random.key(seed)
        ks = jax.random.split(key, 5)
        B, L, D, F, E = (8, 1024, 256, 1024, 8)
        h = jax.random.normal(ks[0], (B, L, D), dtype=jnp.float32)
        gate_w = jax.random.normal(ks[1], (D, E), dtype=jnp.float32) * 0.02
        gate_b = jnp.zeros((E,), dtype=jnp.float32)
        w1 = jax.random.normal(ks[2], (E, D, F), dtype=jnp.float32) * (1.0 / math.sqrt(D))
        b1 = jnp.zeros((E, F), dtype=jnp.float32)
        w2 = jax.random.normal(ks[3], (E, F, D), dtype=jnp.float32) * (1.0 / math.sqrt(F))
        b2 = jnp.zeros((E, D), dtype=jnp.float32)
        return {'h': h, 'gate_w': gate_w, 'gate_b': gate_b, 'w1': w1, 'b1': b1, 'w2': w2, 'b2': b2}
    _L0_ffn_all = _L0_ffn_setup()
    _L0_ffn_in = {k: v for k, v in _L0_ffn_all.items() if k in ('gate_w', 'gate_b', 'w1', 'b1', 'w2', 'b2')}
    del _L0_ffn_all
    return {'x': x, 'src': src, 'dst': dst, 'L0_gnn_r': _L0_gnn_in['r'], 'L0_gnn_W': _L0_gnn_in['W'], 'L0_gnn_y': _L0_gnn_in['y'], 'L0_ffn_gate_w': _L0_ffn_in['gate_w'], 'L0_ffn_gate_b': _L0_ffn_in['gate_b'], 'L0_ffn_w1': _L0_ffn_in['w1'], 'L0_ffn_b1': _L0_ffn_in['b1'], 'L0_ffn_w2': _L0_ffn_in['w2'], 'L0_ffn_b2': _L0_ffn_in['b2']}

def reference(x, src, dst, L0_gnn_r, L0_gnn_W, L0_gnn_y, L0_ffn_gate_w, L0_ffn_gate_b, L0_ffn_w1, L0_ffn_b1, L0_ffn_w2, L0_ffn_b2):
    import jax
    import jax.numpy as jnp

    def _L0_gnn_ref(mems, r, W, y, edge_index):
        import jax, jax.numpy as jnp
        import numpy as np
        MEM_LEN = 12500
        Z_DIM = 256
        K = 7
        NUM_EDGES = 62500
        'DTM.write(y, r): scatter-write -> edge mask -> kNN rebuild -> GCNConv.\n            Returns the new memory matrix [MEM_LEN, Z_DIM].'
        yi = y[0]
        mems2 = mems.at[yi].set(r[0])
        keep_w = (edge_index[1] != yi).astype(mems.dtype)
        d2 = jnp.sum(jnp.square(mems2 - r), axis=-1)
        _, nbr = jax.lax.top_k(-d2, K)
        row = jnp.concatenate([edge_index[0], nbr])
        col = jnp.concatenate([edge_index[1], jnp.full((K,), yi, dtype=edge_index.dtype)])
        w = jnp.concatenate([keep_w, jnp.ones((K,), dtype=mems.dtype)])
        SELF_LOOP_W = 2.0
        deg = jax.ops.segment_sum(w, col, num_segments=MEM_LEN) + SELF_LOOP_W
        dinv = jax.lax.rsqrt(deg)
        norm = dinv[row] * w * dinv[col]
        xw = mems2 @ W
        msg = norm[:, None] * xw[row]
        out = jax.ops.segment_sum(msg, col, num_segments=MEM_LEN)
        out = out + (SELF_LOOP_W * dinv * dinv)[:, None] * xw
        return out

    def _L0_ffn_ref(h, gate_w, gate_b, w1, b1, w2, b2):
        import math
        import jax, jax.numpy as jnp
        import numpy as np
        CAPACITY_FACTOR = 1.25
        B, L, D = h.shape
        E = gate_w.shape[1]
        T = B * L
        C = max(1, math.ceil(CAPACITY_FACTOR * T / E))
        x = h.reshape(T, D)
        logits = x @ gate_w + gate_b
        probs = jax.nn.softmax(logits, axis=-1)
        idx = jnp.argmax(probs, axis=-1)
        prb = jnp.take_along_axis(probs, idx[:, None], axis=1)[:, 0]
        one_hot = jax.nn.one_hot(idx, E, dtype=jnp.float32)
        pos = (jnp.cumsum(one_hot, axis=0) * one_hot).sum(-1).astype(jnp.int32) - 1
        kept = pos < C
        pos_safe = jnp.where(kept, pos, C)
        buf = jnp.zeros((E, C, D), dtype=h.dtype).at[idx, pos_safe].set(x, mode='drop')
        hmid = jax.nn.relu(jnp.einsum('ecd,edf->ecf', buf, w1) + b1[:, None, :])
        ybuf = jnp.einsum('ecf,efd->ecd', hmid, w2) + b2[:, None, :]
        pos_g = jnp.minimum(pos, C - 1)
        y_tok = ybuf[idx, pos_g] * (prb * kept)[:, None]
        y = y_tok.reshape(B, L, D)
        y = jnp.nan_to_num(y, nan=0.0, posinf=10000.0, neginf=-10000.0)
        return y
    edge_index = jnp.stack([src, dst])
    x = x + _L0_gnn_ref(_layernorm(x, axis=-1), L0_gnn_r, L0_gnn_W, L0_gnn_y, edge_index)
    x = x + _L0_ffn_ref(_layernorm(x, axis=-1)[None], L0_ffn_gate_w, L0_ffn_gate_b, L0_ffn_w1, L0_ffn_b1, L0_ffn_w2, L0_ffn_b2)[0]
    return x

_drawn_inputs = setup_inputs


def setup_inputs(seed=0):
    import zlib

    import numpy as np

    out = dict(_drawn_inputs(seed))
    spreads = {'L0_ffn_gate_b': (0.0, 0.1), 'L0_ffn_b1': (0.0, 0.633), 'L0_ffn_b2': (0.0, 0.446)}
    factors = {'L0_gnn_r': 8.0}
    for name, (base, spread) in spreads.items():
        noise = np.random.default_rng([zlib.crc32(name.encode()), seed]).standard_normal(out[name].shape)
        drawn = base * np.exp(spread * noise) if base else spread * noise
        out[name] = jnp.asarray(drawn.astype(out[name].dtype))
    for name, factor in factors.items():
        out[name] = (out[name] * factor).astype(out[name].dtype)
    return out
```

```python
import concourse.bass as bass
from concourse import mybir
from contextlib import ExitStack

F32, I32, BF16 = mybir.dt.float32, mybir.dt.int32, mybir.dt.bfloat16
ALU = mybir.AluOpType
ACT = mybir.ActivationFunctionType
AX = mybir.AxisListType

P = 128
STOP_AT = None


def build(nc, x, src, dst, gnn_r, gnn_w, yidx, gate_w, gate_b, w1, b1, w2, b2, out, dbg=None):
    N, D = x.shape
    E = src.shape[0]
    KD = D // P
    NW = -(-N // P)
    LAST = N - (NW - 1) * P
    EPS = 1e-5
    TOPK = 7
    SELF_W = 2.0
    GT = 4
    TILES = -(-E // (P * 16)) * 16
    GROUPS = TILES // GT
    EB = -(-TILES // P)
    FULL = E // P
    FB = FULL // P
    PAD_DST = 16384
    FAR = 1048576.0
    TOP_BASE = float((NW - 1) * P)
    HSTEPS = TILES // 16
    GS = 8
    PAIRS = NW // 2
    ZC = 14
    NZC = NW // ZC
    NE = gate_w.shape[1]
    F = w1.shape[2]
    FT = F // P
    CAP = max(1, -(-N * 5 // (4 * NE)))
    SLOTS = NE * CAP
    NCH = -(-CAP // 512)
    CHUNKS = [(c, min(512, CAP - c)) for c in range(0, CAP, 512)]
    ARENA = 20096

    ctx = ExitStack()
    with ctx:
        def sb(name, shape, dt=F32):
            return ctx.enter_context(nc.sbuf_tensor(name, shape, dt))

        def sem(name):
            return ctx.enter_context(nc.semaphore(name))

        def dram(name, shape, dt=F32):
            return nc.dram_tensor(name, shape, dt, kind="Internal").ap()

        bank = [ctx.enter_context(nc.psum_tensor(f"bank{i}", [P, 512], F32)) for i in range(8)]

        z_table = dram("z_table", [NW * P, D])
        xs = dram("xs", [SLOTS, D])
        ys = dram("ys", [SLOTS, D])

        nodes = sb("nodes", [P, KD, NW, P])
        agg = nodes[:, :, :, :].rearrange("p k w c -> p k (w c)")

        iota_i = sb("iota_i", [P, P], I32)
        iota_b = sb("iota_b", [P, P], BF16)
        ident = sb("ident", [P, P])
        two_ident = sb("two_ident", [P, P])
        ones = sb("ones", [P, P])
        tri = sb("tri", [P, P])
        zeros = sb("zeros", [P, D])
        neg_half = sb("neg_half", [P, NW])
        node_i = sb("node_i", [P, NW], I32)
        node_id = sb("node_id", [P, NW])
        win_i = sb("win_i", [P, NW], I32)
        win_f = sb("win_f", [P, NW])
        rep_rel = sb("rep_rel", [P, GT], BF16)

        r_rows = sb("r_rows", [P, D])
        y_i = sb("y_i", [P, 1], I32)
        y_f = sb("y_f", [P, 1])
        wy_i = sb("wy_i", [P, 1], I32)
        is_y = sb("is_y", [P, NW])
        not_y = sb("not_y", [P, NW])
        invalid = sb("invalid", [P, NW])

        arena = sb("arena", [P, ARENA])
        at = [0]

        def carve(shape, dt=F32):
            size = 1
            for n in shape:
                size *= n
            words = size if dt != BF16 else size // 2
            flat = arena[:, at[0]:at[0] + words]
            at[0] += words
            assert at[0] <= ARENA, (at[0], ARENA)
            if dt != F32:
                flat = flat.bitcast(dt)
            if len(shape) == 1:
                return flat
            names = "abcd"[:len(shape)]
            return flat.rearrange(f"p ({' '.join(names)}) -> p {' '.join(names)}", **dict(zip(names[1:], shape[1:])))

        gath = carve([GS, GT, D])
        at[0] = 0
        HALF = 2 * EB * P
        stage_i = carve([2, EB, P], I32)
        stage_f = carve([2, EB, P])
        grp_min = carve([GROUPS])[0:1, :]
        grp_max = carve([GROUPS])[0:1, :]
        at[0] = 0
        dst_i = carve([EB * P], I32)
        low_i = carve([EB * P], I32)
        lim_row = carve([2, EB * P])[0:1, :, :]
        at[0] = GS * GT * D
        src_idx = carve([EB * P], I32)
        dst_f = carve([EB * P])
        lo_b = carve([EB * P], BF16)
        hi_b = carve([EB * P], BF16)
        rel_b = carve([EB * P], BF16)
        here = at[0]
        oh_lo = carve([2, 16, P], BF16)
        oh_hi = carve([2, 16, NW], BF16)
        at[0] = here
        stage_f2 = carve([EB, P])
        at[0] = here
        near_row = carve([8 * P])[0:1, :]
        at[0] = here
        sel = carve([2, GT, P])
        at[0] = here + (2 * 16 * (P + NW)) // 2
        junk = carve([2, KD, P])
        diff = carve([2, KD, P])
        z_stat = carve([2, KD, P])
        idx_ring = carve([2, 16], I32)

        at[0] = here + (2 * 16 * (P + NW)) // 2
        grp_far = carve([GROUPS])

        at[0] = 0
        w1_sb = carve([2, KD, F])
        w2_sb = carve([2, FT, D])
        b2_rows = carve([NE, D])
        gnnw_sb = carve([KD, D])
        gatew_sb = carve([KD, NE])
        b1_cols = carve([NE * FT])
        turn = at[0]
        x_tile = carve([2, D])
        agg_stat = carve([2, KD, P])
        h_tile = carve([2, KD, P])
        h_feat = carve([2, KD, P])
        bn = carve([NW, 6])
        gate_l = carve([NW, NE])
        gate_e = carve([NW, NE])
        gate_t = carve([NW, NE])
        pick = carve([NW, NE])
        b1_rows = carve([P])
        at[0] = turn
        h_send = carve([ZC, D])
        send_idx = carve([2, ZC // 2], I32)
        at[0] = turn
        xs_rows = carve([2, 4, D])
        xs_feat = carve([2, KD, 512])
        hid = carve([FT, 512])
        y_tile = carve([4, D])
        at[0] = turn
        y_got = carve([ZC, D])
        y_gated = carve([2, D])
        y_clip = carve([2, D])
        y_low = carve([2, D])
        y_fin = carve([2, D], I32)
        o_tile = carve([2, D])
        take_idx = carve([2, ZC // 2], I32)

        tile_lim = sb("tile_lim", [P, 2, EB])
        grp_base = sb("grp_base", [1, GROUPS])
        grp_bad = sb("grp_bad", [1, GROUPS])
        grp_cmp = sb("grp_cmp", [1, GROUPS])
        base_i = sb("base_i", [1, GROUPS], I32)
        bad_sum = sb("bad_sum", [1, 1])
        bad_i = sb("bad_i", [1, 1], I32)
        mine_y = sb("mine_y", [P, 1])
        r_y = sb("r_y", [P, D])
        EDGE_TURNS = [(i, b, min(4, EB - b)) for i in range(2) for b in range(0, EB, 4)]
        LIM_TURNS = EDGE_TURNS

        neg_mean = sb("neg_mean", [P, NW])
        sq_sum = sb("sq_sum", [P, NW])
        rstd = sb("rstd", [P, NW])
        shift = sb("shift", [P, NW])
        dist = sb("dist", [P, NW])
        deg = sb("deg", [P, NW])
        dinv = sb("dinv", [P, NW])

        near = sb("near", [P, NW])
        near8 = sb("near8", [P, 8])
        top8 = sb("top8", [1, 8])
        thr = sb("thr", [P, 1])
        above = sb("above", [P, NW])
        tied = sb("tied", [P, NW])
        n_above = sb("n_above", [P, 1])
        room = sb("room", [P, 1])
        tie_scan = sb("tie_scan", [P, NW])
        tie_rank = sb("tie_rank", [P, NW])
        chosen = sb("chosen", [P, NW])

        col_fix = sb("col_fix", [P, KD])

        mean2 = sb("mean2", [P, NW])
        var2 = sb("var2", [P, NW])
        gap2 = sb("gap2", [P, NW])
        rstd2 = sb("rstd2", [P, NW])
        shift2 = sb("shift2", [P, NW])
        best = sb("best", [P, NW])
        norm = sb("norm", [P, NW])
        expert = sb("expert", [P, NW])
        place = sb("place", [P, NW])
        kept = sb("kept", [P, NW])
        weight = sb("weight", [P, NW])
        slot_f = sb("slot_f", [P, NW])
        put_idx = sb("put_idx", [P, NW], I32)
        get_idx = sb("get_idx", [P, NW], I32)
        rank_e = sb("rank_e", [P, NE])
        iota_f = sb("iota_f", [P, NE])
        gateb_sb = sb("gateb_sb", [1, NE])

        S = {}
        for name in ("""edges_cleared edges_in x_in r_in y_in consts edges_float edge_psum edges_out  
                     lims limps lim_rows bases cmp_ps pre hist_built hist_used hist_ps mean_sum ssum  
                     rstd_ok shift_ok mem_ok mem_patched diff_ok dist_ok deg_ok z_ok table_out  
                     tick near_ok near_ps chosen_ok zstat_ok zT_ps agg_init selps fix_saved  
                     idx_ok sel_ok agg_ps agg_added fixed tick3 rep_idx rep_got rep_free rep_relok rep_sel rep_ps rep_added rep_bad rep_dst tick2 clean bn_ok zeroed xs_zero w_small w_in0 w_in1 xt_in0 xt_in1 aggst_ok conv_ps x1_ok var_ok lnb_ok h_ok hT_ps
                     hT_ok logit_ps gate_in gate_out pick_ok rank_ps routed send_h sidx sent0 sent1 xs_in0 xs_in1 xT_ps xT_ok
                     l1_ps hid_ok l2_ps y_ok ys_out0 ys_out1 ys_out2 ys_out3 tidx got0 got1 gated_ok o_ok
                     out_done0 out_done1 b1_ps b1_ok fin_ch act_ch dve_ch pool_ch hist_start""").split():
            S[name] = sem(name)
        gathered = [sem(f"gathered{i}") for i in range(GS)]

        def tally(name):
            return [S[name], 0]

        block = ctx.enter_context(nc.Block())

        x_win = x[0:(NW - 1) * P, :].rearrange("(w p) (k c) -> p k w c", p=P, k=KD)
        x_last = x[(NW - 1) * P:N, :].rearrange("p (k c) -> p k c", k=KD)
        z_win = z_table.rearrange("(w p) (k c) -> p k w c", p=P, k=KD)

        @block.sync
        def _(sp):
            for i, e in enumerate((dst, src)):
                sp.dma_start(stage_i[:, i, 0:FB, :],
                             e[0:FB * P * P].rearrange("(b r e) -> r b e", r=P, e=P)).then_inc(S["edges_in"], 16)
            sp.wait_ge(S["edges_cleared"], 2)
            for i, e in enumerate((dst, src)):
                rows = FULL - FB * P
                sp.dma_start(stage_i[0:rows, i, FB, :],
                             e[FB * P * P:FULL * P].rearrange("(r e) -> r e", e=P)).then_inc(S["edges_in"], 16)
                sp.dma_start(stage_i[rows:rows + 1, i, FB, 0:E - FULL * P],
                             e[FULL * P:E].rearrange("(r e) -> r e", r=1)).then_inc(S["edges_in"], 16)
            sp.dma_start(y_i[:, :], yidx.rearrange("(a b) -> a b", a=1).to_broadcast([P, 1])).then_inc(S["y_in"], 16)
            sp.dma_start(r_rows[:, :], gnn_r.to_broadcast([P, D])).then_inc(S["r_in"], 16)
            for c in range(NZC):
                a, b = c * ZC, min((c + 1) * ZC, NW - 1)
                for k in range(KD):
                    sp.dma_start(nodes[:, k, a:b, :], x_win[:, k, a:b, :]).then_inc(S["x_in"], 16)
            sp.wait_ge(S["edges_cleared"], 3)
            sp.dma_start(nodes[0:LAST, :, NW - 1, :], x_last).then_inc(S["x_in"], 16)

            sp.wait_ge(S["zeroed"], 1)
            sp.dma_start(xs.rearrange("(p a) d -> p a d", p=16),
                         zeros[0:16, :].unsqueeze(1).to_broadcast([16, SLOTS // 16, D])).then_inc(S["xs_zero"], 16)

            for c in range(NZC):
                sp.wait_ge(S["z_ok"], c + 1)
                for k in range(KD):
                    sp.dma_start(z_win[:, k, c * ZC:(c + 1) * ZC, :],
                                 nodes[:, k, c * ZC:(c + 1) * ZC, :]).then_inc(S["table_out"], 16)

            def load_weights(e, j, small=False):
                sp.dma_start(w1_sb[:, j, :, :], w1[bass.ds(e, 1), :, :].rearrange("o (k p) f -> p (o k) f", p=P)).then_inc(S[f"w_in{j}"], 16)
                sp.dma_start(w2_sb[:, j, :, :], w2[bass.ds(e, 1), :, :].rearrange("o (t p) d -> p (o t) d", p=P)).then_inc(S[f"w_in{j}"], 16)

            sp.wait_ge(S["fixed"], 1)
            sp.dma_start(gnnw_sb, gnn_w.rearrange("(k p) d -> p k d", p=P)).then_inc(S["w_small"], 16)
            sp.dma_start(gatew_sb, gate_w.rearrange("(k p) e -> p k e", p=P)).then_inc(S["w_small"], 16)
            sp.dma_start(gateb_sb[:, :], gate_b.rearrange("(o e) -> o e", o=1)).then_inc(S["w_small"], 16)
            sp.dma_start(b1_rows[0:NE * FT, :], b1.rearrange("e (t c) -> (e t) c", c=P)).then_inc(S["w_small"], 16)
            sp.dma_start(b2_rows, b2.rearrange("(o e) d -> o e d", o=1).to_broadcast([P, NE, D])).then_inc(S["w_small"], 16)

            def load_x(w, j):
                sp.dma_start(x_tile[:, j, :], x[bass.ds(w * P, P), :]).then_inc(S[f"xt_in{j}"], 16)
            load_x(0, 0)
            load_x(1, 1)
            with sp.Fori(1, PAIRS - 1) as q:
                for j in range(2):
                    sp.wait_ge(S["x1_ok"], q * 2 + (j - 1))
                    load_x(q * 2 + j, j)
            sp.wait_ge(S["x1_ok"], NW - 3)
            load_x(NW - 2, 0)
            sp.wait_ge(S["x1_ok"], NW - 2)
            sp.dma_start(x_tile[0:LAST, 1, :], x[(NW - 1) * P:N, :]).then_inc(S["xt_in1"], 16)
            load_weights(0, 0)
            load_weights(1, 1)

            def load_chunk(e, c, slot):
                c0, n = CHUNKS[c]
                full = n // P
                sp.dma_start(xs_rows[:, slot, 0:full, :],
                             xs[bass.ds(e * CAP + c0, full * P), :].rearrange("(t p) d -> p t d", p=P)).then_inc(S[f"xs_in{slot}"], 16)
                if n % P:
                    sp.dma_start(xs_rows[0:n % P, slot, full:full + 1, :],
                                 xs[bass.ds(e * CAP + (c0 + full * P), n % P), :].rearrange("(t p) d -> p t d", t=1)).then_inc(S[f"xs_in{slot}"], 16)
                else:
                    sp.sem_inc(S[f"xs_in{slot}"], 16)

            def expert_pair(q, last):
                for j in range(2):
                    e = q * 2 + j
                    for c in range(NCH):
                        s = j * NCH + c
                        more = s + 2
                        if not (last and more >= 2 * NCH):
                            sp.wait_ge(S["xT_ps"], q * (2 * NCH) + s + 1)
                            load_chunk(q * 2 + more // NCH, more % NCH, s % 2)
                        for t in range(4):
                            n = min(P, CHUNKS[c][1] - t * P)
                            sp.wait_ge(S["y_ok"], q * (8 * NCH) + (4 * s + t + 1))
                            sp.dma_start(ys[bass.ds(e * CAP + (CHUNKS[c][0] + t * P), n), :], y_tile[0:n, t, :]).then_inc(S[f"ys_out{t}"], 16)
                    if not last:
                        load_weights(e + 2, j)
            sp.wait_ge(S["sent0"], 16 * ZC // 2 * NZC)
            sp.wait_ge(S["sent1"], 16 * ZC // 2 * NZC)
            load_chunk(0, 0, 0)
            load_chunk(0, 1, 1)
            with sp.Fori(0, NE // 2 - 1) as q:
                expert_pair(q, False)
            expert_pair(NE // 2 - 1, True)

            with sp.Fori(0, PAIRS - 1) as q:
                for j in range(2):
                    sp.wait_ge(S["o_ok"], q * 2 + j + 1)
                    sp.dma_start(out[bass.ds((q * 2 + j) * P, P), :], o_tile[:, j, :]).then_inc(S[f"out_done{j}"], 16)
            for j, n in ((0, P), (1, LAST)):
                sp.wait_ge(S["o_ok"], NW - 1 + j)
                sp.dma_start(out[(NW - 2 + j) * P:(NW - 2 + j) * P + n, :], o_tile[0:n, j, :]).then_inc(S[f"out_done{j}"], 16)
            for j in range(2):
                sp.wait_ge(S[f"out_done{j}"], 16 * PAIRS)
            for t in range(4):
                sp.wait_ge(S[f"ys_out{t}"], 16 * NE * NCH)

        @block.gpsimd
        def _(pool):
            nc.gpsimd.memset(stage_i[:, 0, FB, :], PAD_DST).then_inc(S["edges_cleared"], 1)
            nc.gpsimd.memset(stage_i[:, 1, FB:EB, :], 0).then_inc(S["edges_cleared"], 1)
            pool.wait_ge(S["edges_cleared"], 2)
            nc.gpsimd.memset(nodes[64:P, :, NW - 1, :], 0.0).then_inc(S["edges_cleared"], 1)
            pool.wait_ge(S["edges_cleared"], 3)
            nc.gpsimd.iota(iota_i[:, :], [[1, P]], base=0, channel_multiplier=0).then_inc(S["pool_ch"], 1)
            nc.gpsimd.iota(node_i[:, :], [[P, NW]], base=0, channel_multiplier=1).then_inc(S["pool_ch"], 1)
            nc.gpsimd.iota(win_i[:, :], [[P, NW]], base=0, channel_multiplier=0).then_inc(S["pool_ch"], 1)
            nc.gpsimd.memset(zeros[:, :], 0.0).then_inc(S["pool_ch"], 1)
            nc.gpsimd.memset(ones[:, :], 1.0).then_inc(S["pool_ch"], 1)
            nc.gpsimd.memset(neg_half[:, :], -0.5).then_inc(S["pool_ch"], 1)
            pool.wait_ge(S["pool_ch"], 6)
            pool.sem_inc(S["zeroed"], 1)
            nc.gpsimd.tensor_copy(iota_b[:, :], iota_i[:, :]).then_inc(S["consts"], 1)
            nc.gpsimd.tensor_copy(node_id[:, :], node_i[:, :]).then_inc(S["consts"], 1)
            nc.gpsimd.tensor_copy(win_f[:, :], win_i[:, :]).then_inc(S["consts"], 1)
            for m, v in ((ident, 1.0), (two_ident, SELF_W)):
                nc.gpsimd.affine_select(out=m[:, :], in_=zeros[:, 0:P], compare_op=ALU.not_equal, fill=v,
                                        base=0, pattern=[[-1, P]], channel_multiplier=1).then_inc(S["consts"], 1)
            nc.gpsimd.affine_select(out=tri[:, :], in_=ones[:, :], compare_op=ALU.is_ge, fill=0.0,
                                    base=0, pattern=[[1, P]], channel_multiplier=-1).then_inc(S["consts"], 1)

            pool.wait_ge(S["ssum"], 1)
            pool.wait_ge(S["pre"], 1)
            nc.gpsimd.tensor_scalar(rstd[:, :], sq_sum[:, :], 1.0 / D, EPS, ALU.mult, ALU.add).then_inc(S["pool_ch"], 1)
            pool.wait_ge(S["pool_ch"], 7)
            nc.gpsimd.tensor_tensor(rstd[:, :], rstd[:, :], neg_half[:, :], ALU.pow).then_inc(S["pool_ch"], 1)
            pool.wait_ge(S["pool_ch"], 8)
            nc.gpsimd.tensor_tensor(rstd[:, :], rstd[:, :], not_y[:, :], ALU.mult).then_inc(S["pool_ch"], 1)
            pool.wait_ge(S["pool_ch"], 9)
            nc.gpsimd.tensor_tensor(shift[:, :], rstd[:, :], neg_mean[:, :], ALU.mult).then_inc(S["shift_ok"], 1)

            pool.wait_ge(S["mem_ok"], 1)
            wy = pool.value_load(wy_i[0:1, 0:1], min_val=0, max_val=NW - 1)
            for k in range(KD):
                nc.gpsimd.tensor_tensor(nodes[:, k, bass.ds(wy, 1), :], nodes[:, k, bass.ds(wy, 1), :],
                                        r_y[:, k * P:(k + 1) * P].unsqueeze(1), ALU.add).then_inc(S["mem_patched"], 1)
            pool.wait_ge(S["mem_patched"], KD)
            def differ(w, j):
                nc.gpsimd.tensor_tensor(diff[:, j, :, :], nodes[:, :, w, :],
                                        r_rows[:, :].rearrange("p (k c) -> p k c", k=KD), ALU.subtract).then_inc(S["diff_ok"], 1)
            differ(0, 0)
            differ(1, 1)
            with pool.Fori(1, PAIRS) as q:
                for j in range(2):
                    pool.wait_ge(S["dist_ok"], q * 2 + (j - 1))
                    differ(q * 2 + j, j)

            pool.wait_ge(S["deg_ok"], 1)
            nc.gpsimd.tensor_tensor(dinv[:, :], deg[:, :], neg_half[:, :], ALU.pow).then_inc(S["deg_ok"], 1)

            pool.wait_ge(S["table_out"], 16 * KD * NZC)
            STEPS = TILES // 32
            def take_indices(t0, half):
                nc.gpsimd.tensor_copy(idx_ring[:, half, :], src_idx[:, bass.ds(t0, 16)]).then_inc(S["idx_ok"], 1)

            def gather_body(q, first):
                for half in range(2):
                    if not first:
                        for s in range(4):
                            pool.wait_ge(gathered[half * 4 + s], q * 64)
                        pool.sem_inc(S["tick"], 1)
                    take_indices(q * 32 + half * 16, half)
                    pool.wait_ge(S["idx_ok"], q * 2 + half + 1)
                    pool.sem_inc(S["tick"], 1)
                    for s in range(4):
                        slot = half * 4 + s
                        if not first:
                            pool.wait_ge(S["agg_ps"], (q - 1) * 8 + slot + 1)
                            pool.sem_inc(S["tick"], 1)
                        for t in range(GT):
                            nc.gpsimd.indirect_dma_start(
                                gath[:, slot, t, :], None, z_table,
                                bass.IndirectOffsetOnAxis(ap=idx_ring[:, half, s * GT + t:s * GT + t + 1], axis=0),
                            ).then_inc(gathered[slot], 16)

            gather_body(0, True)
            with pool.Fori(1, STEPS) as q:
                gather_body(q, False)


            pool.wait_ge(S["bases"], 1)
            n_bad = pool.value_load(bad_i[0:1, 0:1], min_val=0, max_val=GROUPS)
            with pool.If(n_bad > 0):
                pool.wait_ge(S["agg_ps"], GROUPS)
                with pool.Fori(0, GROUPS) as g:
                    pool.wait_ge(S["rep_free"], g + 1)
                    pool.sem_inc(S["tick"], 1)
                    nc.gpsimd.tensor_copy(idx_ring[:, 0, 0:GT], src_idx[:, bass.ds(g * GT, GT)]).then_inc(S["rep_idx"], 1)
                    pool.wait_ge(S["rep_idx"], g + 1)
                    pool.sem_inc(S["tick"], 1)
                    for t in range(GT):
                        nc.gpsimd.indirect_dma_start(
                            gath[:, 0, t, :], None, z_table,
                            bass.IndirectOffsetOnAxis(ap=idx_ring[:, 0, t:t + 1], axis=0)).then_inc(S["rep_got"], 16)

            pool.wait_ge(S["var_ok"], 1)
            nc.gpsimd.tensor_tensor(rstd2[:, :], var2[:, :], neg_half[:, :], ALU.pow).then_inc(S["var_ok"], 1)

            pool.wait_ge(S["routed"], 1)
            pool.wait_ge(S["xs_zero"], 16)
            last_row = pool.to_reg(SLOTS - 1)
            HZ = ZC // 2

            def index_half(to, frm, q, half, s_idx):
                nc.gpsimd.tensor_copy(to[:, half, :], frm[:, bass.ds(q * ZC + half * HZ, HZ)]).then_inc(S[s_idx], 1)
                pool.wait_ge(S[s_idx], q * 2 + half + 1)
                pool.sem_inc(S["tick"], 1)

            def send(q, first):
                for half in range(2):
                    if not first:
                        pool.wait_ge(S[f"sent{half}"], q * (16 * HZ))
                        pool.sem_inc(S["tick"], 1)
                    index_half(send_idx, put_idx, q, half, "sidx")
                    for s in range(HZ):
                        pool.wait_ge(S["send_h"], q * ZC + (half * HZ + s + 1))
                        pool.sem_inc(S["tick"], 1)
                        nc.gpsimd.indirect_dma_start(
                            xs, bass.IndirectOffsetOnAxis(ap=send_idx[:, half, s:s + 1], axis=0), h_send[:, half * HZ + s, :], None,
                            bounds_check=last_row, oob_is_err=False).then_inc(S[f"sent{half}"], 16)
            send(0, True)
            with pool.Fori(1, NZC) as q:
                send(q, False)

            for t in range(4):
                pool.wait_ge(S[f"ys_out{t}"], 16 * NE * NCH)

            def fetch(q, first):
                for half in range(2):
                    if not first:
                        pool.wait_ge(S["gated_ok"], q * ZC + (half * HZ - HZ))
                        pool.sem_inc(S["tick"], 1)
                    index_half(take_idx, get_idx, q, half, "tidx")
                    for s in range(HZ):
                        nc.gpsimd.indirect_dma_start(
                            y_got[:, half * HZ + s, :], None, ys,
                            bass.IndirectOffsetOnAxis(ap=take_idx[:, half, s:s + 1], axis=0)).then_inc(S[f"got{half}"], 16)
            fetch(0, True)
            with pool.Fori(1, NZC) as q:
                fetch(q, False)

        @block.scalar
        def _(act):
            def node_row(w):
                return nodes[:, :, w, :]

            act.wait_ge(S["x_in"], 16 * (KD * NZC + 1))
            with act.Fori(0, PAIRS) as q:
                for j in range(2):
                    nc.scalar.activation(junk[:, j, :, :], node_row(q * 2 + j), ACT.Copy,
                                         accum_out=neg_mean[:, bass.ds(q * 2 + j, 1)]).then_inc(S["mean_sum"], 1)
                    act.wait_ge(S["mean_sum"], q * 2 + j + 1)
            nc.scalar.mul(neg_mean[:, :], neg_mean[:, :], -1.0 / D).then_inc(S["act_ch"], 1)
            act.wait_ge(S["act_ch"], 1)
            with act.Fori(0, PAIRS) as q:
                for j in range(2):
                    nc.scalar.activation(junk[:, j, :, :], node_row(q * 2 + j), ACT.Square,
                                         bias=neg_mean[:, bass.ds(q * 2 + j, 1)],
                                         accum_out=sq_sum[:, bass.ds(q * 2 + j, 1)]).then_inc(S["mean_sum"], 1)
                    act.wait_ge(S["mean_sum"], q * 2 + (NW + j + 1))
            act.sem_inc(S["ssum"], 1)
            act.wait_ge(S["shift_ok"], 1)
            with act.Fori(0, PAIRS) as q:
                for j in range(2):
                    nc.scalar.activation(node_row(q * 2 + j), node_row(q * 2 + j), ACT.Identity,
                                         bias=shift[:, bass.ds(q * 2 + j, 1)],
                                         scale=rstd[:, bass.ds(q * 2 + j, 1)]).then_inc(S["mean_sum"], 1)
            act.wait_ge(S["mean_sum"], 3 * NW)
            act.sem_inc(S["mem_ok"], 1)
            with act.Fori(0, PAIRS) as q:
                for j in range(2):
                    act.wait_ge(S["diff_ok"], q * 2 + j + 1)
                    nc.scalar.activation(junk[:, j, :, :], diff[:, j, :, :], ACT.Square,
                                         accum_out=dist[:, bass.ds(q * 2 + j, 1)]).then_inc(S["dist_ok"], 1)
                    act.wait_ge(S["dist_ok"], q * 2 + j + 1)

            act.wait_ge(S["z_ok"], NZC)
            def z_tile(w, j):
                nc.scalar.activation(z_stat[:, j, :, :], node_row(w), ACT.Copy).then_inc(S["zstat_ok"], 1)
            z_tile(0, 0)
            z_tile(1, 1)
            with act.Fori(1, PAIRS) as q:
                for j in range(2):
                    act.wait_ge(S["zT_ps"], q * 2 + (j - 1))
                    z_tile(q * 2 + j, j)


            act.wait_ge(S["fixed"], 1)
            def agg_tile(w, j):
                nc.scalar.activation(agg_stat[:, j, :, :], node_row(w), ACT.Copy).then_inc(S["aggst_ok"], 1)
            agg_tile(0, 0)
            agg_tile(1, 1)
            with act.Fori(1, PAIRS) as q:
                for j in range(2):
                    act.wait_ge(S["conv_ps"], q * 2 + (j - 1))
                    agg_tile(q * 2 + j, j)
            act.wait_ge(S["lnb_ok"], 1)
            def norm_tile(to, w, sm):
                nc.scalar.activation(to, node_row(w), ACT.Identity, bias=shift2[:, bass.ds(w, 1)],
                                     scale=rstd2[:, bass.ds(w, 1)]).then_inc(S[sm], 1)
            norm_tile(h_tile[:, 0, :, :], 0, "h_ok")
            norm_tile(h_tile[:, 1, :, :], 1, "h_ok")
            with act.Fori(1, PAIRS) as q:
                for j in range(2):
                    act.wait_ge(S["hT_ps"], q * 2 + (j - 1))
                    norm_tile(h_tile[:, j, :, :], q * 2 + j, "h_ok")
            act.wait_ge(S["gate_in"], 1)
            nc.scalar.activation(gate_e, gate_l, ACT.Exp).then_inc(S["gate_out"], 1)
            act.wait_ge(S["routed"], 1)
            def send_tile(w, s):
                norm_tile(h_send[:, s, :].rearrange("p (k c) -> p k c", k=KD), w, "send_h")
            for s in range(ZC):
                send_tile(s, s)
            with act.Fori(1, NZC) as q:
                for half in range(2):
                    act.wait_ge(S[f"sent{half}"], q * (16 * ZC // 2))
                    act.sem_inc(S["tick2"], 1)
                    for s in range(half * ZC // 2, (half + 1) * ZC // 2):
                        send_tile(q * ZC + s, s)

            def hidden(q, j, c, first):
                n = CHUNKS[c][1]
                s = j * NCH + c
                for f in range(FT):
                    act.wait_ge(S["l1_ps"], q * (2 * NCH * FT) + (s * FT + f + 1))
                    if not (first and s == 0):
                        act.wait_ge(S["l2_ps"], q * (8 * NCH) + 4 * s)
                    act.sem_inc(S["tick2"], 1)
                    nc.scalar.activation(hid[:, f, 0:n], bank[2 + f % 2][:, 0:n], ACT.Relu,
                                         bias=b1_cols[:, bass.ds((q * 2 + j) * FT + f, 1)]).then_inc(S["hid_ok"], 1)
            for j in range(2):
                for c in range(NCH):
                    hidden(0, j, c, True)
            with act.Fori(1, NE // 2) as q:
                for j in range(2):
                    for c in range(NCH):
                        hidden(q, j, c, False)

            def gate_rows(q, first):
                for half in range(2):
                    act.wait_ge(S[f"got{half}"], q * (16 * ZC // 2) + 16 * ZC // 2)
                    act.sem_inc(S["tick2"], 1)
                    for i in range(ZC // 2):
                        s = half * ZC // 2 + i
                        if not (first and s < 2):
                            act.wait_ge(S["o_ok"], q * ZC + (s - 1))
                            act.sem_inc(S["tick2"], 1)
                        nc.scalar.activation(y_gated[:, s % 2, :], y_got[:, s, :], ACT.Copy,
                                             scale=weight[:, bass.ds(q * ZC + s, 1)]).then_inc(S["gated_ok"], 1)
            gate_rows(0, True)
            with act.Fori(1, NZC) as q:
                gate_rows(q, False)

        @block.vector
        def _(dve):
            ch = [0]

            def then(ins):
                ch[0] += 1
                ins.then_inc(S["dve_ch"], 1)
                dve.wait_ge(S["dve_ch"], ch[0])

            dve.wait_ge(S["edges_in"], 6 * 16)
            nc.vector.tensor_copy(stage_f[:, 0, :, :], stage_i[:, 0, :, :]).then_inc(S["edges_float"], 1)
            nc.vector.tensor_copy(stage_f[:, 1, :, :], stage_i[:, 1, :, :]).then_inc(S["edges_float"], 1)
            dve.wait_ge(S["edges_float"], 1)
            then(nc.vector.tensor_reduce(tile_lim[:, 0, :], stage_f[:, 0, :, :], AX.X, ALU.min))
            then(nc.vector.scalar_tensor_tensor(stage_f2[:, :, :], stage_f[:, 0, :, :], float(PAD_DST), stage_f[:, 0, :, :],
                                                ALU.is_lt, ALU.mult))
            nc.vector.tensor_reduce(tile_lim[:, 1, :], stage_f2[:, :, :], AX.X, ALU.max).then_inc(S["lims"], 1)
            for n, (i, b0, nb) in enumerate(EDGE_TURNS):
                dve.wait_ge(S["edge_psum"], n + 1)
                to = (dst_f if i == 0 else src_idx)[:, b0 * P:(b0 + nb) * P]
                nc.vector.tensor_copy(to, bank[n % 2][:, 0:nb * P]).then_inc(S["edges_out"], 1)
            dve.wait_ge(S["edges_out"], len(EDGE_TURNS))
            then(nc.vector.tensor_copy(dst_i[:, :], dst_f[:, :]))
            then(nc.vector.tensor_single_scalar(low_i[:, :], dst_i[:, :], 127, ALU.bitwise_and))
            then(nc.vector.tensor_copy(lo_b[:, :], low_i[:, :]))
            then(nc.vector.tensor_single_scalar(low_i[:, :], dst_i[:, :], 7, ALU.arith_shift_right))
            then(nc.vector.tensor_copy(hi_b[:, :], low_i[:, :]))
            for n in range(len(LIM_TURNS)):
                i, b0, nb = LIM_TURNS[n]
                dve.wait_ge(S["limps"], n + 1)
                then(nc.vector.tensor_copy(lim_row[0:1, i, b0 * P:(b0 + nb) * P], bank[2 + n % 2][0:1, 0:nb * P]))
                dve.sem_inc(S["lim_rows"], 1)
            lim_grp = lim_row[0:1, :, 0:TILES].rearrange("p i (g t) -> p i g t", t=GT)
            then(nc.vector.tensor_reduce(grp_min[:, :], lim_grp[:, 0, :, :], AX.X, ALU.min))
            then(nc.vector.tensor_reduce(grp_max[:, :], lim_grp[:, 1, :, :], AX.X, ALU.max))
            then(nc.vector.tensor_scalar(grp_base[:, :], grp_min[:, :], TOP_BASE, None, ALU.min))
            then(nc.vector.tensor_tensor(grp_max[:, :], grp_max[:, :], grp_base[:, :], ALU.subtract))
            then(nc.vector.tensor_scalar(grp_bad[:, :], grp_max[:, :], float(P), None, ALU.is_ge))
            then(nc.vector.tensor_reduce(bad_sum[:, :], grp_bad[:, :], AX.X, ALU.add))
            then(nc.vector.tensor_copy(bad_i[:, :], bad_sum[:, :]))
            then(nc.vector.tensor_copy(base_i[:, :], grp_base[:, :]))
            then(nc.vector.scalar_tensor_tensor(grp_cmp[:, :], grp_bad[:, :], -FAR, grp_base[:, :], ALU.mult, ALU.add))
            dve.sem_inc(S["bases"], 1)
            dve.wait_ge(S["cmp_ps"], 1)
            then(nc.vector.tensor_tensor(rel_b[:, 0:TILES].rearrange("p (g t) -> p g t", t=GT),
                                         dst_f[:, 0:TILES].rearrange("p (g t) -> p g t", t=GT),
                                         bank[4][:, 0:GROUPS].unsqueeze(2).to_broadcast([P, GROUPS, GT]), ALU.subtract))
            dve.wait_ge(S["y_in"], 16)
            dve.wait_ge(S["consts"], 6)
            dve.wait_ge(S["r_in"], 16)
            then(nc.vector.memset(rel_b[:, TILES:EB * P], -1.0))
            then(nc.vector.tensor_copy(y_f[:, :], y_i[:, :]))
            then(nc.vector.tensor_single_scalar(wy_i[:, :], y_i[:, :], 7, ALU.arith_shift_right))
            then(nc.vector.tensor_scalar(is_y[:, :], node_id[:, :], y_f[:, 0:1], None, ALU.is_equal))
            then(nc.vector.tensor_scalar(not_y[:, :], is_y[:, :], -1.0, 1.0, ALU.mult, ALU.add))
            then(nc.vector.tensor_reduce(mine_y[:, :], is_y[:, :], AX.X, ALU.add))
            then(nc.vector.tensor_scalar(r_y[:, :], r_rows[:, :], mine_y[:, 0:1], None, ALU.mult))
            then(nc.vector.tensor_scalar(invalid[:, :], node_id[:, :], float(N), -3.0e38, ALU.is_ge, ALU.mult))
            dve.sem_inc(S["pre"], 1)

            def one_hots(s, j):
                t0 = s * 16
                nc.vector.tensor_tensor(oh_lo[:, j, :, :], iota_b[:, :].unsqueeze(1).to_broadcast([P, 16, P]),
                                        lo_b[:, bass.ds(t0, 16)].unsqueeze(2).to_broadcast([P, 16, P]),
                                        ALU.is_equal).then_inc(S["hist_built"], 1)
                nc.vector.tensor_tensor(oh_hi[:, j, :, :], iota_b[:, 0:NW].unsqueeze(1).to_broadcast([P, 16, NW]),
                                        hi_b[:, bass.ds(t0, 16)].unsqueeze(2).to_broadcast([P, 16, NW]),
                                        ALU.is_equal).then_inc(S["hist_built"], 1)
            one_hots(0, 0)
            one_hots(1, 1)
            with dve.Fori(1, HSTEPS // 2) as q:
                for j in range(2):
                    dve.wait_ge(S["hist_used"], q * 2 + (j - 1))
                    one_hots(q * 2 + j, j)
            dve.wait_ge(S["hist_ps"], 1)
            then(nc.vector.tensor_tensor(deg[:, :], bank[5][:, 0:NW], not_y[:, :], ALU.mult))
            then(nc.vector.scalar_tensor_tensor(deg[:, :], is_y[:, :], float(TOPK), deg[:, :], ALU.mult, ALU.add))
            nc.vector.tensor_scalar(deg[:, :], deg[:, :], SELF_W, None, ALU.add).then_inc(S["deg_ok"], 1)
            dve.wait_ge(S["deg_ok"], 2)
            dve.wait_ge(S["diff_ok"], NW)
            for c in range(NZC):
                for k in range(KD):
                    rows = nodes[:, k, c * ZC:(c + 1) * ZC, :]
                    ins = nc.vector.tensor_tensor(rows, rows, dinv[:, c * ZC:(c + 1) * ZC].unsqueeze(2).to_broadcast([P, ZC, P]),
                                                  ALU.mult)
                ch[0] += 1
                ins.then_inc(S["z_ok"], 1)
                ch[0] -= 1

            dve.wait_ge(S["dist_ok"], NW)
            then(nc.vector.scalar_tensor_tensor(near[:, :], dist[:, :], -1.0, not_y[:, :], ALU.mult, ALU.mult))
            then(nc.vector.tensor_tensor(near[:, :], near[:, :], invalid[:, :], ALU.add))
            then(nc.vector.max(near8[:, :], near[:, :]))
            dve.sem_inc(S["near_ok"], 1)
            dve.wait_ge(S["near_ps"], 1)
            nc.vector.tensor_copy(near_row[0:1, 0:4 * P], bank[0][0:1, :])
            then(nc.vector.tensor_copy(near_row[0:1, 4 * P:8 * P], bank[1][0:1, :]))
            dve.drain()
            then(nc.vector.max(top8[:, :], near_row[:, :]))
            dve.sem_inc(S["near_ok"], 1)
            dve.wait_ge(S["near_ps"], 2)
            then(nc.vector.tensor_copy(thr[:, :], bank[2][:, 0:1]))
            then(nc.vector.tensor_scalar(above[:, :], near[:, :], thr[:, 0:1], None, ALU.is_gt))
            then(nc.vector.tensor_scalar(tied[:, :], near[:, :], thr[:, 0:1], None, ALU.is_equal))
            then(nc.vector.tensor_reduce(n_above[:, :], above[:, :], AX.X, ALU.add))
            dve.sem_inc(S["near_ok"], 1)
            dve.wait_ge(S["near_ps"], 3)
            then(nc.vector.tensor_scalar(room[:, :], bank[2][:, 1:2], -1.0, float(TOPK), ALU.mult, ALU.add))
            then(nc.vector.tensor_tensor_scan(tie_scan[:, :], ones[:, 0:NW], bank[3][:, NW:2 * NW], 0.0, ALU.mult, ALU.add))
            then(nc.vector.tensor_tensor(tie_rank[:, :], tie_scan[:, :], bank[3][:, NW:2 * NW], ALU.subtract))
            then(nc.vector.tensor_tensor(tie_rank[:, :], tie_rank[:, :], bank[3][:, 0:NW], ALU.add))
            then(nc.vector.tensor_scalar(tie_rank[:, :], tie_rank[:, :], room[:, 0:1], None, ALU.is_le))
            then(nc.vector.tensor_tensor(chosen[:, :], tied[:, :], tie_rank[:, :], ALU.mult))
            then(nc.vector.tensor_tensor(chosen[:, :], chosen[:, :], above[:, :], ALU.add))
            dve.sem_inc(S["chosen_ok"], 1)

            dve.wait_ge(S["table_out"], 16 * KD * NZC)
            with dve.Fori(0, PAIRS) as q:
                for j in range(2):
                    dve.wait_ge(S["zT_ps"], q * 2 + j + 1)
                    nc.vector.tensor_copy(nodes[:, :, q * 2 + j, :],
                                          bank[4 + j][:, 0:D].rearrange("p (k c) -> p k c", k=KD)).then_inc(S["agg_init"], 1)
            dve.wait_ge(S["agg_init"], NW)
            dve.wait_ge(S["selps"], 1)
            ycol = dve.value_load(y_i[0:1, 0:1], min_val=0, max_val=N - 1)
            then(nc.vector.tensor_tensor(col_fix[:, :], agg[:, :, bass.ds(ycol, 1)].rearrange("p k o -> p (k o)"),
                                         bank[3][:, 0:KD], ALU.add))

            def select(g, j):
                nc.vector.tensor_tensor(sel[:, j, :, :], iota_b[:, :].unsqueeze(1).to_broadcast([P, GT, P]),
                                        rel_b[:, bass.ds(g * GT, GT)].unsqueeze(2).to_broadcast([P, GT, P]),
                                        ALU.is_equal).then_inc(S["sel_ok"], 1)

            def add_group(g, j, first):
                base = dve.value_load(base_i[0:1, bass.ds(g, 1)], min_val=0, max_val=(NW - 1) * P)
                if not first:
                    dve.wait_ge(S["agg_added"], g)
                dve.wait_ge(S["agg_ps"], g + 1)
                where = agg[:, :, bass.ds(base, P)]
                nc.vector.tensor_tensor(where, where, bank[j][:, 0:D].rearrange("p (k c) -> p k c", k=KD),
                                        ALU.add).then_inc(S["agg_added"], 1)

            select(0, 0)
            select(1, 1)
            add_group(0, 0, True)
            with dve.Fori(0, (GROUPS - 2) // 2) as q:
                for j in range(2):
                    dve.wait_ge(S["agg_ps"], q * 2 + j + 1)
                    select(q * 2 + (j + 2), j)
                    add_group(q * 2 + (j + 1), (j + 1) % 2, False)
            add_group(GROUPS - 1, 1, False)
            dve.wait_ge(S["agg_added"], GROUPS)
            n_bad = dve.value_load(bad_i[0:1, 0:1], min_val=0, max_val=GROUPS)
            with dve.If(n_bad > 0):
                dve.sem_inc(S["rep_bad"], 1)
                dve.wait_ge(S["rep_dst"], 1)
                nc.vector.tensor_scalar(grp_far, bank[4][:, 0:GROUPS], -FAR, FAR, ALU.mult, ALU.add).then_inc(S["rep_bad"], 1)
                dve.wait_ge(S["rep_bad"], 2)
                by_group = dst_f[:, 0:TILES].rearrange("p (g t) -> p g t", t=GT)
                nc.vector.tensor_tensor(by_group, by_group, grp_far.unsqueeze(2).to_broadcast([P, GROUPS, GT]),
                                        ALU.add).then_inc(S["rep_bad"], 1)
                dve.wait_ge(S["rep_bad"], 3)
                with dve.Fori(0, GROUPS) as g:
                    with dve.Fori(0, NW) as w:
                        nc.vector.tensor_scalar(rep_rel[:, :], dst_f[:, bass.ds(g * GT, GT)], win_f[:, bass.ds(w, 1)], None,
                                                ALU.subtract).then_inc(S["rep_relok"], 1)
                        dve.wait_ge(S["rep_relok"], g * NW + (w + 1))
                        nc.vector.tensor_tensor(sel[:, 0, :, :], iota_b[:, :].unsqueeze(1).to_broadcast([P, GT, P]),
                                                rep_rel[:, :].unsqueeze(2).to_broadcast([P, GT, P]),
                                                ALU.is_equal).then_inc(S["rep_sel"], 1)
                        where = agg[:, :, bass.ds(w * P, P)]
                        dve.wait_ge(S["rep_ps"], g * NW + (w + 1))
                        nc.vector.tensor_tensor(where, where, bank[0][:, 0:D].rearrange("p (k c) -> p k c", k=KD),
                                                ALU.add).then_inc(S["rep_added"], 1)
                        dve.wait_ge(S["rep_added"], g * NW + (w + 1))
            then(nc.vector.tensor_copy(agg[:, :, bass.ds(ycol, 1)].rearrange("p k o -> p (k o)"), col_fix[:, :]))
            dve.sem_inc(S["fixed"], 1)


            dve.wait_ge(S["aggst_ok"], 1)
            def residual(q, j):
                w = q * 2 + j
                dve.wait_ge(S["conv_ps"], w + 1)
                dve.wait_ge(S[f"xt_in{j}"], q * 16 + 16)
                nc.vector.scalar_tensor_tensor(nodes[:, :, w, :], bank[j][:, 0:D].rearrange("p (k c) -> p k c", k=KD),
                                               dinv[:, bass.ds(w, 1)], x_tile[:, j, :].rearrange("p (k c) -> p k c", k=KD),
                                               ALU.mult, ALU.add).then_inc(S["x1_ok"], 1)
            with dve.Fori(0, PAIRS) as q:
                for j in range(2):
                    residual(q, j)
                for j in range(2):
                    dve.wait_ge(S["x1_ok"], q * 2 + j + 1)
                    dve.sem_inc(S["fin_ch"], 1)
                    nc.vector.bn_stats(bn[:, bass.ds(q * 2 + j, 1), :].rearrange("p o s -> p (o s)"),
                                       nodes[:, :, q * 2 + j, :]).then_inc(S["bn_ok"], 1)
            dve.wait_ge(S["bn_ok"], NW)
            then(nc.vector.tensor_tensor(mean2[:, :], bn[:, :, 1], bn[:, :, 4], ALU.add))
            then(nc.vector.tensor_tensor(gap2[:, :], bn[:, :, 1], bn[:, :, 4], ALU.subtract))
            then(nc.vector.tensor_tensor(gap2[:, :], gap2[:, :], gap2[:, :], ALU.mult))
            then(nc.vector.tensor_tensor(var2[:, :], bn[:, :, 2], bn[:, :, 5], ALU.add))
            then(nc.vector.tensor_scalar(var2[:, :], var2[:, :], 1.0 / D, EPS, ALU.mult, ALU.add))
            nc.vector.scalar_tensor_tensor(var2[:, :], gap2[:, :], 0.25, var2[:, :], ALU.mult, ALU.add).then_inc(S["var_ok"], 1)
            dve.wait_ge(S["var_ok"], 2)
            then(nc.vector.scalar_tensor_tensor(shift2[:, :], mean2[:, :], -0.5, rstd2[:, :], ALU.mult, ALU.mult))
            dve.sem_inc(S["lnb_ok"], 1)
            def feat(w, j, first):
                dve.wait_ge(S["hT_ps"], w + 1)
                if not first:
                    dve.wait_ge(S["logit_ps"], w - 1)
                nc.vector.tensor_copy(h_feat[:, j, :, :], bank[2 + j][:, 0:D].rearrange("p (k c) -> p k c", k=KD)).then_inc(S["hT_ok"], 1)
            feat(0, 0, True)
            feat(1, 1, True)
            with dve.Fori(1, PAIRS) as q:
                for j in range(2):
                    feat(q * 2 + j, j, False)

            def over(ap):
                return ap.unsqueeze(2).to_broadcast([P, NW, NE])
            def per_expert(ap):
                return ap.unsqueeze(1).to_broadcast([P, NW, NE])
            dve.wait_ge(S["logit_ps"], NW)
            by_parity = gate_l.rearrange("p (q j) e -> p j q e", j=2)
            for j in range(2):
                then(nc.vector.tensor_copy(by_parity[:, j, :, :], bank[6 + j][:, 0:PAIRS * NE].rearrange("p (q e) -> p q e", e=NE)))
            then(nc.vector.tensor_reduce(best[:, :], gate_l, AX.X, ALU.max))
            then(nc.vector.tensor_tensor(gate_l, gate_l, over(best[:, :]), ALU.subtract))
            dve.sem_inc(S["gate_in"], 1)
            then(nc.vector.tensor_copy(iota_f[:, :], iota_i[:, 0:NE]))
            then(nc.vector.tensor_scalar(rank_e[:, :], iota_f[:, :], -1.0, float(NE), ALU.mult, ALU.add))
            dve.wait_ge(S["gate_out"], 1)
            then(nc.vector.tensor_reduce(norm[:, :], gate_e, AX.X, ALU.add))
            then(nc.vector.reciprocal(norm[:, :], norm[:, :]))
            then(nc.vector.tensor_tensor(gate_e, gate_e, over(norm[:, :]), ALU.mult))
            then(nc.vector.tensor_reduce(best[:, :], gate_e, AX.X, ALU.max))
            then(nc.vector.tensor_tensor(gate_t, gate_e, over(best[:, :]), ALU.is_equal))
            then(nc.vector.tensor_tensor(gate_t, gate_t, per_expert(rank_e[:, :]), ALU.mult))
            then(nc.vector.tensor_reduce(expert[:, :], gate_t, AX.X, ALU.max))
            then(nc.vector.tensor_tensor(pick, gate_t, over(expert[:, :]), ALU.is_equal))
            then(nc.vector.tensor_scalar(kept[:, :], invalid[:, :], 0.0, None, ALU.is_ge))
            then(nc.vector.tensor_tensor(pick, pick, over(kept[:, :]), ALU.mult))
            dve.sem_inc(S["pick_ok"], 1)
            dve.wait_ge(S["rank_ps"], 1)
            HW = NW // 2
            for i in range(2):
                rows = slice(i * HW, (i + 1) * HW)
                then(nc.vector.tensor_copy(gate_t[:, rows, :], bank[2 + i][:, 0:HW * NE].rearrange("p (w e) -> p w e", e=NE)))
            for e in range(NE):
                then(nc.vector.tensor_tensor_scan(gate_l[:, :, e], ones[:, 0:NW], gate_t[:, :, e], 0.0, ALU.mult, ALU.add))
            then(nc.vector.tensor_tensor(gate_l, gate_l, gate_t, ALU.subtract))
            for i in range(2):
                rows = slice(i * HW, (i + 1) * HW)
                then(nc.vector.tensor_tensor(gate_l[:, rows, :], gate_l[:, rows, :],
                                             bank[i][:, 0:HW * NE].rearrange("p (w e) -> p w e", e=NE), ALU.add))
            then(nc.vector.tensor_tensor(gate_l, gate_l, pick, ALU.mult))
            then(nc.vector.tensor_reduce(place[:, :], gate_l, AX.X, ALU.add))
            then(nc.vector.tensor_scalar(expert[:, :], expert[:, :], -1.0, float(NE), ALU.mult, ALU.add))
            then(nc.vector.tensor_scalar(norm[:, :], place[:, :], float(CAP), None, ALU.is_le))
            then(nc.vector.tensor_tensor(kept[:, :], kept[:, :], norm[:, :], ALU.mult))
            then(nc.vector.tensor_tensor(weight[:, :], best[:, :], kept[:, :], ALU.mult))
            then(nc.vector.tensor_scalar(place[:, :], place[:, :], float(CAP), -1.0, ALU.min, ALU.add))
            then(nc.vector.scalar_tensor_tensor(slot_f[:, :], expert[:, :], float(CAP), place[:, :], ALU.mult, ALU.add))
            then(nc.vector.tensor_scalar(slot_f[:, :], slot_f[:, :], 0.0, None, ALU.max))
            then(nc.vector.tensor_copy(get_idx[:, :], slot_f[:, :]))
            then(nc.vector.tensor_scalar(kept[:, :], kept[:, :], -FAR, FAR, ALU.mult, ALU.add))
            then(nc.vector.tensor_tensor(slot_f[:, :], slot_f[:, :], kept[:, :], ALU.add))
            then(nc.vector.tensor_copy(put_idx[:, :], slot_f[:, :]))
            dve.sem_inc(S["routed"], 1)

            dve.wait_ge(S["b1_ps"], 1)
            nc.vector.tensor_copy(b1_cols, bank[4][:, 0:NE * FT]).then_inc(S["b1_ok"], 1)

            def feats(q, j, c, first):
                s, n = j * NCH + c, CHUNKS[c][1]
                dve.wait_ge(S["xT_ps"], q * (2 * NCH) + s + 1)
                if not (first and s < 2):
                    dve.wait_ge(S["l1_ps"], q * (2 * NCH * FT) + (s - 1) * FT)
                for k in range(KD):
                    nc.vector.tensor_copy(xs_feat[:, s % 2, k, 0:n], bank[k][:, 0:n]).then_inc(S["xT_ok"], 1)

            def results(q, j, c, first):
                s = j * NCH + c
                for t in range(4):
                    n = min(P, CHUNKS[c][1] - t * P)
                    if not (first and s == 0):
                        dve.wait_ge(S[f"ys_out{t}"], q * (32 * NCH) + 16 * s)
                    dve.wait_ge(S["l2_ps"], q * (8 * NCH) + (4 * s + t + 1))
                    nc.vector.tensor_tensor(y_tile[0:n, t, :], bank[4 + t % 2][0:n, 0:D],
                                            b2_rows[0:n, bass.ds(q * 2 + j, 1), :].rearrange("p o d -> p (o d)"),
                                            ALU.add).then_inc(S["y_ok"], 1)

            def experts(q, first, last):
                for j in range(2):
                    for c in range(NCH):
                        s = j * NCH + c
                        if not (last and s == 2 * NCH - 1):
                            more = s + 1
                            feats(q if more < 2 * NCH else q + 1, more // NCH % 2, more % NCH, False if more > 1 else first)
                        results(q, j, c, first)
            feats(0, 0, 0, True)
            experts(0, True, False)
            with dve.Fori(1, NE // 2 - 1) as q:
                experts(q, False, False)
            experts(NE // 2 - 1, False, True)

            BIG = 3.4028234e38
            fc = [0]
            def finish_window(w, j, n, fresh):
                g, lo, cl, fin, o = (v[:, j, :] for v in (y_gated, y_low, y_clip, y_fin, o_tile))
                dve.wait_ge(S["gated_ok"], w + 1)
                nc.vector.tensor_scalar(lo, g, -BIG, -1.0e4, ALU.is_lt, ALU.mult).then_inc(S["clean"], 1)
                nc.vector.tensor_scalar(cl, g, BIG, 1.0e4, ALU.is_gt, ALU.mult).then_inc(S["clean"], 1)
                nc.vector.tensor_scalar(fin, g, 0.0, 0.0, ALU.mult, ALU.is_equal).then_inc(S["clean"], 1)
                dve.wait_ge(S["clean"], w * 5 + 3)
                nc.vector.tensor_tensor(cl, cl, lo, ALU.add).then_inc(S["clean"], 1)
                dve.wait_ge(S["clean"], w * 5 + 4)
                dve.sem_inc(S["fin_ch"], 1)
                nc.vector.copy_predicated(cl, fin, g).then_inc(S["clean"], 1)
                if not fresh:
                    dve.wait_ge(S[f"out_done{j}"], n * 16)
                dve.wait_ge(S["clean"], w * 5 + 5)
                nc.vector.tensor_tensor(o.rearrange("p (k c) -> p k c", k=KD), nodes[:, :, w, :],
                                        cl.rearrange("p (k c) -> p k c", k=KD), ALU.add).then_inc(S["o_ok"], 1)
            for j in range(2):
                finish_window(j, j, 0, True)
            with dve.Fori(1, PAIRS) as q:
                for j in range(2):
                    finish_window(q * 2 + j, j, q, False)

        @block.tensor
        def _(pe):
            pe.wait_ge(S["consts"], 6)
            for n, (i, b0, nb) in enumerate(EDGE_TURNS):
                pe.wait_ge(S["edges_float"], i + 1)
                if n >= 2:
                    pe.wait_ge(S["edges_out"], n - 1)
                for b in range(nb):
                    last = nc.tensor.transpose(bank[n % 2][:, b * P:(b + 1) * P], stage_f[:, i, b0 + b, :], ident[:, :])
                last.then_inc(S["edge_psum"], 1)
            pe.wait_ge(S["lims"], 1)
            for n, (i, b0, nb) in enumerate(LIM_TURNS):
                if n >= 2:
                    pe.wait_ge(S["lim_rows"], n - 1)
                for b in range(nb):
                    last = nc.tensor.matmul(bank[2 + n % 2][0:1, b * P:(b + 1) * P], tile_lim[:, i, b0 + b:b0 + b + 1],
                                            ident[:, :], start=True, stop=True)
                last.then_inc(S["limps"], 1)
            pe.wait_ge(S["bases"], 1)
            nc.tensor.matmul(bank[4][:, 0:GROUPS], ones[0:1, :], grp_cmp[0:1, :], start=True, stop=True).then_inc(S["cmp_ps"], 1)

            nc.tensor.matmul(bank[5][:, 0:NW], zeros[:, 0:P], zeros[:, 0:NW], start=True, stop=False)
            with pe.Fori(0, HSTEPS // 2) as q:
                for j in range(2):
                    pe.wait_ge(S["hist_built"], q * 4 + 2 * (j + 1))
                    for t in range(16):
                        last = nc.tensor.matmul(bank[5][:, 0:NW], oh_lo[:, j, t, :], oh_hi[:, j, t, :], start=False, stop=False)
                    last.then_inc(S["hist_used"], 1)
            nc.tensor.matmul(bank[5][:, 0:NW], zeros[:, 0:P], zeros[:, 0:NW], start=False, stop=True).then_inc(S["hist_ps"], 1)

            pe.wait_ge(S["near_ok"], 1)
            for i in range(8):
                last = nc.tensor.matmul(bank[i // 4][0:1, (i % 4) * P:(i % 4 + 1) * P], near8[:, i:i + 1], ident[:, :],
                                        start=True, stop=True)
            last.then_inc(S["near_ps"], 1)
            pe.wait_ge(S["near_ok"], 2)
            nc.tensor.matmul(bank[2][:, 0:1], ones[0:1, :], top8[0:1, TOPK - 1:TOPK], start=True, stop=True).then_inc(S["near_ps"], 1)
            pe.wait_ge(S["near_ok"], 3)
            nc.tensor.matmul(bank[2][:, 1:2], ones[:, :], n_above[:, :], start=True, stop=True)
            nc.tensor.matmul(bank[3][:, 0:NW], tri[:, :], tied[:, :], start=True, stop=True)
            nc.tensor.matmul(bank[3][:, NW:2 * NW], ones[:, :], tied[:, :], start=True, stop=True).then_inc(S["near_ps"], 1)

            pe.wait_ge(S["chosen_ok"], 1)
            nc.tensor.matmul(bank[3][:, 0:KD], zeros[:, 0:P], zeros[:, 0:KD], start=True, stop=False)

            def start_window(w, j):
                for k in range(KD):
                    nc.tensor.matmul(bank[4 + j][:, k * P:(k + 1) * P], z_stat[:, j, k, :], two_ident[:, :], start=True, stop=True)
                for k in range(KD):
                    last = nc.tensor.matmul(bank[3][:, k:k + 1], z_stat[:, j, k, :], chosen[:, bass.ds(w, 1)],
                                            start=False, stop=False)
                last.then_inc(S["zT_ps"], 1)
            for j in range(2):
                pe.wait_ge(S["zstat_ok"], j + 1)
                start_window(j, j)
            with pe.Fori(1, PAIRS) as q:
                for j in range(2):
                    pe.wait_ge(S["zstat_ok"], q * 2 + j + 1)
                    pe.wait_ge(S["agg_init"], q * 2 + (j - 1))
                    start_window(q * 2 + j, j)
            nc.tensor.matmul(bank[3][:, 0:KD], zeros[:, 0:P], zeros[:, 0:KD], start=False, stop=True).then_inc(S["selps"], 1)

            def group(g, q, slot, first):
                j = slot % 2
                pe.wait_ge(S["sel_ok"], g + 1)
                pe.wait_ge(gathered[slot], q * 64 + 64)
                if not first:
                    pe.wait_ge(S["agg_added"], g - 1)
                for k in range(KD):
                    for t in range(GT):
                        last = nc.tensor.matmul(bank[j][:, k * P:(k + 1) * P], gath[:, slot, t, k * P:(k + 1) * P],
                                                sel[:, j, t, :], start=(t == 0), stop=(t == GT - 1))
                last.then_inc(S["agg_ps"], 1)
            for slot in range(GS):
                group(slot, 0, slot, slot < 2)
            with pe.Fori(1, GROUPS // GS) as q:
                for slot in range(GS):
                    group(q * GS + slot, q, slot, False)

            n_bad = pe.value_load(bad_i[0:1, 0:1], min_val=0, max_val=GROUPS)
            with pe.If(n_bad > 0):
                pe.wait_ge(S["rep_bad"], 1)
                nc.tensor.matmul(bank[4][:, 0:GROUPS], ones[0:1, :], grp_bad[0:1, :], start=True, stop=True).then_inc(S["rep_dst"], 1)
                pe.sem_inc(S["rep_free"], 1)
                with pe.Fori(0, GROUPS) as g:
                    pe.wait_ge(S["rep_got"], g * (16 * GT) + 16 * GT)
                    pe.sem_inc(S["tick3"], 1)
                    with pe.Fori(0, NW) as w:
                        pe.wait_ge(S["rep_sel"], g * NW + (w + 1))
                        for k in range(KD):
                            for t in range(GT):
                                last = nc.tensor.matmul(bank[0][:, k * P:(k + 1) * P], gath[:, 0, t, k * P:(k + 1) * P],
                                                        sel[:, 0, t, :], start=(t == 0), stop=(t == GT - 1))
                        last.then_inc(S["rep_ps"], 1)
                    pe.wait_ge(S["rep_ps"], g * NW + NW)
                    pe.sem_inc(S["rep_free"], 1)

            pe.wait_ge(S["w_small"], 5 * 16)
            nc.tensor.transpose(bank[4][:, 0:NE * FT], b1_rows[0:NE * FT, :], ident[0:NE * FT, 0:NE * FT]).then_inc(S["b1_ps"], 1)
            def convolve(w, j, first):
                pe.wait_ge(S["aggst_ok"], w + 1)
                if not first:
                    pe.wait_ge(S["x1_ok"], w - 1)
                for k in range(KD):
                    last = nc.tensor.matmul(bank[j][:, 0:D], agg_stat[:, j, k, :], gnnw_sb[:, k, :], start=(k == 0), stop=(k == KD - 1))
                last.then_inc(S["conv_ps"], 1)
            convolve(0, 0, True)
            convolve(1, 1, True)
            with pe.Fori(1, PAIRS) as q:
                for j in range(2):
                    convolve(q * 2 + j, j, False)

            def turn_rows(w, j, first):
                pe.wait_ge(S["h_ok"], w + 1)
                if not first:
                    pe.wait_ge(S["hT_ok"], w - 1)
                for k in range(KD):
                    last = nc.tensor.transpose(bank[2 + j][:, k * P:(k + 1) * P], h_tile[:, j, k, :], ident[:, :])
                last.then_inc(S["hT_ps"], 1)

            def logits(q, j):
                pe.wait_ge(S["hT_ok"], q * 2 + j + 1)
                cols = bank[6 + j][:, bass.ds(q * NE, NE)]
                nc.tensor.matmul(cols, ones[0:1, :], gateb_sb[0:1, :], start=True, stop=False)
                for k in range(KD):
                    last = nc.tensor.matmul(cols, h_feat[:, j, k, :], gatew_sb[:, k, :], start=False, stop=(k == KD - 1))
                last.then_inc(S["logit_ps"], 1)
            for j in range(2):
                turn_rows(j, j, True)
            with pe.Fori(0, PAIRS - 1) as q:
                for j in range(2):
                    logits(q, j)
                    turn_rows(q * 2 + (2 + j), j, False)
            for j in range(2):
                logits(PAIRS - 1, j)

            pe.wait_ge(S["pick_ok"], 1)
            HW = NW // 2
            for i in range(2):
                rows = pick[:, i * HW:(i + 1) * HW, :].rearrange("p w e -> p (w e)")
                nc.tensor.matmul(bank[i][:, 0:HW * NE], tri[:, :], rows, start=True, stop=True)
                last = nc.tensor.matmul(bank[2 + i][:, 0:HW * NE], ones[:, :], rows, start=True, stop=True)
            last.then_inc(S["rank_ps"], 1)

            pe.wait_ge(S["b1_ok"], 1)
            def turn_chunk(q, s, first):
                c = s % NCH
                n = CHUNKS[c][1]
                pe.wait_ge(S[f"xs_in{s % 2}"], q * (32 * NCH) + 32 * (s // 2) + 32)
                if not (first and s == 0):
                    pe.wait_ge(S["xT_ok"], q * (4 * NCH) + 2 * s)
                for k in range(KD):
                    for t in range(-(-n // P)):
                        m = min(P, n - t * P)
                        last = nc.tensor.transpose(bank[k][:, t * P:t * P + m], xs_rows[0:m, s % 2, t, k * P:(k + 1) * P], ident[0:m, 0:m])
                last.then_inc(S["xT_ps"], 1)

            def up(q, j, c, first):
                s, n = j * NCH + c, CHUNKS[c][1]
                pe.wait_ge(S["xT_ok"], q * (4 * NCH) + 2 * s + 2)
                if c == 0:
                    pe.wait_ge(S[f"w_in{j}"], q * 32 + 32)
                for f in range(FT):
                    if not (first and s == 0 and f < 2):
                        pe.wait_ge(S["hid_ok"], q * (2 * NCH * FT) + (s * FT + f - 1))
                    for k in range(KD):
                        last = nc.tensor.matmul(bank[2 + f % 2][:, 0:n], w1_sb[:, j, k, f * P:(f + 1) * P], xs_feat[:, s % 2, k, 0:n],
                                                start=(k == 0), stop=(k == KD - 1))
                    last.then_inc(S["l1_ps"], 1)

            def down(q, j, c, first):
                s, n = j * NCH + c, CHUNKS[c][1]
                pe.wait_ge(S["hid_ok"], q * (2 * NCH * FT) + (s + 1) * FT)
                for t in range(4):
                    m = min(P, n - t * P)
                    if not (first and s == 0 and t < 2):
                        pe.wait_ge(S["y_ok"], q * (8 * NCH) + (4 * s + t - 1))
                    for f in range(FT):
                        last = nc.tensor.matmul(bank[4 + t % 2][0:m, 0:D], hid[:, f, t * P:t * P + m], w2_sb[:, j, f, :],
                                                start=(f == 0), stop=(f == FT - 1))
                    last.then_inc(S["l2_ps"], 1)

            def experts(q, first, last):
                for j in range(2):
                    for c in range(NCH):
                        s = j * NCH + c
                        up(q, j, c, first)
                        if s + 1 < 2 * NCH:
                            turn_chunk(q, s + 1, False)
                        elif not last:
                            turn_chunk(q + 1, 0, False)
                        down(q, j, c, first)
            turn_chunk(0, 0, True)
            experts(0, True, False)
            with pe.Fori(1, NE // 2 - 1) as q:
                experts(q, False, False)
            experts(NE // 2 - 1, False, True)


_INS = ["x", "src", "dst", "L0_gnn_r", "L0_gnn_W", "L0_gnn_y", "L0_ffn_gate_w", "L0_ffn_gate_b",
        "L0_ffn_w1", "L0_ffn_b1", "L0_ffn_w2", "L0_ffn_b2"]


def kernel(**inputs):
    import numpy as np
    import concourse.bacc as bacc
    from concourse.bass_utils import run_bass_kernel_spmd as run

    nc = bacc.Bacc("TRN2", target_bir_lowering=False, num_devices=1)
    arrays, args = {}, []
    for name in _INS:
        v = np.ascontiguousarray(inputs[name])
        arrays[f"in_{name}"] = v
        args.append(nc.dram_tensor(f"in_{name}", v.shape, mybir.dt.from_np(v.dtype), kind="ExternalInput").ap())
    out = nc.dram_tensor("out", arrays["in_x"].shape, F32, kind="ExternalOutput").ap()
    build(nc, *args, out)
    r = run(nc, [arrays], core_ids=[0])
    return r.results[0]["out"]
```

```python
import concourse.bass as bass
from concourse import mybir
from contextlib import ExitStack

F32, I32, BF16 = mybir.dt.float32, mybir.dt.int32, mybir.dt.bfloat16
ALU = mybir.AluOpType
ACT = mybir.ActivationFunctionType
AX = mybir.AxisListType

P = 128
STOP_AT = None


def build(nc, x, src, dst, gnn_r, gnn_w, yidx, gate_w, gate_b, w1, b1, w2, b2, out, dbg=None):
    N, D = x.shape
    E = src.shape[0]
    KD = D // P
    NW = -(-N // P)
    LAST = N - (NW - 1) * P
    EPS = 1e-5
    TOPK = 7
    SELF_W = 2.0
    GT = 4
    TILES = -(-E // (P * 16)) * 16
    GROUPS = TILES // GT
    EB = -(-TILES // P)
    FULL = E // P
    FB = FULL // P
    PAD_DST = 16384
    FAR = 1048576.0
    TOP_BASE = float((NW - 1) * P)
    HSTEPS = TILES // 16
    GS = 8
    PAIRS = NW // 2
    ZC = 14
    NZC = NW // ZC
    U = ZC // 2
    NU = NW // U
    DVE_WIN = (NZC - 1) * U
    DVE_NORM = [i for i in range(ZC) if i % 3 == 1]
    ACT_NORM = [i for i in range(ZC) if i % 3 != 1]
    ACT_WIN = NW - DVE_WIN
    NE = gate_w.shape[1]
    F = w1.shape[2]
    FT = F // P
    CAP = max(1, -(-N * 5 // (4 * NE)))
    SLOTS = NE * CAP
    CR = 2 * P
    NCH = -(-CAP // CR)
    CHUNKS = [(c, min(CR, CAP - c)) for c in range(0, CAP, CR)]
    PC = 2 * NCH
    FB2 = FT // 2
    assert NCH % 2 == 0 and FB2 == 4 and KD == 2
    ARENA = 20096

    ctx = ExitStack()
    with ctx:
        def sb(name, shape, dt=F32):
            return ctx.enter_context(nc.sbuf_tensor(name, shape, dt))

        def sem(name):
            return ctx.enter_context(nc.semaphore(name))

        def dram(name, shape, dt=F32):
            return nc.dram_tensor(name, shape, dt, kind="Internal").ap()

        bank = [ctx.enter_context(nc.psum_tensor(f"bank{i}", [P, 512], F32)) for i in range(8)]

        up_bank = [bank[2], bank[3], bank[6], bank[7]]

        def turn_bank(j):
            return j if j < 6 else 2

        z_table = dram("z_table", [NW * P, D])
        dst_rows = dram("dst_rows", [EB * P, P])
        xs = dram("xs", [SLOTS, D])
        ys = dram("ys", [SLOTS, D])

        nodes = sb("nodes", [P, KD, NW, P])
        agg = nodes[:, :, :, :].rearrange("p k w c -> p k (w c)")

        iota_i = sb("iota_i", [P, P], I32)
        iota_b = sb("iota_b", [P, P], BF16)
        ident = sb("ident", [P, P])
        ones = sb("ones", [P, P])
        down_one = sb("down_one", [P, P])
        corner = sb("corner", [P, P])
        tri = sb("tri", [P, P])
        zeros = sb("zeros", [P, D])
        neg_half = sb("neg_half", [P, NW])
        node_i = sb("node_i", [P, NW], I32)
        node_id = sb("node_id", [P, NW])
        win_i = sb("win_i", [P, NW], I32)
        win_f = sb("win_f", [P, NW])
        rep_rel = sb("rep_rel", [P, GT], BF16)

        r_rows = sb("r_rows", [P, D])
        y_i = sb("y_i", [P, 1], I32)
        y_f = sb("y_f", [P, 1])
        wy_i = sb("wy_i", [P, 1], I32)
        is_y = sb("is_y", [P, NW])
        not_y = sb("not_y", [P, NW])
        invalid = sb("invalid", [P, NW])

        arena = sb("arena", [P, ARENA])
        at = [0]

        def carve(shape, dt=F32):
            size = 1
            for n in shape:
                size *= n
            words = size if dt != BF16 else size // 2
            flat = arena[:, at[0]:at[0] + words]
            at[0] += words
            assert at[0] <= ARENA, (at[0], ARENA)
            if dt != F32:
                flat = flat.bitcast(dt)
            if len(shape) == 1:
                return flat
            names = "abcd"[:len(shape)]
            return flat.rearrange(f"p ({' '.join(names)}) -> p {' '.join(names)}", **dict(zip(names[1:], shape[1:])))

        gath = carve([GS, GT, D])
        at[0] = 0
        HALF = 2 * EB * P
        stage_i = carve([2, EB, P], I32)
        stage_f = carve([2, EB, P])
        grp_min = carve([GROUPS])[0:1, :]
        grp_max = carve([GROUPS])[0:1, :]
        at[0] = 0
        dst_i = carve([EB * P], I32)
        low_i = carve([EB * P], I32)
        lim_row = carve([2, EB * P])[0:1, :, :]
        at[0] = GS * GT * D
        src_idx = carve([EB * P], I32)
        dst_f = carve([EB * P])
        lo_b = carve([EB * P], BF16)
        hi_b = carve([EB * P], BF16)
        rel_b = carve([EB * P], BF16)
        here = at[0]
        oh_lo = carve([2, 16, P], BF16)
        oh_hi = carve([2, 16, NW], BF16)
        at[0] = here
        stage_f2 = carve([EB, P])
        at[0] = here
        near_row = carve([8 * P])[0:1, :]
        at[0] = here
        cross_row = carve([TILES])[0:1, :]
        at[0] = here
        sel = carve([2, GT, P])
        at[0] = here + (2 * 16 * (P + NW)) // 2
        idx_ring = carve([2, 16], I32)
        bn1 = carve([NW, 6])
        last_i = carve([EB], I32)
        last_low = carve([EB], I32)
        last_lo = carve([16], BF16)
        last_hi = carve([16], BF16)
        first_ring = carve([2, U], I32)
        at[0] = 0
        first_rows = carve([2, U, P])
        is_less = carve([U, P])
        diff = carve([2, U, KD, P])
        at[0] = here + GT * P * 2
        z_stat = carve([U, KD, P])
        z_back = carve([2, D])

        at[0] = here + (2 * 16 * (P + NW)) // 2
        grp_far = carve([GROUPS])

        at[0] = 0
        w1_sb = carve([2, KD, F])
        w2_sb = carve([2, FT, D])
        b2_rows = carve([NE, D])
        gnnw_sb = carve([KD, D])
        gatew_sb = carve([KD, NE])
        b1_cols = carve([NE * FT])
        turn = at[0]
        x_tile = carve([U, D])
        agg_stat = carve([U, KD, P])
        at[0] = turn
        h_tile = carve([U, KD, P])
        h_feat = carve([U, KD, P])
        bn = carve([NW, 6])
        gate_l = carve([NW, NE])
        gate_e = carve([NW, NE])
        gate_t = carve([NW, NE])
        pick = carve([NW, NE])
        b1_rows = carve([P])
        at[0] = turn
        h_send = carve([ZC, D])
        send_idx = carve([2, ZC // 2], I32)
        at[0] = turn
        xs_rows = carve([2, 2, D])
        xs_feat = carve([2, KD, CR])
        hid = carve([FT, CR])
        y_tile = carve([4, D])
        b1_pair = carve([2 * FT])
        at[0] = turn
        y_got = carve([ZC, D])
        y_gated = carve([D])
        y_clip = carve([D])
        y_low = carve([D])
        y_fin = carve([D], I32)
        o_tile = carve([U, D])
        row_sum = carve([NW])
        odd = carve([NW])
        odd_n = carve([1])
        odd_i = carve([1], I32)
        take_idx = carve([2, ZC // 2], I32)

        tile_lim = sb("tile_lim", [P, 2, EB])
        grp_base = sb("grp_base", [1, GROUPS])
        grp_bad = sb("grp_bad", [1, GROUPS])
        grp_cmp = sb("grp_cmp", [1, GROUPS])
        base_i = sb("base_i", [1, GROUPS], I32)
        bad_sum = sb("bad_sum", [1, 1])
        bad_i = sb("bad_i", [1, 1], I32)
        mine_y = sb("mine_y", [P, 1])
        r_y = sb("r_y", [P, D])
        EDGE_TURNS = [(i, b, min(4, EB - b)) for i in range(2) for b in range(0, EB, 4)]
        LIM_TURNS = EDGE_TURNS

        neg_mean = sb("neg_mean", [P, NW])
        rstd = sb("rstd", [P, NW])
        shift = sb("shift", [P, NW])
        dist = sb("dist", [P, NW])
        deg = sb("deg", [P, NW])
        last_hist = sb("last_hist", [P, NW])
        first_f = sb("first_f", [P, NW])
        first_i = sb("first_i", [P, NW], I32)
        n_less = sb("n_less", [P, NW])
        row_start = sb("row_start", [P, NW + 1])
        disorder = sb("disorder", [P, 1])
        cross_sum = sb("cross_sum", [1, 1])
        unsorted_i = sb("unsorted_i", [1, 1], I32)
        dinv = sb("dinv", [P, NW])

        near = sb("near", [P, NW])
        near8 = sb("near8", [P, 8])
        top8 = sb("top8", [1, 8])
        thr = sb("thr", [P, 1])
        above = sb("above", [P, NW])
        tied = sb("tied", [P, NW])
        n_above = sb("n_above", [P, 1])
        room = sb("room", [P, 1])
        tie_scan = sb("tie_scan", [P, NW])
        tie_rank = sb("tie_rank", [P, NW])
        chosen = sb("chosen", [P, NW])

        col_fix = sb("col_fix", [P, KD])

        mean2 = sb("mean2", [P, NW])
        var2 = sb("var2", [P, NW])
        gap2 = sb("gap2", [P, NW])
        rstd2 = sb("rstd2", [P, NW])
        shift2 = sb("shift2", [P, NW])
        best = sb("best", [P, NW])
        norm = sb("norm", [P, NW])
        expert = sb("expert", [P, NW])
        place = sb("place", [P, NW])
        kept = sb("kept", [P, NW])
        weight = sb("weight", [P, NW])
        slot_f = sb("slot_f", [P, NW])
        put_idx = sb("put_idx", [P, NW], I32)
        get_idx = sb("get_idx", [P, NW], I32)
        rank_e = sb("rank_e", [P, NE])
        iota_f = sb("iota_f", [P, NE])
        gateb_sb = sb("gateb_sb", [P, NE])
        taken_f = sb("taken_f", [1, NE])
        taken_i = sb("taken_i", [1, NE + 1], I32)

        S = {}
        for name in ("""edges_cleared edges_in r_in y_in consts edges_float edge_psum edges_out lims limps lim_rows bases
                     cmp_ps hist_built hist_used hist_ps mean_sum square_ok ssum dst_rows_out last_built first_ok
                     first_idx first_in0 first_in1 first_used starts_ok starts_ps hist_start less_ok bn1_ok shift_ok
                     mem_ok mem_patched diff_ok dist_ok deg_ok z_ok tick near_ok near_ps chosen_ok zstat_ok zT_ps
                     agg_init selps idx_ok sel_ok agg_ps agg_added fixed xt_in2 xt_in3 xt_in4 xt_in5 xt_in6 out_done2
                     out_done3 out_done4 out_done5 out_done6 zb_in0 zb_in1 zb_used odd_rows odd_ps odd_ok clean_ok
                     clean_out clean_free clean_idx clean_got rep_idx rep_got rep_free rep_relok rep_sel rep_ps
                     rep_added rep_bad rep_dst clean bn_ok zeroed rows_zero w_small w_in0 w_in1 xt_in0 xt_in1 aggst_ok
                     conv_ps x1_ok var_ok lnb_ok h_ok h_dve hT_ps hT_ok logit_ps gate_taken gate_in gate_out pick_ok
                     rank_ps routed send_h sidx sent0 sent1 xs_in0 xs_in1 xT_ps xT_ok l1_ps hid_ok l2_ps y_ok ys_out0
                     ys_out1 ys_out2 ys_out3 b1_now tidx got0 got1 o_ok out_done0 out_done1 b1_ps b1_ok dve_ch pool_ch""").split():
            S[name] = sem(name)
        x_chunk = [sem(f"x_chunk{c}") for c in range(NZC)]
        table_out = [sem(f"table_out{c}") for c in range(NZC)]
        gathered = [sem(f"gathered{i}") for i in range(GS)]

        def tally(name):
            return [S[name], 0]

        block = ctx.enter_context(nc.Block())

        x_win = x[0:(NW - 1) * P, :].rearrange("(w p) (k c) -> p k w c", p=P, k=KD)
        x_last = x[(NW - 1) * P:N, :].rearrange("p (k c) -> p k c", k=KD)
        z_win = z_table.rearrange("(w p) (k c) -> p k w c", p=P, k=KD)

        @block.sync
        def _(sp):
            for i, e in enumerate((dst, src)):
                sp.dma_start(stage_i[:, i, 0:FB, :],
                             e[0:FB * P * P].rearrange("(b r e) -> r b e", r=P, e=P)).then_inc(S["edges_in"], 16)
            sp.wait_ge(S["edges_cleared"], 2)
            for i, e in enumerate((dst, src)):
                rows = FULL - FB * P
                sp.dma_start(stage_i[0:rows, i, FB, :],
                             e[FB * P * P:FULL * P].rearrange("(r e) -> r e", e=P)).then_inc(S["edges_in"], 16)
                sp.dma_start(stage_i[rows:rows + 1, i, FB, 0:E - FULL * P],
                             e[FULL * P:E].rearrange("(r e) -> r e", r=1)).then_inc(S["edges_in"], 16)
            sp.dma_start(y_i[:, :], yidx.rearrange("(a b) -> a b", a=1).to_broadcast([P, 1])).then_inc(S["y_in"], 16)
            sp.dma_start(r_rows[:, :], gnn_r.to_broadcast([P, D])).then_inc(S["r_in"], 16)
            def load_nodes(c):
                a, b = c * ZC, min((c + 1) * ZC, NW - 1)
                for k in range(KD):
                    sp.dma_start(nodes[:, k, a:b, :], x_win[:, k, a:b, :]).then_inc(x_chunk[c], 16)
            sp.wait_ge(S["edges_float"], 1)
            sp.dma_start(dst_rows.rearrange("(b r) e -> r b e", r=P), stage_f[:, 0, :, :]).then_inc(S["dst_rows_out"], 16)
            for c in range(NZC):
                load_nodes(c)
            sp.wait_ge(S["edges_cleared"], 3)
            sp.dma_start(nodes[0:LAST, :, NW - 1, :], x_last).then_inc(x_chunk[NZC - 1], 16)

            for c in range(NZC):
                sp.wait_ge(S["z_ok"], c + 1)
                for k in range(KD):
                    sp.dma_start(z_win[:, k, c * ZC:(c + 1) * ZC, :],
                                 nodes[:, k, c * ZC:(c + 1) * ZC, :]).then_inc(table_out[c], 16)

            def load_weights(e, j, small=False):
                sp.dma_start(w1_sb[:, j, :, :], w1[bass.ds(e, 1), :, :].rearrange("o (k p) f -> p (o k) f", p=P)).then_inc(S[f"w_in{j}"], 16)
                sp.dma_start(w2_sb[:, j, :, :], w2[bass.ds(e, 1), :, :].rearrange("o (t p) d -> p (o t) d", p=P)).then_inc(S[f"w_in{j}"], 16)

            for j in range(2):
                sp.wait_ge(S["agg_init"], NW)
                sp.dma_start(z_back[:, j, :], z_table[j * P:(j + 1) * P, :]).then_inc(S[f"zb_in{j}"], 16)
            with sp.Fori(1, PAIRS) as q:
                for j in range(2):
                    sp.wait_ge(S["zb_used"], q * 2 + (j - 1))
                    sp.dma_start(z_back[:, j, :], z_table[bass.ds((q * 2 + j) * P, P), :]).then_inc(S[f"zb_in{j}"], 16)

            sp.wait_ge(S["fixed"], 1)
            sp.dma_start(gnnw_sb, gnn_w.rearrange("(k p) d -> p k d", p=P)).then_inc(S["w_small"], 16)
            sp.dma_start(gatew_sb, gate_w.rearrange("(k p) e -> p k e", p=P)).then_inc(S["w_small"], 16)
            sp.dma_start(gateb_sb[:, :], gate_b.rearrange("(o e) -> o e", o=1).to_broadcast([P, NE])).then_inc(S["w_small"], 16)
            sp.dma_start(b1_rows[0:NE * FT, :], b1.rearrange("e (t c) -> (e t) c", c=P)).then_inc(S["w_small"], 16)
            sp.dma_start(b2_rows, b2.rearrange("(o e) d -> o e d", o=1).to_broadcast([P, NE, D])).then_inc(S["w_small"], 16)

            def load_x(w, j):
                sp.dma_start(x_tile[:, j, :], x[bass.ds(w * P, P), :]).then_inc(S[f"xt_in{j}"], 16)
            for j in range(U):
                load_x(j, j)
            with sp.Fori(1, NU - 1) as q:
                for j in range(U):
                    sp.wait_ge(S["x1_ok"], q * U + (j - U + 1))
                    load_x(q * U + j, j)
            for j in range(U):
                w = NW - U + j
                n = P if w < NW - 1 else LAST
                sp.wait_ge(S["x1_ok"], w - U + 1)
                sp.dma_start(x_tile[0:n, j, :], x[w * P:w * P + n, :]).then_inc(S[f"xt_in{j}"], 16)
            load_weights(0, 0)
            load_weights(1, 1)

            def load_chunk(e, c, slot):
                c0, n = CHUNKS[c]
                full = n // P
                sp.dma_start(xs_rows[:, slot, 0:full, :],
                             xs[bass.ds(e * CAP + c0, full * P), :].rearrange("(t p) d -> p t d", p=P)).then_inc(S[f"xs_in{slot}"], 16)
                if n % P:
                    sp.dma_start(xs_rows[0:n % P, slot, full:full + 1, :],
                                 xs[bass.ds(e * CAP + (c0 + full * P), n % P), :].rearrange("(t p) d -> p t d", t=1)).then_inc(S[f"xs_in{slot}"], 16)
                else:
                    sp.sem_inc(S[f"xs_in{slot}"], 16)

            def load_or_skip(e, c, slot, took):
                with sp.If(took > CHUNKS[c][0]):
                    load_chunk(e, c, slot)
                with sp.Else():
                    sp.sem_inc(S[f"xs_in{slot}"], 32)

            def expert_pair(q, last):
                took = [sp.value_load(taken_i[0:1, bass.ds(q * 2 + i, 1)], min_val=0, max_val=N) for i in range(3)]
                for j in range(2):
                    for c in range(NCH):
                        s = j * NCH + c
                        more = s + 2
                        sp.wait_ge(S["xT_ps"], q * PC + (s + 2))
                        sp.sem_inc(S["tick"], 1)
                        if not (last and more >= PC):
                            load_or_skip(q * 2 + more // NCH, more % NCH, s % 2, took[more // NCH])
                        with sp.If(took[j] > CHUNKS[c][0]):
                            for t in range(2):
                                n, slot = min(P, CHUNKS[c][1] - t * P), s % 2 * 2 + t
                                sp.wait_ge(S["y_ok"], q * (2 * PC) + (2 * s + t + 3))
                                sp.dma_start(ys[bass.ds((q * 2 + j) * CAP + (CHUNKS[c][0] + t * P), n), :],
                                             y_tile[0:n, slot, :]).then_inc(S[f"ys_out{slot}"], 16)
                        with sp.Else():
                            for slot in (s % 2 * 2, s % 2 * 2 + 1):
                                sp.wait_ge(S[f"ys_out{slot}"], q * (16 * NCH) + (16 * (s // 2) + 16))
                                sp.sem_inc(S[f"ys_out{slot}"], 16)
                    if not last:
                        sp.wait_ge(S["y_ok"], q * (2 * PC) + (2 * (j + 1) * NCH + 2))
                        load_weights(q * 2 + (j + 2), j)
            sp.wait_ge(S["rows_zero"], 32 * (SLOTS // P + 1))
            sp.wait_ge(S["sent0"], 16 * ZC // 2 * NZC)
            sp.wait_ge(S["sent1"], 16 * ZC // 2 * NZC)
            for slot in range(4):
                sp.sem_inc(S[f"ys_out{slot}"], 16)
            for c in range(2):
                load_or_skip(0, c, c, sp.value_load(taken_i[0:1, 0:1], min_val=0, max_val=N))
            with sp.Fori(0, NE // 2 - 1) as q:
                expert_pair(q, False)
            expert_pair(NE // 2 - 1, True)

            with sp.Fori(0, NU - 1) as q:
                for j in range(U):
                    sp.wait_ge(S["o_ok"], q * U + j + 1)
                    sp.dma_start(out[bass.ds((q * U + j) * P, P), :], o_tile[:, j, :]).then_inc(S[f"out_done{j}"], 16)
            for j in range(U):
                w = NW - U + j
                n = P if w < NW - 1 else LAST
                sp.wait_ge(S["o_ok"], w + 1)
                sp.dma_start(out[w * P:w * P + n, :], o_tile[0:n, j, :]).then_inc(S[f"out_done{j}"], 16)
            for j in range(U):
                sp.wait_ge(S[f"out_done{j}"], 16 * NU)
            sp.wait_ge(S["odd_ok"], 1)
            n_odd = sp.value_load(odd_i[0:1, 0:1], min_val=0, max_val=P * NW)
            with sp.If(n_odd > 0):
                with sp.Fori(0, NW - 1) as w:
                    sp.wait_ge(S["clean_ok"], w + 1)
                    sp.dma_start(out[bass.ds(w * P, P), :], o_tile[:, 0, :]).then_inc(S["clean_out"], 16)
                sp.wait_ge(S["clean_ok"], NW)
                sp.dma_start(out[(NW - 1) * P:N, :], o_tile[0:LAST, 0, :]).then_inc(S["clean_out"], 16)
                sp.wait_ge(S["clean_out"], 16 * NW + 16)
            for t in range(4):
                sp.wait_ge(S[f"ys_out{t}"], 16 * (NE * NCH // 2 + 1))

        @block.gpsimd
        def _(pool):
            nc.gpsimd.memset(stage_i[:, 0, FB, :], PAD_DST).then_inc(S["edges_cleared"], 1)
            nc.gpsimd.memset(stage_i[:, 1, FB:EB, :], 0).then_inc(S["edges_cleared"], 1)
            pool.wait_ge(S["edges_cleared"], 2)
            nc.gpsimd.memset(nodes[64:P, :, NW - 1, :], 0.0).then_inc(S["edges_cleared"], 1)
            pool.wait_ge(S["edges_cleared"], 3)
            nc.gpsimd.iota(iota_i[:, :], [[1, P]], base=0, channel_multiplier=0).then_inc(S["pool_ch"], 1)
            nc.gpsimd.iota(node_i[:, :], [[P, NW]], base=0, channel_multiplier=1).then_inc(S["pool_ch"], 1)
            nc.gpsimd.iota(win_i[:, :], [[P, NW]], base=0, channel_multiplier=0).then_inc(S["pool_ch"], 1)
            nc.gpsimd.memset(zeros[:, :], 0.0).then_inc(S["pool_ch"], 1)
            nc.gpsimd.memset(ones[:, :], 1.0).then_inc(S["pool_ch"], 1)
            nc.gpsimd.memset(neg_half[:, :], -0.5).then_inc(S["pool_ch"], 1)
            pool.wait_ge(S["pool_ch"], 6)
            pool.sem_inc(S["zeroed"], 1)
            nc.gpsimd.tensor_copy(iota_b[:, :], iota_i[:, :]).then_inc(S["consts"], 1)
            nc.gpsimd.tensor_copy(node_id[:, :], node_i[:, :]).then_inc(S["consts"], 1)
            nc.gpsimd.tensor_copy(win_f[:, :], win_i[:, :]).then_inc(S["consts"], 1)
            for m, shifted in ((ident, 0), (down_one, -1), (corner, P - 1)):
                nc.gpsimd.affine_select(out=m[:, :], in_=zeros[:, 0:P], compare_op=ALU.not_equal, fill=1.0,
                                        base=shifted, pattern=[[-1, P]], channel_multiplier=1).then_inc(S["consts"], 1)
            nc.gpsimd.affine_select(out=tri[:, :], in_=ones[:, :], compare_op=ALU.is_ge, fill=0.0,
                                    base=0, pattern=[[1, P]], channel_multiplier=-1).then_inc(S["consts"], 1)

            pool.wait_ge(S["first_ok"], 1)
            pool.wait_ge(S["dst_rows_out"], 16)

            def fetch_first(q, half, first):
                if not first:
                    pool.wait_ge(S["first_used"], q * 2 + (half - 1))
                    pool.sem_inc(S["tick"], 1)
                nc.gpsimd.tensor_copy(first_ring[:, half, :], first_i[:, bass.ds(q * ZC + half * U, U)]).then_inc(S["first_idx"], 1)
                pool.wait_ge(S["first_idx"], q * 2 + (half + 1))
                pool.sem_inc(S["tick"], 1)
                for i in range(U):
                    nc.gpsimd.indirect_dma_start(
                        first_rows[:, half, i, :], None, dst_rows,
                        bass.IndirectOffsetOnAxis(ap=first_ring[:, half, i:i + 1], axis=0)).then_inc(S[f"first_in{half}"], 16)
            fetch_first(0, 0, True)
            fetch_first(0, 1, True)
            with pool.Fori(1, NZC // 2 + 1) as q:
                fetch_first(q, 0, False)
                fetch_first(q, 1, False)

            pool.wait_ge(S["ssum"], 1)
            nc.gpsimd.tensor_tensor(rstd[:, :], var2[:, :], neg_half[:, :], ALU.pow).then_inc(S["pool_ch"], 1)
            pool.wait_ge(S["pool_ch"], 7)
            nc.gpsimd.tensor_tensor(rstd[:, :], rstd[:, :], not_y[:, :], ALU.mult).then_inc(S["pool_ch"], 1)
            pool.wait_ge(S["pool_ch"], 8)
            nc.gpsimd.tensor_tensor(shift[:, :], rstd[:, :], neg_mean[:, :], ALU.mult).then_inc(S["shift_ok"], 1)
            with pool.Fori(NZC // 2 + 1, NZC) as q:
                fetch_first(q, 0, False)
                fetch_first(q, 1, False)

            pool.wait_ge(S["deg_ok"], 1)
            nc.gpsimd.tensor_tensor(dinv[:, :], deg[:, :], neg_half[:, :], ALU.pow).then_inc(S["deg_ok"], 1)

            for c in range(NZC):
                pool.wait_ge(table_out[c], 16 * KD)
            pool.wait_ge(S["dist_ok"], 2 * NZC)
            STEPS = TILES // 32
            def take_indices(t0, half):
                nc.gpsimd.tensor_copy(idx_ring[:, half, :], src_idx[:, bass.ds(t0, 16)]).then_inc(S["idx_ok"], 1)

            def gather_body(q, first):
                for half in range(2):
                    if not first:
                        for s in range(4):
                            pool.wait_ge(gathered[half * 4 + s], q * 64)
                        pool.sem_inc(S["tick"], 1)
                    take_indices(q * 32 + half * 16, half)
                    pool.wait_ge(S["idx_ok"], q * 2 + half + 1)
                    pool.sem_inc(S["tick"], 1)
                    for s in range(4):
                        slot = half * 4 + s
                        if not first:
                            pool.wait_ge(S["agg_ps"], (q - 1) * 8 + slot + 1)
                            pool.sem_inc(S["tick"], 1)
                        for t in range(GT):
                            nc.gpsimd.indirect_dma_start(
                                gath[:, slot, t, :], None, z_table,
                                bass.IndirectOffsetOnAxis(ap=idx_ring[:, half, s * GT + t:s * GT + t + 1], axis=0),
                            ).then_inc(gathered[slot], 16)

            gather_body(0, True)
            with pool.Fori(1, STEPS) as q:
                gather_body(q, False)


            pool.wait_ge(S["bases"], 1)
            n_bad = pool.value_load(bad_i[0:1, 0:1], min_val=0, max_val=GROUPS)
            with pool.If(n_bad > 0):
                pool.wait_ge(S["agg_ps"], GROUPS)
                with pool.Fori(0, GROUPS) as g:
                    pool.wait_ge(S["rep_free"], g + 1)
                    pool.sem_inc(S["tick"], 1)
                    nc.gpsimd.tensor_copy(idx_ring[:, 0, 0:GT], src_idx[:, bass.ds(g * GT, GT)]).then_inc(S["rep_idx"], 1)
                    pool.wait_ge(S["rep_idx"], g + 1)
                    pool.sem_inc(S["tick"], 1)
                    for t in range(GT):
                        nc.gpsimd.indirect_dma_start(
                            gath[:, 0, t, :], None, z_table,
                            bass.IndirectOffsetOnAxis(ap=idx_ring[:, 0, t:t + 1], axis=0)).then_inc(S["rep_got"], 16)

            pool.wait_ge(S["var_ok"], 1)
            nc.gpsimd.tensor_tensor(rstd2[:, :], var2[:, :], neg_half[:, :], ALU.pow).then_inc(S["var_ok"], 1)

            pool.wait_ge(S["routed"], 1)
            pool.wait_ge(S["rows_zero"], 32 * (SLOTS // P + 1))
            last_row = pool.to_reg(SLOTS - 1)
            HZ = ZC // 2

            def index_half(to, frm, q, half, s_idx):
                nc.gpsimd.tensor_copy(to[:, half, :], frm[:, bass.ds(q * ZC + half * HZ, HZ)]).then_inc(S[s_idx], 1)
                pool.wait_ge(S[s_idx], q * 2 + half + 1)
                pool.sem_inc(S["tick"], 1)

            def send(q, first):
                for half in range(2):
                    if not first:
                        pool.wait_ge(S[f"sent{half}"], q * (16 * HZ))
                        pool.sem_inc(S["tick"], 1)
                    index_half(send_idx, put_idx, q, half, "sidx")
                    for s in range(HZ):
                        pool.wait_ge(S["send_h"], q * ZC + (half * HZ + s + 1))
                        pool.sem_inc(S["tick"], 1)
                        nc.gpsimd.indirect_dma_start(
                            xs, bass.IndirectOffsetOnAxis(ap=send_idx[:, half, s:s + 1], axis=0), h_send[:, half * HZ + s, :], None,
                            bounds_check=last_row, oob_is_err=False).then_inc(S[f"sent{half}"], 16)
            send(0, True)
            with pool.Fori(1, NZC) as q:
                send(q, False)

            for t in range(4):
                pool.wait_ge(S[f"ys_out{t}"], 16 * (NE * NCH // 2 + 1))

            def fetch(q, first):
                for half in range(2):
                    if not first:
                        pool.wait_ge(S["o_ok"], q * ZC + (half * HZ - HZ))
                        pool.sem_inc(S["tick"], 1)
                    index_half(take_idx, get_idx, q, half, "tidx")
                    for s in range(HZ):
                        nc.gpsimd.indirect_dma_start(
                            y_got[:, half * HZ + s, :], None, ys,
                            bass.IndirectOffsetOnAxis(ap=take_idx[:, half, s:s + 1], axis=0),
                            bounds_check=last_row, oob_is_err=False).then_inc(S[f"got{half}"], 16)
            fetch(0, True)
            with pool.Fori(1, NZC) as q:
                fetch(q, False)
            pool.wait_ge(S["odd_ok"], 1)
            n_odd = pool.value_load(odd_i[0:1, 0:1], min_val=0, max_val=P * NW)
            with pool.If(n_odd > 0):
                with pool.Fori(0, NW) as w:
                    pool.wait_ge(S["clean_free"], w + 1)
                    pool.sem_inc(S["tick"], 1)
                    nc.gpsimd.tensor_copy(take_idx[:, 0, 0:1], get_idx[:, bass.ds(w, 1)]).then_inc(S["clean_idx"], 1)
                    pool.wait_ge(S["clean_idx"], w + 1)
                    pool.sem_inc(S["tick"], 1)
                    nc.gpsimd.indirect_dma_start(
                        y_got[:, 0, :], None, ys, bass.IndirectOffsetOnAxis(ap=take_idx[:, 0, 0:1], axis=0),
                        bounds_check=last_row, oob_is_err=False).then_inc(S["clean_got"], 16)

        @block.scalar
        def _(act):
            def node_row(w):
                return nodes[:, :, w, :]

            act.wait_ge(S["shift_ok"], 1)
            with act.Fori(0, ACT_WIN // 2) as q:
                for j in range(2):
                    nc.scalar.activation(node_row(q * 2 + j), node_row(q * 2 + j), ACT.Identity,
                                         bias=shift[:, bass.ds(q * 2 + j, 1)],
                                         scale=rstd[:, bass.ds(q * 2 + j, 1)]).then_inc(S["mean_sum"], 1)
            act.wait_ge(S["mean_sum"], ACT_WIN)
            act.sem_inc(S["mem_ok"], 1)
            for b in range(2 * NZC):
                act.wait_ge(S["diff_ok"], KD * (b + 1))
                nc.scalar.activation(diff[:, b % 2, :, :, :], diff[:, b % 2, :, :, :], ACT.Square).then_inc(S["square_ok"], 1)

            def z_tile(w, j):
                nc.scalar.activation(z_stat[:, j, :, :], node_row(w), ACT.Copy).then_inc(S["zstat_ok"], 1)
            act.wait_ge(S["z_ok"], 1)
            for i in range(ZC):
                if i >= U:
                    act.wait_ge(S["zT_ps"], i - U + 1)
                z_tile(i, i % U)
            with act.Fori(1, NZC) as q:
                act.wait_ge(S["z_ok"], q + 1)
                act.sem_inc(S["tick"], 1)
                for i in range(ZC):
                    act.wait_ge(S["zT_ps"], q * ZC + (i - U + 1))
                    z_tile(q * ZC + i, i % U)

            act.wait_ge(S["zeroed"], 1)
            ROW_WIN = SLOTS // P
            with act.Fori(0, ROW_WIN) as i:
                act.wait_ge(S["agg_ps"], i * (GROUPS // ROW_WIN) + 1)
                for rows in (xs, ys):
                    act.dma_start(rows[bass.ds(i * P, P), :], zeros[:, :]).then_inc(S["rows_zero"], 16)
            for rows in (xs, ys):
                act.dma_start(rows[ROW_WIN * P:SLOTS, :], zeros[0:SLOTS - ROW_WIN * P, :]).then_inc(S["rows_zero"], 16)

            act.wait_ge(S["fixed"], 1)
            def agg_tile(w, j):
                nc.scalar.activation(agg_stat[:, j, :, :], node_row(w), ACT.Copy).then_inc(S["aggst_ok"], 1)
            for j in range(U):
                agg_tile(j, j)
            with act.Fori(1, NU) as q:
                for j in range(U):
                    act.wait_ge(S["conv_ps"], q * U + (j - U + 1))
                    agg_tile(q * U + j, j)
            act.wait_ge(S["lnb_ok"], 1)
            def norm_tile(to, w, sm):
                nc.scalar.activation(to, node_row(w), ACT.Identity, bias=shift2[:, bass.ds(w, 1)],
                                     scale=rstd2[:, bass.ds(w, 1)]).then_inc(S[sm], 1)
            for i in ACT_NORM:
                if i >= U:
                    act.wait_ge(S["hT_ps"], i - U + 1)
                    act.sem_inc(S["tick"], 1)
                norm_tile(h_tile[:, i % U, :, :], i, "h_ok")
            with act.Fori(1, NZC) as q:
                for i in ACT_NORM:
                    act.wait_ge(S["hT_ps"], q * ZC + (i - U + 1))
                    act.sem_inc(S["tick"], 1)
                    norm_tile(h_tile[:, i % U, :, :], q * ZC + i, "h_ok")
            act.wait_ge(S["gate_in"], 1)
            nc.scalar.activation(gate_e, gate_l, ACT.Exp).then_inc(S["gate_out"], 1)
            act.wait_ge(S["routed"], 1)
            def send_tile(w, s):
                norm_tile(h_send[:, s, :].rearrange("p (k c) -> p k c", k=KD), w, "send_h")
            for s in range(ZC):
                send_tile(s, s)
            with act.Fori(1, NZC) as q:
                for half in range(2):
                    act.wait_ge(S[f"sent{half}"], q * (16 * ZC // 2))
                    act.sem_inc(S["tick"], 1)
                    for s in range(half * ZC // 2, (half + 1) * ZC // 2):
                        send_tile(q * ZC + s, s)

            act.sem_inc(S["hid_ok"], FT)
            with act.Fori(0, NE // 2) as q:
                took = [act.value_load(taken_i[0:1, bass.ds(q * 2 + i, 1)], min_val=0, max_val=N) for i in range(2)]
                act.wait_ge(S["hid_ok"], q * (PC * FT) + FT)
                nc.scalar.activation(b1_pair, b1_cols[:, bass.ds(q * (2 * FT), 2 * FT)], ACT.Copy).then_inc(S["b1_now"], 1)
                act.wait_ge(S["b1_now"], q + 1)
                act.sem_inc(S["tick"], 1)
                for j in range(2):
                    for c in range(NCH):
                        n, s = CHUNKS[c][1], j * NCH + c
                        with act.If(took[j] > CHUNKS[c][0]):
                            act.wait_ge(S["l2_ps"], q * (2 * PC) + (2 * s + 2))
                            for f in range(FT):
                                act.wait_ge(S["l1_ps"], q * (PC * FB2) + ((s + 2) * FB2 + f // 2 + 1))
                                nc.scalar.activation(hid[:, f, 0:n], up_bank[f // 2][:, f % 2 * CR:f % 2 * CR + n], ACT.Relu,
                                                     bias=b1_pair[:, j * FT + f:j * FT + f + 1]).then_inc(S["hid_ok"], 1)
                        with act.Else():
                            act.wait_ge(S["hid_ok"], q * (PC * FT) + (s + 1) * FT)
                            act.sem_inc(S["hid_ok"], FT)

        @block.vector
        def _(dve):
            ch = [0]

            def then(ins):
                ch[0] += 1
                ins.then_inc(S["dve_ch"], 1)
                dve.wait_ge(S["dve_ch"], ch[0])

            dve.wait_ge(S["edges_in"], 6 * 16)
            nc.vector.tensor_copy(stage_f[:, 0, :, :], stage_i[:, 0, :, :]).then_inc(S["edges_float"], 1)
            nc.vector.tensor_copy(stage_f[:, 1, :, :], stage_i[:, 1, :, :]).then_inc(S["edges_float"], 1)
            dve.wait_ge(S["edges_float"], 1)
            then(nc.vector.tensor_tensor(stage_f2[:, :, 0:P - 1], stage_f[:, 0, :, 0:P - 1], stage_f[:, 0, :, 1:P], ALU.is_gt))
            then(nc.vector.tensor_reduce(disorder[:, :], stage_f2[:, :, 0:P - 1], AX.XY, ALU.add))
            then(nc.vector.tensor_copy(last_i, stage_f[:, 0, :, P - 1]))
            then(nc.vector.tensor_single_scalar(last_low, last_i, 127, ALU.bitwise_and))
            then(nc.vector.tensor_copy(last_lo[:, 0:EB], last_low))
            then(nc.vector.tensor_single_scalar(last_low, last_i, 7, ALU.arith_shift_right))
            then(nc.vector.tensor_copy(last_hi[:, 0:EB], last_low))
            then(nc.vector.tensor_reduce(tile_lim[:, 0, :], stage_f[:, 0, :, :], AX.X, ALU.min))
            then(nc.vector.scalar_tensor_tensor(stage_f2[:, :, :], stage_f[:, 0, :, :], float(PAD_DST), stage_f[:, 0, :, :],
                                                ALU.is_lt, ALU.mult))
            nc.vector.tensor_reduce(tile_lim[:, 1, :], stage_f2[:, :, :], AX.X, ALU.max).then_inc(S["lims"], 1)
            for n, (i, b0, nb) in enumerate(EDGE_TURNS):
                dve.wait_ge(S["edge_psum"], n + 1)
                to = (dst_f if i == 0 else src_idx)[:, b0 * P:(b0 + nb) * P]
                nc.vector.tensor_copy(to, bank[n % 2][:, 0:nb * P]).then_inc(S["edges_out"], 1)
            dve.wait_ge(S["edges_out"], len(EDGE_TURNS))
            dve.wait_ge(S["dst_rows_out"], 16)
            for n in range(len(LIM_TURNS)):
                i, b0, nb = LIM_TURNS[n]
                dve.wait_ge(S["limps"], n + 1)
                then(nc.vector.tensor_copy(lim_row[0:1, i, b0 * P:(b0 + nb) * P], bank[2 + n % 2][0:1, 0:nb * P]))
                dve.sem_inc(S["lim_rows"], 1)
            lim_grp = lim_row[0:1, :, 0:TILES].rearrange("p i (g t) -> p i g t", t=GT)
            then(nc.vector.tensor_reduce(grp_min[:, :], lim_grp[:, 0, :, :], AX.X, ALU.min))
            then(nc.vector.tensor_reduce(grp_max[:, :], lim_grp[:, 1, :, :], AX.X, ALU.max))
            then(nc.vector.tensor_scalar(grp_base[:, :], grp_min[:, :], TOP_BASE, None, ALU.min))
            then(nc.vector.tensor_tensor(grp_max[:, :], grp_max[:, :], grp_base[:, :], ALU.subtract))
            then(nc.vector.tensor_scalar(grp_bad[:, :], grp_max[:, :], float(P), None, ALU.is_ge))
            then(nc.vector.tensor_reduce(bad_sum[:, :], grp_bad[:, :], AX.X, ALU.add))
            then(nc.vector.tensor_copy(bad_i[:, :], bad_sum[:, :]))
            then(nc.vector.tensor_copy(base_i[:, :], grp_base[:, :]))
            then(nc.vector.scalar_tensor_tensor(grp_cmp[:, :], grp_bad[:, :], -FAR, grp_base[:, :], ALU.mult, ALU.add))
            dve.sem_inc(S["bases"], 1)
            dve.wait_ge(S["cmp_ps"], 1)
            then(nc.vector.tensor_tensor(rel_b[:, 0:TILES].rearrange("p (g t) -> p g t", t=GT),
                                         dst_f[:, 0:TILES].rearrange("p (g t) -> p g t", t=GT),
                                         bank[4][:, 0:GROUPS].unsqueeze(2).to_broadcast([P, GROUPS, GT]), ALU.subtract))
            then(nc.vector.tensor_tensor(cross_row[0:1, 0:TILES - 1], lim_row[0:1, 0, 1:TILES], lim_row[0:1, 1, 0:TILES - 1], ALU.is_lt))
            then(nc.vector.tensor_reduce(cross_sum[:, :], cross_row[0:1, 0:TILES - 1], AX.X, ALU.add))
            then(nc.vector.tensor_tensor(cross_sum[:, :], cross_sum[:, :], bank[4][0:1, GROUPS:GROUPS + 1], ALU.add))
            then(nc.vector.tensor_copy(unsorted_i[:, :], cross_sum[:, :]))
            nc.vector.tensor_tensor(oh_lo[:, 0, 0:EB, :], iota_b[:, :].unsqueeze(1).to_broadcast([P, EB, P]),
                                    last_lo[:, 0:EB].unsqueeze(2).to_broadcast([P, EB, P]), ALU.is_equal).then_inc(S["last_built"], 1)
            nc.vector.tensor_tensor(oh_hi[:, 0, 0:EB, :], iota_b[:, 0:NW].unsqueeze(1).to_broadcast([P, EB, NW]),
                                    last_hi[:, 0:EB].unsqueeze(2).to_broadcast([P, EB, NW]), ALU.is_equal).then_inc(S["last_built"], 1)
            dve.wait_ge(S["starts_ps"], 1)
            then(nc.vector.tensor_copy(last_hist[:, :], bank[5][:, 0:NW]))
            dve.sem_inc(S["starts_ok"], 1)
            dve.wait_ge(S["starts_ps"], 2)
            then(nc.vector.tensor_tensor_scan(first_f[:, :], ones[:, 0:NW], bank[0][:, NW:2 * NW], 0.0, ALU.mult, ALU.add))
            then(nc.vector.tensor_tensor(first_f[:, :], first_f[:, :], bank[0][:, NW:2 * NW], ALU.subtract))
            then(nc.vector.tensor_tensor(first_f[:, :], first_f[:, :], bank[0][:, 0:NW], ALU.add))
            then(nc.vector.tensor_tensor(first_f[:, :], first_f[:, :], last_hist[:, :], ALU.subtract))
            then(nc.vector.tensor_copy(first_i[:, :], first_f[:, :]))
            dve.sem_inc(S["first_ok"], 1)
            dve.wait_ge(S["y_in"], 16)
            dve.wait_ge(S["r_in"], 16)
            then(nc.vector.memset(rel_b[:, TILES:EB * P], -1.0))
            then(nc.vector.tensor_copy(y_f[:, :], y_i[:, :]))
            then(nc.vector.tensor_single_scalar(wy_i[:, :], y_i[:, :], 7, ALU.arith_shift_right))
            then(nc.vector.tensor_scalar(is_y[:, :], node_id[:, :], y_f[:, 0:1], None, ALU.is_equal))
            then(nc.vector.tensor_scalar(not_y[:, :], is_y[:, :], -1.0, 1.0, ALU.mult, ALU.add))
            then(nc.vector.tensor_reduce(mine_y[:, :], is_y[:, :], AX.X, ALU.add))
            then(nc.vector.tensor_scalar(r_y[:, :], r_rows[:, :], mine_y[:, 0:1], None, ALU.mult))
            then(nc.vector.tensor_scalar(invalid[:, :], node_id[:, :], float(N), -3.0e38, ALU.is_ge, ALU.mult))

            def count_first(q, half):
                w = q * ZC + half * U
                dve.wait_ge(S[f"first_in{half}"], q * (16 * U) + 16 * U)
                nc.vector.tensor_tensor(is_less, first_rows[:, half, :, :],
                                        node_id[:, bass.ds(w, U)].unsqueeze(2).to_broadcast([P, U, P]), ALU.is_lt).then_inc(S["less_ok"], 1)
                dve.wait_ge(S["less_ok"], q * 2 + (half + 1))
                nc.vector.tensor_reduce(n_less[:, bass.ds(w, U)], is_less, AX.X, ALU.add).then_inc(S["first_used"], 1)
                dve.wait_ge(S["first_used"], q * 2 + (half + 1))

            for c in range(NZC):
                dve.wait_ge(x_chunk[c], 16 * (KD + (c == NZC - 1)))
                with dve.Fori(0, 2) as h:
                    for i in range(U):
                        w = h * U + (c * ZC + i)
                        nc.vector.bn_stats(bn1[:, bass.ds(w, 1), :].rearrange("p o s -> p (o s)"), nodes[:, :, w, :]).then_inc(S["bn1_ok"], 1)
                count_first(c // 2, c % 2)
            dve.wait_ge(S["bn1_ok"], NW)
            then(nc.vector.tensor_tensor(neg_mean[:, :], bn1[:, :, 1], bn1[:, :, 4], ALU.add))
            then(nc.vector.tensor_scalar(neg_mean[:, :], neg_mean[:, :], -0.5, None, ALU.mult))
            then(nc.vector.tensor_tensor(gap2[:, :], bn1[:, :, 1], bn1[:, :, 4], ALU.subtract))
            then(nc.vector.tensor_tensor(gap2[:, :], gap2[:, :], gap2[:, :], ALU.mult))
            then(nc.vector.tensor_tensor(var2[:, :], bn1[:, :, 2], bn1[:, :, 5], ALU.add))
            then(nc.vector.tensor_scalar(var2[:, :], var2[:, :], 1.0 / D, EPS, ALU.mult, ALU.add))
            then(nc.vector.scalar_tensor_tensor(var2[:, :], gap2[:, :], 0.25, var2[:, :], ALU.mult, ALU.add))
            dve.sem_inc(S["ssum"], 1)
            for b in range(NZC, 2 * NZC):
                count_first(b // 2, b % 2)
                if b > NZC:
                    dve.wait_ge(S["shift_ok"], 1)
                    wins = slice(ACT_WIN + (b - NZC - 1) * U, ACT_WIN + (b - NZC) * U)
                    for scale, op in ((rstd, ALU.mult), (shift, ALU.add)):
                        for k in range(KD):
                            ins = nc.vector.tensor_tensor(nodes[:, k, wins, :], nodes[:, k, wins, :],
                                                          scale[:, wins].unsqueeze(2).to_broadcast([P, U, P]), op)
                            if k == 0:
                                ins.then_inc(S["dve_ch"], 1)
                                ch[0] += 1
                        then(ins)
            then(nc.vector.scalar_tensor_tensor(row_start[:, 0:NW], first_f[:, :], float(P), n_less[:, :], ALU.mult, ALU.add))
            then(nc.vector.memset(row_start[:, NW:NW + 1], float(E)))
            dve.sem_inc(S["starts_ok"], 1)
            dve.wait_ge(S["starts_ps"], 3)
            then(nc.vector.tensor_tensor(deg[:, :], bank[1][:, 0:NW], row_start[:, 0:NW], ALU.subtract))

            def one_hots(s, j):
                t0 = s * 16
                nc.vector.tensor_tensor(oh_lo[:, j, :, :], iota_b[:, :].unsqueeze(1).to_broadcast([P, 16, P]),
                                        lo_b[:, bass.ds(t0, 16)].unsqueeze(2).to_broadcast([P, 16, P]),
                                        ALU.is_equal).then_inc(S["hist_built"], 1)
                nc.vector.tensor_tensor(oh_hi[:, j, :, :], iota_b[:, 0:NW].unsqueeze(1).to_broadcast([P, 16, NW]),
                                        hi_b[:, bass.ds(t0, 16)].unsqueeze(2).to_broadcast([P, 16, NW]),
                                        ALU.is_equal).then_inc(S["hist_built"], 1)
            n_unsorted = dve.value_load(unsorted_i[0:1, 0:1], min_val=0, max_val=E)
            with dve.If(n_unsorted > 0):
                nc.vector.tensor_copy(dst_i[:, :], dst_f[:, :]).then_inc(S["hist_start"], 1)
                dve.wait_ge(S["hist_start"], 1)
                nc.vector.tensor_single_scalar(low_i[:, :], dst_i[:, :], 127, ALU.bitwise_and).then_inc(S["hist_start"], 1)
                dve.wait_ge(S["hist_start"], 2)
                nc.vector.tensor_copy(lo_b[:, :], low_i[:, :]).then_inc(S["hist_start"], 1)
                dve.wait_ge(S["hist_start"], 3)
                nc.vector.tensor_single_scalar(low_i[:, :], dst_i[:, :], 7, ALU.arith_shift_right).then_inc(S["hist_start"], 1)
                dve.wait_ge(S["hist_start"], 4)
                nc.vector.tensor_copy(hi_b[:, :], low_i[:, :]).then_inc(S["hist_start"], 1)
                dve.wait_ge(S["hist_start"], 5)
                one_hots(0, 0)
                one_hots(1, 1)
                with dve.Fori(1, HSTEPS // 2) as q:
                    for j in range(2):
                        dve.wait_ge(S["hist_used"], q * 2 + (j - 1))
                        one_hots(q * 2 + j, j)
                dve.wait_ge(S["hist_ps"], 1)
                nc.vector.tensor_copy(deg[:, :], bank[5][:, 0:NW]).then_inc(S["hist_start"], 1)
                dve.wait_ge(S["hist_start"], 6)
            then(nc.vector.tensor_tensor(deg[:, :], deg[:, :], not_y[:, :], ALU.mult))
            then(nc.vector.scalar_tensor_tensor(deg[:, :], is_y[:, :], float(TOPK), deg[:, :], ALU.mult, ALU.add))
            nc.vector.tensor_scalar(deg[:, :], deg[:, :], SELF_W, None, ALU.add).then_inc(S["deg_ok"], 1)
            wy = dve.value_load(wy_i[0:1, 0:1], min_val=0, max_val=NW - 1)
            dve.wait_ge(S["mem_ok"], 1)
            for k in range(KD):
                nc.vector.tensor_tensor(nodes[:, k, bass.ds(wy, 1), :], nodes[:, k, bass.ds(wy, 1), :],
                                        r_y[:, k * P:(k + 1) * P].unsqueeze(1), ALU.add).then_inc(S["mem_patched"], 1)
            dve.wait_ge(S["mem_patched"], KD)
            def differ(b):
                if b >= 2:
                    dve.wait_ge(S["dist_ok"], b - 1)
                for k in range(KD):
                    nc.vector.tensor_tensor(diff[:, b % 2, :, k, :], nodes[:, k, b * U:(b + 1) * U, :],
                                            r_rows[:, k * P:(k + 1) * P].unsqueeze(1).to_broadcast([P, U, P]),
                                            ALU.subtract).then_inc(S["diff_ok"], 1)
                if b >= 1:
                    sum_squares(b - 1)

            def sum_squares(b):
                dve.wait_ge(S["square_ok"], b + 1)
                nc.vector.tensor_reduce(dist[:, b * U:(b + 1) * U], diff[:, b % 2, :, :, :], AX.XY, ALU.add).then_inc(S["dist_ok"], 1)

            AHEAD = 3
            for b in range(2 * AHEAD):
                differ(b)
            dve.wait_ge(S["deg_ok"], 2)
            for c in range(NZC):
                dve.wait_ge(S["diff_ok"], 2 * KD * (c + 1))
                for k in range(KD):
                    rows = nodes[:, k, c * ZC:(c + 1) * ZC, :]
                    ins = nc.vector.tensor_tensor(rows, rows, dinv[:, c * ZC:(c + 1) * ZC].unsqueeze(2).to_broadcast([P, ZC, P]),
                                                  ALU.mult)
                ins.then_inc(S["z_ok"], 1)
                if c + AHEAD < NZC:
                    differ(2 * (c + AHEAD))
                    differ(2 * (c + AHEAD) + 1)
            sum_squares(2 * NZC - 1)

            for c in range(NZC):
                dve.wait_ge(table_out[c], 16 * KD)
                with dve.Fori(0, 2) as h:
                    for j in range(U):
                        dve.wait_ge(S["zT_ps"], h * U + (c * ZC + j + 1))
                        nc.vector.tensor_scalar(nodes[:, :, h * U + (c * ZC + j), :], bank[j][:, 0:D].rearrange("p (k c) -> p k c", k=KD),
                                                SELF_W, None, ALU.mult).then_inc(S["agg_init"], 1)
            dve.wait_ge(S["agg_init"], NW)
            ycol = dve.value_load(y_i[0:1, 0:1], min_val=0, max_val=N - 1)
            then(nc.vector.tensor_copy(col_fix[:, :], agg[:, :, bass.ds(ycol, 1)].rearrange("p k o -> p (k o)")))
            dve.wait_ge(S["dist_ok"], 2 * NZC)
            then(nc.vector.scalar_tensor_tensor(near[:, :], dist[:, :], -1.0, not_y[:, :], ALU.mult, ALU.mult))
            then(nc.vector.tensor_tensor(near[:, :], near[:, :], invalid[:, :], ALU.add))
            then(nc.vector.max(near8[:, :], near[:, :]))
            dve.sem_inc(S["near_ok"], 1)
            dve.wait_ge(S["near_ps"], 1)
            nc.vector.tensor_copy(near_row[0:1, 0:4 * P], bank[0][0:1, :])
            then(nc.vector.tensor_copy(near_row[0:1, 4 * P:8 * P], bank[1][0:1, :]))
            dve.drain()
            then(nc.vector.max(top8[:, :], near_row[:, :]))
            dve.sem_inc(S["near_ok"], 1)
            dve.wait_ge(S["near_ps"], 2)
            then(nc.vector.tensor_copy(thr[:, :], bank[2][:, 0:1]))
            then(nc.vector.tensor_scalar(above[:, :], near[:, :], thr[:, 0:1], None, ALU.is_gt))
            then(nc.vector.tensor_scalar(tied[:, :], near[:, :], thr[:, 0:1], None, ALU.is_equal))
            then(nc.vector.tensor_reduce(n_above[:, :], above[:, :], AX.X, ALU.add))
            dve.sem_inc(S["near_ok"], 1)
            dve.wait_ge(S["near_ps"], 3)
            then(nc.vector.tensor_scalar(room[:, :], bank[2][:, 1:2], -1.0, float(TOPK), ALU.mult, ALU.add))
            then(nc.vector.tensor_tensor_scan(tie_scan[:, :], ones[:, 0:NW], bank[3][:, NW:2 * NW], 0.0, ALU.mult, ALU.add))
            then(nc.vector.tensor_tensor(tie_rank[:, :], tie_scan[:, :], bank[3][:, NW:2 * NW], ALU.subtract))
            then(nc.vector.tensor_tensor(tie_rank[:, :], tie_rank[:, :], bank[3][:, 0:NW], ALU.add))
            then(nc.vector.tensor_scalar(tie_rank[:, :], tie_rank[:, :], room[:, 0:1], None, ALU.is_le))
            then(nc.vector.tensor_tensor(chosen[:, :], tied[:, :], tie_rank[:, :], ALU.mult))
            then(nc.vector.tensor_tensor(chosen[:, :], chosen[:, :], above[:, :], ALU.add))
            dve.sem_inc(S["chosen_ok"], 1)

            def select(g, j):
                nc.vector.tensor_tensor(sel[:, j, :, :], iota_b[:, :].unsqueeze(1).to_broadcast([P, GT, P]),
                                        rel_b[:, bass.ds(g * GT, GT)].unsqueeze(2).to_broadcast([P, GT, P]),
                                        ALU.is_equal).then_inc(S["sel_ok"], 1)

            def add_group(g, j, first):
                base = dve.value_load(base_i[0:1, bass.ds(g, 1)], min_val=0, max_val=(NW - 1) * P)
                if not first:
                    dve.wait_ge(S["agg_added"], g)
                dve.wait_ge(S["agg_ps"], g + 1)
                where = agg[:, :, bass.ds(base, P)]
                nc.vector.tensor_tensor(where, where, bank[j][:, 0:D].rearrange("p (k c) -> p k c", k=KD),
                                        ALU.add).then_inc(S["agg_added"], 1)

            select(0, 0)
            select(1, 1)
            add_group(0, 0, True)
            with dve.Fori(0, (GROUPS - 2) // 2) as q:
                for j in range(2):
                    dve.wait_ge(S["agg_ps"], q * 2 + j + 1)
                    select(q * 2 + (j + 2), j)
                    add_group(q * 2 + (j + 1), (j + 1) % 2, False)
            add_group(GROUPS - 1, 1, False)
            dve.wait_ge(S["agg_added"], GROUPS)
            n_bad = dve.value_load(bad_i[0:1, 0:1], min_val=0, max_val=GROUPS)
            with dve.If(n_bad > 0):
                dve.sem_inc(S["rep_bad"], 1)
                dve.wait_ge(S["rep_dst"], 1)
                nc.vector.tensor_scalar(grp_far, bank[4][:, 0:GROUPS], -FAR, FAR, ALU.mult, ALU.add).then_inc(S["rep_bad"], 1)
                dve.wait_ge(S["rep_bad"], 2)
                by_group = dst_f[:, 0:TILES].rearrange("p (g t) -> p g t", t=GT)
                nc.vector.tensor_tensor(by_group, by_group, grp_far.unsqueeze(2).to_broadcast([P, GROUPS, GT]),
                                        ALU.add).then_inc(S["rep_bad"], 1)
                dve.wait_ge(S["rep_bad"], 3)
                with dve.Fori(0, GROUPS) as g:
                    with dve.Fori(0, NW) as w:
                        nc.vector.tensor_scalar(rep_rel[:, :], dst_f[:, bass.ds(g * GT, GT)], win_f[:, bass.ds(w, 1)], None,
                                                ALU.subtract).then_inc(S["rep_relok"], 1)
                        dve.wait_ge(S["rep_relok"], g * NW + (w + 1))
                        nc.vector.tensor_tensor(sel[:, 0, :, :], iota_b[:, :].unsqueeze(1).to_broadcast([P, GT, P]),
                                                rep_rel[:, :].unsqueeze(2).to_broadcast([P, GT, P]),
                                                ALU.is_equal).then_inc(S["rep_sel"], 1)
                        where = agg[:, :, bass.ds(w * P, P)]
                        dve.wait_ge(S["rep_ps"], g * NW + (w + 1))
                        nc.vector.tensor_tensor(where, where, bank[0][:, 0:D].rearrange("p (k c) -> p k c", k=KD),
                                                ALU.add).then_inc(S["rep_added"], 1)
                        dve.wait_ge(S["rep_added"], g * NW + (w + 1))
            dve.wait_ge(S["selps"], 1)
            then(nc.vector.tensor_tensor(agg[:, :, bass.ds(ycol, 1)].rearrange("p k o -> p (k o)"), col_fix[:, :],
                                         bank[3][:, 0:KD], ALU.add))
            dve.sem_inc(S["fixed"], 1)


            dve.wait_ge(S["b1_ps"], 1)
            nc.vector.tensor_copy(b1_cols, bank[4][:, 0:NE * FT]).then_inc(S["b1_ok"], 1)
            dve.wait_ge(S["aggst_ok"], 1)
            def residual(q, j):
                w = q * U + j
                dve.wait_ge(S["conv_ps"], w + 1)
                dve.wait_ge(S[f"xt_in{j}"], q * 16 + 16)
                nc.vector.scalar_tensor_tensor(nodes[:, :, w, :], bank[j][:, 0:D].rearrange("p (k c) -> p k c", k=KD),
                                               dinv[:, bass.ds(w, 1)], x_tile[:, j, :].rearrange("p (k c) -> p k c", k=KD),
                                               ALU.mult, ALU.add).then_inc(S["x1_ok"], 1)

            def stats(q, j):
                dve.wait_ge(S["x1_ok"], q * U + j + 1)
                dve.sem_inc(S["tick"], 1)
                nc.vector.bn_stats(bn[:, bass.ds(q * U + j, 1), :].rearrange("p o s -> p (o s)"),
                                   nodes[:, :, q * U + j, :]).then_inc(S["bn_ok"], 1)
            with dve.Fori(0, NU) as q:
                for j in range(U + 1):
                    if j < U:
                        residual(q, j)
                    if j:
                        stats(q, j - 1)
            dve.wait_ge(S["bn_ok"], NW)
            then(nc.vector.tensor_tensor(mean2[:, :], bn[:, :, 1], bn[:, :, 4], ALU.add))
            then(nc.vector.tensor_tensor(gap2[:, :], bn[:, :, 1], bn[:, :, 4], ALU.subtract))
            then(nc.vector.tensor_tensor(gap2[:, :], gap2[:, :], gap2[:, :], ALU.mult))
            then(nc.vector.tensor_tensor(var2[:, :], bn[:, :, 2], bn[:, :, 5], ALU.add))
            then(nc.vector.tensor_scalar(var2[:, :], var2[:, :], 1.0 / D, EPS, ALU.mult, ALU.add))
            nc.vector.scalar_tensor_tensor(var2[:, :], gap2[:, :], 0.25, var2[:, :], ALU.mult, ALU.add).then_inc(S["var_ok"], 1)
            dve.wait_ge(S["var_ok"], 2)
            then(nc.vector.scalar_tensor_tensor(shift2[:, :], mean2[:, :], -0.5, rstd2[:, :], ALU.mult, ALU.mult))
            dve.sem_inc(S["lnb_ok"], 1)
            def feat(w, j, first):
                dve.wait_ge(S["hT_ps"], w + 1)
                if not first:
                    dve.wait_ge(S["logit_ps"], w - U + 1)
                nc.vector.tensor_copy(h_feat[:, j, :, :], bank[turn_bank(j)][:, 0:D].rearrange("p (k c) -> p k c", k=KD)).then_inc(S["hT_ok"], 1)
            def take_logits(step, half):
                dve.wait_ge(S["logit_ps"], step * U + U)
                nc.vector.tensor_copy(gate_l[:, bass.ds(step * U, U), :],
                                      bank[6 + half][:, 0:U * NE].rearrange("p (w e) -> p w e", e=NE)).then_inc(S["gate_taken"], 1)
            def norm_ahead(q, i):
                if i % ZC in DVE_NORM:
                    w = q * ZC + i
                    nc.vector.tensor_scalar(h_tile[:, i % U, :, :], nodes[:, :, w, :], rstd2[:, bass.ds(w, 1)],
                                            shift2[:, bass.ds(w, 1)], ALU.mult, ALU.add).then_inc(S["h_dve"], 1)

            def gate_windows(q, first, last):
                for half in range(2):
                    for j in range(U):
                        feat(q * ZC + (half * U + j), j, first and half == 0)
                        if not (last and half == 1):
                            norm_ahead(q, half * U + j + U)
                    if not (first and half == 0):
                        take_logits(q * 2 + (half - 1), 1 - half)
            for i in range(U):
                norm_ahead(0, i)
            gate_windows(0, True, False)
            with dve.Fori(1, NZC - 1) as q:
                gate_windows(q, False, False)
            gate_windows(NZC - 1, False, True)
            take_logits(NU - 1, 1)
            dve.wait_ge(S["gate_taken"], NU)

            def over(ap):
                return ap.unsqueeze(2).to_broadcast([P, NW, NE])
            def per_expert(ap):
                return ap.unsqueeze(1).to_broadcast([P, NW, NE])
            then(nc.vector.tensor_tensor(gate_l, gate_l, per_expert(gateb_sb[:, :]), ALU.add))
            then(nc.vector.tensor_reduce(best[:, :], gate_l, AX.X, ALU.max))
            then(nc.vector.tensor_tensor(gate_l, gate_l, over(best[:, :]), ALU.subtract))
            dve.sem_inc(S["gate_in"], 1)
            then(nc.vector.tensor_copy(iota_f[:, :], iota_i[:, 0:NE]))
            then(nc.vector.tensor_scalar(rank_e[:, :], iota_f[:, :], -1.0, float(NE), ALU.mult, ALU.add))
            dve.wait_ge(S["gate_out"], 1)
            then(nc.vector.tensor_reduce(norm[:, :], gate_e, AX.X, ALU.add))
            then(nc.vector.reciprocal(norm[:, :], norm[:, :]))
            then(nc.vector.tensor_tensor(gate_e, gate_e, over(norm[:, :]), ALU.mult))
            then(nc.vector.tensor_reduce(best[:, :], gate_e, AX.X, ALU.max))
            then(nc.vector.tensor_tensor(gate_t, gate_e, over(best[:, :]), ALU.is_equal))
            then(nc.vector.tensor_tensor(gate_t, gate_t, per_expert(rank_e[:, :]), ALU.mult))
            then(nc.vector.tensor_reduce(expert[:, :], gate_t, AX.X, ALU.max))
            then(nc.vector.tensor_tensor(pick, gate_t, over(expert[:, :]), ALU.is_equal))
            then(nc.vector.tensor_scalar(kept[:, :], invalid[:, :], 0.0, None, ALU.is_ge))
            then(nc.vector.tensor_tensor(pick, pick, over(kept[:, :]), ALU.mult))
            dve.sem_inc(S["pick_ok"], 1)
            dve.wait_ge(S["rank_ps"], 1)
            HW = NW // 2
            for i in range(2):
                rows = slice(i * HW, (i + 1) * HW)
                then(nc.vector.tensor_copy(gate_t[:, rows, :], bank[2 + i][:, 0:HW * NE].rearrange("p (w e) -> p w e", e=NE)))
            for e in range(NE):
                then(nc.vector.tensor_tensor_scan(gate_l[:, :, e], ones[:, 0:NW], gate_t[:, :, e], 0.0, ALU.mult, ALU.add))
            then(nc.vector.tensor_copy(taken_f[0:1, :], gate_l[0:1, NW - 1, :]))
            then(nc.vector.memset(taken_i[:, :], 0))
            then(nc.vector.tensor_copy(taken_i[0:1, 0:NE], taken_f[0:1, :]))
            then(nc.vector.tensor_tensor(gate_l, gate_l, gate_t, ALU.subtract))
            for i in range(2):
                rows = slice(i * HW, (i + 1) * HW)
                then(nc.vector.tensor_tensor(gate_l[:, rows, :], gate_l[:, rows, :],
                                             bank[i][:, 0:HW * NE].rearrange("p (w e) -> p w e", e=NE), ALU.add))
            then(nc.vector.tensor_tensor(gate_l, gate_l, pick, ALU.mult))
            then(nc.vector.tensor_reduce(place[:, :], gate_l, AX.X, ALU.add))
            then(nc.vector.tensor_scalar(expert[:, :], expert[:, :], -1.0, float(NE), ALU.mult, ALU.add))
            then(nc.vector.tensor_scalar(norm[:, :], place[:, :], float(CAP), None, ALU.is_le))
            then(nc.vector.tensor_tensor(kept[:, :], kept[:, :], norm[:, :], ALU.mult))
            then(nc.vector.tensor_tensor(weight[:, :], best[:, :], kept[:, :], ALU.mult))
            then(nc.vector.tensor_scalar(place[:, :], place[:, :], float(CAP), -1.0, ALU.min, ALU.add))
            then(nc.vector.scalar_tensor_tensor(slot_f[:, :], expert[:, :], float(CAP), place[:, :], ALU.mult, ALU.add))
            then(nc.vector.tensor_scalar(norm[:, :], node_id[:, :], float(N), FAR, ALU.is_ge, ALU.mult))
            then(nc.vector.tensor_tensor(slot_f[:, :], slot_f[:, :], norm[:, :], ALU.add))
            then(nc.vector.tensor_copy(get_idx[:, :], slot_f[:, :]))
            then(nc.vector.tensor_scalar(kept[:, :], kept[:, :], -FAR, FAR, ALU.mult, ALU.add))
            then(nc.vector.tensor_tensor(slot_f[:, :], slot_f[:, :], kept[:, :], ALU.add))
            then(nc.vector.tensor_copy(put_idx[:, :], slot_f[:, :]))
            dve.sem_inc(S["routed"], 1)

            def feats(q, s, took):
                n = CHUNKS[s % NCH][1]
                with dve.If(took > CHUNKS[s % NCH][0]):
                    dve.wait_ge(S["xT_ps"], q * PC + (s + 2))
                    dve.wait_ge(S["l1_ps"], q * (PC * FB2) + (s + 1) * FB2)
                    nc.vector.tensor_copy(xs_feat[:, s % 2, :, 0:n],
                                          bank[s % 2].rearrange("p (k c) -> p k c", k=KD)[:, :, 0:n]).then_inc(S["xT_ok"], 1)
                with dve.Else():
                    dve.wait_ge(S["xT_ok"], q * PC + (s + 2))
                    dve.sem_inc(S["xT_ok"], 1)

            def results(q, s, took):
                j, c = s // NCH, s % NCH
                with dve.If(took > CHUNKS[c][0]):
                    for t in range(2):
                        n, slot = min(P, CHUNKS[c][1] - t * P), s % 2 * 2 + t
                        dve.wait_ge(S[f"ys_out{slot}"], q * (16 * NCH) + (16 * (s // 2) + 16))
                        dve.wait_ge(S["l2_ps"], q * (2 * PC) + (2 * s + t + 3))
                        nc.vector.tensor_tensor(y_tile[0:n, slot, :], bank[4 + t][0:n, 0:D],
                                                b2_rows[0:n, bass.ds(q * 2 + j, 1), :].rearrange("p o d -> p (o d)"),
                                                ALU.add).then_inc(S["y_ok"], 1)
                with dve.Else():
                    dve.wait_ge(S["y_ok"], q * (2 * PC) + (2 * s + 2))
                    dve.sem_inc(S["y_ok"], 2)

            dve.sem_inc(S["xT_ok"], 2)
            dve.sem_inc(S["y_ok"], 2)
            feats(0, 0, dve.value_load(taken_i[0:1, 0:1], min_val=0, max_val=N))
            with dve.Fori(0, NE // 2) as q:
                took = [dve.value_load(taken_i[0:1, bass.ds(q * 2 + i, 1)], min_val=0, max_val=N) for i in range(3)]
                for s in range(PC):
                    feats(q, s + 1, took[(s + 1) // NCH])
                    results(q, s, took[s // NCH])

            def finish(q, s, first):
                w, j = q * ZC + s, s % U
                half_of = s // U
                if s % U == 0:
                    dve.wait_ge(S[f"got{half_of}"], q * (16 * U) + 16 * U)
                    dve.sem_inc(S["tick"], 1)
                if not (first and s < U):
                    dve.wait_ge(S[f"out_done{j}"], q * 32 + 16 * half_of)
                nc.vector.scalar_tensor_tensor(o_tile[:, j, :].rearrange("p (k c) -> p k c", k=KD),
                                               y_got[:, s, :].rearrange("p (k c) -> p k c", k=KD), weight[:, bass.ds(w, 1)],
                                               nodes[:, :, w, :], ALU.mult, ALU.add,
                                               accum_out=row_sum[:, bass.ds(w, 1)]).then_inc(S["o_ok"], 1)
            for s in range(ZC):
                finish(0, s, True)
            with dve.Fori(1, NZC) as q:
                for s in range(ZC):
                    finish(q, s, False)
            dve.wait_ge(S["o_ok"], NW)
            then(nc.vector.tensor_scalar(odd, row_sum, 0.0, 0.0, ALU.mult, ALU.is_equal))
            then(nc.vector.tensor_scalar(odd, odd, -1.0, 1.0, ALU.mult, ALU.add))
            then(nc.vector.tensor_reduce(odd_n, odd, AX.X, ALU.add))
            dve.sem_inc(S["odd_rows"], 1)
            dve.wait_ge(S["odd_ps"], 1)
            then(nc.vector.tensor_copy(odd_i, bank[0][:, 0:1]))
            dve.sem_inc(S["odd_ok"], 1)
            BIG = 3.4028234e38
            n_odd = dve.value_load(odd_i[0:1, 0:1], min_val=0, max_val=P * NW)
            with dve.If(n_odd > 0):
                dve.sem_inc(S["clean_free"], 1)
                dve.sem_inc(S["clean_out"], 16)
                dve.wait_ge(S["out_done0"], 16 * NU)
                with dve.Fori(0, NW) as w:
                    dve.wait_ge(S["clean_got"], w * 16 + 16)
                    dve.sem_inc(S["tick"], 1)
                    nc.vector.tensor_scalar(y_gated, y_got[:, 0, :], weight[:, bass.ds(w, 1)], None, ALU.mult).then_inc(S["clean"], 1)
                    dve.wait_ge(S["clean"], w * 6 + 1)
                    dve.sem_inc(S["clean_free"], 1)
                    nc.vector.tensor_scalar(y_low, y_gated, -BIG, -1.0e4, ALU.is_lt, ALU.mult).then_inc(S["clean"], 1)
                    nc.vector.tensor_scalar(y_clip, y_gated, BIG, 1.0e4, ALU.is_gt, ALU.mult).then_inc(S["clean"], 1)
                    nc.vector.tensor_scalar(y_fin, y_gated, 0.0, 0.0, ALU.mult, ALU.is_equal).then_inc(S["clean"], 1)
                    dve.wait_ge(S["clean"], w * 6 + 4)
                    nc.vector.tensor_tensor(y_clip, y_clip, y_low, ALU.add).then_inc(S["clean"], 1)
                    dve.wait_ge(S["clean"], w * 6 + 5)
                    dve.sem_inc(S["tick"], 1)
                    nc.vector.copy_predicated(y_clip, y_fin, y_gated).then_inc(S["clean"], 1)
                    dve.wait_ge(S["clean"], w * 6 + 6)
                    dve.wait_ge(S["clean_out"], w * 16 + 16)
                    nc.vector.tensor_tensor(o_tile[:, 0, :].rearrange("p (k c) -> p k c", k=KD), nodes[:, :, w, :],
                                            y_clip.rearrange("p (k c) -> p k c", k=KD), ALU.add).then_inc(S["clean_ok"], 1)
                    dve.wait_ge(S["clean_ok"], w + 1)

        @block.tensor
        def _(pe):
            pe.wait_ge(S["consts"], 7)
            for n, (i, b0, nb) in enumerate(EDGE_TURNS):
                pe.wait_ge(S["edges_float"], i + 1)
                if n >= 2:
                    pe.wait_ge(S["edges_out"], n - 1)
                for b in range(nb):
                    last = nc.tensor.transpose(bank[n % 2][:, b * P:(b + 1) * P], stage_f[:, i, b0 + b, :], ident[:, :])
                last.then_inc(S["edge_psum"], 1)
            pe.wait_ge(S["lims"], 1)
            for n, (i, b0, nb) in enumerate(LIM_TURNS):
                if n >= 2:
                    pe.wait_ge(S["lim_rows"], n - 1)
                for b in range(nb):
                    last = nc.tensor.matmul(bank[2 + n % 2][0:1, b * P:(b + 1) * P], tile_lim[:, i, b0 + b:b0 + b + 1],
                                            ident[:, :], start=True, stop=True)
                last.then_inc(S["limps"], 1)
            pe.wait_ge(S["bases"], 1)
            nc.tensor.matmul(bank[4][:, 0:GROUPS], ones[0:1, :], grp_cmp[0:1, :], start=True, stop=True)
            nc.tensor.matmul(bank[4][0:1, GROUPS:GROUPS + 1], disorder[:, :], ones[:, 0:1], start=True, stop=True).then_inc(S["cmp_ps"], 1)

            pe.wait_ge(S["last_built"], 2)
            for b in range(EB):
                last = nc.tensor.matmul(bank[5][:, 0:NW], oh_lo[:, 0, b, :], oh_hi[:, 0, b, :], start=(b == 0), stop=(b == EB - 1))
            last.then_inc(S["starts_ps"], 1)
            pe.wait_ge(S["starts_ok"], 1)
            nc.tensor.matmul(bank[0][:, 0:NW], tri[:, :], last_hist[:, :], start=True, stop=True)
            nc.tensor.matmul(bank[0][:, NW:2 * NW], ones[:, :], last_hist[:, :], start=True, stop=True).then_inc(S["starts_ps"], 1)
            pe.wait_ge(S["starts_ok"], 2)
            nc.tensor.matmul(bank[1][:, 0:NW], down_one[:, :], row_start[:, 0:NW], start=True, stop=False)
            nc.tensor.matmul(bank[1][:, 0:NW], corner[:, :], row_start[:, 1:NW + 1], start=False, stop=True).then_inc(S["starts_ps"], 1)

            n_unsorted = pe.value_load(unsorted_i[0:1, 0:1], min_val=0, max_val=E)
            with pe.If(n_unsorted > 0):
                nc.tensor.matmul(bank[5][:, 0:NW], zeros[:, 0:P], zeros[:, 0:NW], start=True, stop=False)
                with pe.Fori(0, HSTEPS // 2) as q:
                    for j in range(2):
                        pe.wait_ge(S["hist_built"], q * 4 + 2 * (j + 1))
                        for t in range(16):
                            last = nc.tensor.matmul(bank[5][:, 0:NW], oh_lo[:, j, t, :], oh_hi[:, j, t, :], start=False, stop=False)
                        last.then_inc(S["hist_used"], 1)
                nc.tensor.matmul(bank[5][:, 0:NW], zeros[:, 0:P], zeros[:, 0:NW], start=False, stop=True).then_inc(S["hist_ps"], 1)

            def start_window(w, j):
                for k in range(KD):
                    last = nc.tensor.transpose(bank[j][:, k * P:(k + 1) * P], z_stat[:, j, k, :], ident[:, :])
                last.then_inc(S["zT_ps"], 1)
            for j in range(U):
                pe.wait_ge(S["zstat_ok"], j + 1)
                start_window(j, j)
            with pe.Fori(1, NU) as q:
                for j in range(U):
                    pe.wait_ge(S["zstat_ok"], q * U + j + 1)
                    pe.wait_ge(S["agg_init"], q * U + (j - U + 1))
                    start_window(q * U + j, j)

            pe.wait_ge(S["near_ok"], 1)
            for i in range(8):
                last = nc.tensor.matmul(bank[i // 4][0:1, (i % 4) * P:(i % 4 + 1) * P], near8[:, i:i + 1], ident[:, :],
                                        start=True, stop=True)
            last.then_inc(S["near_ps"], 1)
            pe.wait_ge(S["near_ok"], 2)
            nc.tensor.matmul(bank[2][:, 0:1], ones[0:1, :], top8[0:1, TOPK - 1:TOPK], start=True, stop=True).then_inc(S["near_ps"], 1)
            pe.wait_ge(S["near_ok"], 3)
            nc.tensor.matmul(bank[2][:, 1:2], ones[:, :], n_above[:, :], start=True, stop=True)
            nc.tensor.matmul(bank[3][:, 0:NW], tri[:, :], tied[:, :], start=True, stop=True)
            nc.tensor.matmul(bank[3][:, NW:2 * NW], ones[:, :], tied[:, :], start=True, stop=True).then_inc(S["near_ps"], 1)

            pe.wait_ge(S["chosen_ok"], 1)
            nc.tensor.matmul(bank[3][:, 0:KD], zeros[:, 0:P], zeros[:, 0:KD], start=True, stop=False)

            def chosen_rows(q):
                for j in range(2):
                    pe.wait_ge(S[f"zb_in{j}"], q * 16 + 16)
                    for k in range(KD):
                        last = nc.tensor.matmul(bank[3][:, k:k + 1], z_back[:, j, k * P:(k + 1) * P], chosen[:, bass.ds(q * 2 + j, 1)],
                                                start=False, stop=False)
                    last.then_inc(S["zb_used"], 1)

            def group(g, q, slot, first):
                j = slot % 2
                pe.wait_ge(S["sel_ok"], g + 1)
                pe.wait_ge(gathered[slot], q * 64 + 64)
                if not first:
                    pe.wait_ge(S["agg_added"], g - 1)
                for k in range(KD):
                    for t in range(GT):
                        last = nc.tensor.matmul(bank[j][:, k * P:(k + 1) * P], gath[:, slot, t, k * P:(k + 1) * P],
                                                sel[:, j, t, :], start=(t == 0), stop=(t == GT - 1))
                last.then_inc(S["agg_ps"], 1)
            for slot in range(GS):
                group(slot, 0, slot, slot < 2)
            chosen_rows(0)
            with pe.Fori(1, GROUPS // GS) as q:
                for slot in range(GS):
                    group(q * GS + slot, q, slot, False)
                chosen_rows(q)
            nc.tensor.matmul(bank[3][:, 0:KD], zeros[:, 0:P], zeros[:, 0:KD], start=False, stop=True).then_inc(S["selps"], 1)

            n_bad = pe.value_load(bad_i[0:1, 0:1], min_val=0, max_val=GROUPS)
            with pe.If(n_bad > 0):
                pe.wait_ge(S["rep_bad"], 1)
                nc.tensor.matmul(bank[4][:, 0:GROUPS], ones[0:1, :], grp_bad[0:1, :], start=True, stop=True).then_inc(S["rep_dst"], 1)
                pe.sem_inc(S["rep_free"], 1)
                with pe.Fori(0, GROUPS) as g:
                    pe.wait_ge(S["rep_got"], g * (16 * GT) + 16 * GT)
                    pe.sem_inc(S["tick"], 1)
                    with pe.Fori(0, NW) as w:
                        pe.wait_ge(S["rep_sel"], g * NW + (w + 1))
                        for k in range(KD):
                            for t in range(GT):
                                last = nc.tensor.matmul(bank[0][:, k * P:(k + 1) * P], gath[:, 0, t, k * P:(k + 1) * P],
                                                        sel[:, 0, t, :], start=(t == 0), stop=(t == GT - 1))
                        last.then_inc(S["rep_ps"], 1)
                    pe.wait_ge(S["rep_ps"], g * NW + NW)
                    pe.sem_inc(S["rep_free"], 1)

            pe.wait_ge(S["w_small"], 5 * 16)
            nc.tensor.transpose(bank[4][:, 0:NE * FT], b1_rows[0:NE * FT, :], ident[0:NE * FT, 0:NE * FT]).then_inc(S["b1_ps"], 1)
            pe.wait_ge(S["b1_ok"], 1)
            def convolve(w, j, first):
                pe.wait_ge(S["aggst_ok"], w + 1)
                if not first:
                    pe.wait_ge(S["x1_ok"], w - U + 1)
                for k in range(KD):
                    last = nc.tensor.matmul(bank[j][:, 0:D], agg_stat[:, j, k, :], gnnw_sb[:, k, :], start=(k == 0), stop=(k == KD - 1))
                last.then_inc(S["conv_ps"], 1)
            for j in range(U):
                convolve(j, j, True)
            with pe.Fori(1, NU) as q:
                for j in range(U):
                    convolve(q * U + j, j, False)

            def turn_rows(q, i, first):
                w, j = q * ZC + i, i % U
                by, mine = ("h_dve", DVE_NORM) if i % ZC in DVE_NORM else ("h_ok", ACT_NORM)
                pe.wait_ge(S[by], q * len(mine) + (i // ZC * len(mine) + mine.index(i % ZC) + 1))
                if turn_bank(j) == 2:
                    if not (first and j == 2):
                        pe.wait_ge(S["hT_ok"], w - (3 if j == 6 else 2))
                elif not first:
                    pe.wait_ge(S["hT_ok"], w - U + 1)
                for k in range(KD):
                    last = nc.tensor.transpose(bank[turn_bank(j)][:, k * P:(k + 1) * P], h_tile[:, j, k, :], ident[:, :])
                last.then_inc(S["hT_ps"], 1)

            def logits(q, half, j, first):
                pe.wait_ge(S["hT_ok"], q * ZC + (half * U + j + 1))
                if j == 0 and not first:
                    pe.wait_ge(S["gate_taken"], q * 2 + (half - 1))
                for k in range(KD):
                    last = nc.tensor.matmul(bank[6 + half][:, j * NE:(j + 1) * NE], h_feat[:, j, k, :], gatew_sb[:, k, :],
                                            start=(k == 0), stop=(k == KD - 1))
                last.then_inc(S["logit_ps"], 1)

            def gate_step(q, half, first, last):
                for j in range(U):
                    logits(q, half, j, first)
                    if not last:
                        turn_rows(q, half * U + U + j, False)
            for j in range(U):
                turn_rows(0, j, True)
            gate_step(0, 0, True, False)
            gate_step(0, 1, True, False)
            with pe.Fori(1, NZC - 1) as q:
                gate_step(q, 0, False, False)
                gate_step(q, 1, False, False)
            gate_step(NZC - 1, 0, False, False)
            gate_step(NZC - 1, 1, False, True)

            pe.wait_ge(S["pick_ok"], 1)
            HW = NW // 2
            for i in range(2):
                rows = pick[:, i * HW:(i + 1) * HW, :].rearrange("p w e -> p (w e)")
                nc.tensor.matmul(bank[i][:, 0:HW * NE], tri[:, :], rows, start=True, stop=True)
                last = nc.tensor.matmul(bank[2 + i][:, 0:HW * NE], ones[:, :], rows, start=True, stop=True)
            last.then_inc(S["rank_ps"], 1)

            def turn_chunk(q, s):
                n = CHUNKS[s % NCH][1]
                pe.wait_ge(S[f"xs_in{s % 2}"], q * (32 * NCH) + (32 * (s // 2) + 32))
                pe.wait_ge(S["xT_ok"], q * PC + (s + 1))
                for k in range(KD):
                    for t in range(-(-n // P)):
                        m = min(P, n - t * P)
                        last = nc.tensor.transpose(bank[s % 2][:, k * CR + t * P:k * CR + t * P + m],
                                                   xs_rows[0:m, s % 2, t, k * P:(k + 1) * P], ident[0:m, 0:m])
                last.then_inc(S["xT_ps"], 1)

            def skip_turn(q, s):
                pe.wait_ge(S["xT_ps"], q * PC + (s + 1))
                pe.sem_inc(S["xT_ps"], 1)

            def up(q, s):
                j, n = s // NCH, CHUNKS[s % NCH][1]
                pe.wait_ge(S["xT_ok"], q * PC + (s + 3))
                if s % NCH == 0:
                    pe.wait_ge(S[f"w_in{j}"], q * 32 + 32)
                for b in range(FB2):
                    pe.wait_ge(S["hid_ok"], q * (PC * FT) + (s * FT + 2 * b + 2))
                    for i in range(2):
                        f = 2 * b + i
                        for k in range(KD):
                            last = nc.tensor.matmul(up_bank[b][:, i * CR:i * CR + n], w1_sb[:, j, k, f * P:(f + 1) * P],
                                                    xs_feat[:, s % 2, k, 0:n], start=(k == 0), stop=(k == KD - 1))
                    last.then_inc(S["l1_ps"], 1)

            def down(q, s):
                j, n = s // NCH, CHUNKS[s % NCH][1]
                pe.wait_ge(S["hid_ok"], q * (PC * FT) + (s + 2) * FT)
                for t in range(2):
                    m = min(P, n - t * P)
                    pe.wait_ge(S["y_ok"], q * (2 * PC) + (2 * s + t + 1))
                    for f in range(FT):
                        last = nc.tensor.matmul(bank[4 + t][0:m, 0:D], hid[:, f, t * P:t * P + m], w2_sb[:, j, f, :],
                                                start=(f == 0), stop=(f == FT - 1))
                    last.then_inc(S["l2_ps"], 1)

            pe.wait_ge(S["routed"], 1)
            pe.sem_inc(S["xT_ps"], 1)
            pe.sem_inc(S["l1_ps"], 2 * FB2)
            pe.sem_inc(S["l2_ps"], 2)

            def turn_or_skip(q, s, took):
                with pe.If(took > CHUNKS[s % NCH][0]):
                    turn_chunk(q, s)
                with pe.Else():
                    skip_turn(q, s)

            turn_or_skip(0, 0, pe.value_load(taken_i[0:1, 0:1], min_val=0, max_val=N))
            with pe.Fori(0, NE // 2) as q:
                took = [pe.value_load(taken_i[0:1, bass.ds(q * 2 + i, 1)], min_val=0, max_val=N) for i in range(3)]
                for s in range(PC):
                    inside = s % NCH < NCH - 1
                    with pe.If(took[s // NCH] > CHUNKS[s % NCH][0]):
                        up(q, s)
                        if inside:
                            turn_or_skip(q, s + 1, took[s // NCH])
                        down(q, s)
                    with pe.Else():
                        pe.wait_ge(S["l2_ps"], q * (2 * PC) + (2 * s + 2))
                        pe.sem_inc(S["l1_ps"], FB2)
                        pe.sem_inc(S["l2_ps"], 2)
                        if inside:
                            skip_turn(q, s + 1)
                    if not inside:
                        turn_or_skip(q, s + 1, took[(s + 1) // NCH])

            pe.wait_ge(S["odd_rows"], 1)
            nc.tensor.matmul(bank[0][:, 0:1], ones[:, :], odd_n, start=True, stop=True).then_inc(S["odd_ps"], 1)


_INS = ["x", "src", "dst", "L0_gnn_r", "L0_gnn_W", "L0_gnn_y", "L0_ffn_gate_w", "L0_ffn_gate_b",
        "L0_ffn_w1", "L0_ffn_b1", "L0_ffn_w2", "L0_ffn_b2"]


def kernel(**inputs):
    import numpy as np
    import concourse.bacc as bacc
    from concourse.bass_utils import run_bass_kernel_spmd as run

    nc = bacc.Bacc("TRN2", target_bir_lowering=False, num_devices=1)
    arrays, args = {}, []
    for name in _INS:
        v = np.ascontiguousarray(inputs[name])
        arrays[f"in_{name}"] = v
        args.append(nc.dram_tensor(f"in_{name}", v.shape, mybir.dt.from_np(v.dtype), kind="ExternalInput").ap())
    out = nc.dram_tensor("out", arrays["in_x"].shape, F32, kind="ExternalOutput").ap()
    build(nc, *args, out)
    r = run(nc, [arrays], core_ids=[0])
    return r.results[0]["out"]
```

```python
import concourse.bass as bass
from concourse import mybir
from contextlib import ExitStack

F32, I32, BF16 = mybir.dt.float32, mybir.dt.int32, mybir.dt.bfloat16
ALU = mybir.AluOpType
ACT = mybir.ActivationFunctionType
AX = mybir.AxisListType

P = 128


def build(nc, x, src, dst, gnn_r, gnn_w, yidx, gate_w, gate_b, w1, b1, w2, b2, out):
    N, D = x.shape
    E = src.shape[0]
    KD = D // P
    NW = -(-N // P)
    LAST = N - (NW - 1) * P
    EPS = 1e-5
    TOPK = 7
    SELF_W = 2.0
    GT = 4
    TILES = -(-E // (P * 16)) * 16
    GROUPS = TILES // GT
    EB = -(-TILES // P)
    FULL = E // P
    FB = FULL // P
    PAD_DST = 16384
    FAR = 1048576.0
    TOP_BASE = float((NW - 1) * P)
    HSTEPS = TILES // 16
    GS = 8
    PAIRS = NW // 2
    ZC = 14
    NZC = NW // ZC
    U = ZC // 2
    NU = NW // U
    DVE_WIN = (NZC - 1) * U
    DVE_NORM = [i for i in range(ZC) if i % 3 == 1]
    ACT_NORM = [i for i in range(ZC) if i % 3 != 1]
    ACT_WIN = NW - DVE_WIN
    NE = gate_w.shape[1]
    F = w1.shape[2]
    FT = F // P
    CAP = max(1, -(-N * 5 // (4 * NE)))
    SLOTS = NE * CAP
    XW = 2 * D + 2
    TOK, GATE = 2 * D, 2 * D + 1
    CR = 2 * P
    NCH = -(-CAP // CR)
    CHUNKS = [(c, min(CR, CAP - c)) for c in range(0, CAP, CR)]
    PC = 2 * NCH
    XSLOTS = 4
    FB2 = FT // 2
    assert PC % XSLOTS == 0 and NCH % 2 == 0 and FB2 == 4 and KD == 2
    ARENA = 20096

    ctx = ExitStack()
    with ctx:
        def sb(name, shape, dt=F32):
            return ctx.enter_context(nc.sbuf_tensor(name, shape, dt))

        def sem(name):
            return ctx.enter_context(nc.semaphore(name))

        def dram(name, shape, dt=F32):
            return nc.dram_tensor(name, shape, dt, kind="Internal").ap()

        bank = [ctx.enter_context(nc.psum_tensor(f"bank{i}", [P, 512], F32)) for i in range(8)]

        up_bank = [bank[2], bank[3], bank[6], bank[7]]

        def turn_bank(j):
            return j if j < 6 else 2

        z_table = dram("z_table", [NW * P, D])
        dst_rows = dram("dst_rows", [EB * P, P])
        xs = dram("xs", [SLOTS, XW])

        nodes = sb("nodes", [P, KD, NW, P])
        agg = nodes[:, :, :, :].rearrange("p k w c -> p k (w c)")

        iota_i = sb("iota_i", [P, P], I32)
        iota_b = sb("iota_b", [P, P], BF16)
        ident = sb("ident", [P, P])
        ones = sb("ones", [P, P])
        down_one = sb("down_one", [P, P])
        corner = sb("corner", [P, P])
        tri = sb("tri", [P, P])
        zeros = sb("zeros", [P, XW])
        neg_half = sb("neg_half", [P, NW])
        node_i = sb("node_i", [P, NW], I32)
        node_id = sb("node_id", [P, NW])
        win_i = sb("win_i", [P, NW], I32)
        win_f = sb("win_f", [P, NW])
        rep_rel = sb("rep_rel", [P, GT], BF16)

        r_rows = sb("r_rows", [P, D])
        y_i = sb("y_i", [P, 1], I32)
        y_f = sb("y_f", [P, 1])
        wy_i = sb("wy_i", [P, 1], I32)
        is_y = sb("is_y", [P, NW])
        not_y = sb("not_y", [P, NW])
        invalid = sb("invalid", [P, NW])

        arena = sb("arena", [P, ARENA])
        at = [0]

        def carve(shape, dt=F32):
            size = 1
            for n in shape:
                size *= n
            words = size if dt != BF16 else size // 2
            flat = arena[:, at[0]:at[0] + words]
            at[0] += words
            assert at[0] <= ARENA, (at[0], ARENA)
            if dt != F32:
                flat = flat.bitcast(dt)
            if len(shape) == 1:
                return flat
            names = "abcd"[:len(shape)]
            return flat.rearrange(f"p ({' '.join(names)}) -> p {' '.join(names)}", **dict(zip(names[1:], shape[1:])))

        gath = carve([GS, GT, D])
        at[0] = 0
        stage_i = carve([2, EB, P], I32)
        stage_f = carve([2, EB, P])
        grp_min = carve([GROUPS])[0:1, :]
        grp_max = carve([GROUPS])[0:1, :]
        at[0] = 0
        dst_i = carve([EB * P], I32)
        low_i = carve([EB * P], I32)
        lim_row = carve([2, EB * P])[0:1, :, :]
        at[0] = GS * GT * D
        src_idx = carve([EB * P], I32)
        dst_f = carve([EB * P])
        lo_b = carve([EB * P], BF16)
        hi_b = carve([EB * P], BF16)
        rel_b = carve([EB * P], BF16)
        here = at[0]
        oh_lo = carve([2, 16, P], BF16)
        oh_hi = carve([2, 16, NW], BF16)
        at[0] = here
        stage_f2 = carve([EB, P])
        at[0] = here
        near_row = carve([8 * P])[0:1, :]
        at[0] = here
        cross_row = carve([TILES])[0:1, :]
        at[0] = here
        sel = carve([2, GT, P])
        at[0] = here + (2 * 16 * (P + NW)) // 2
        idx_ring = carve([2, 16], I32)
        bn1 = carve([NW, 6])
        last_i = carve([EB], I32)
        last_low = carve([EB], I32)
        last_lo = carve([16], BF16)
        last_hi = carve([16], BF16)
        first_ring = carve([2, U], I32)
        at[0] = 0
        first_rows = carve([2, U, P])
        is_less = carve([U, P])
        diff = carve([2, U, KD, P])
        at[0] = here + GT * P * 2
        z_stat = carve([U, KD, P])
        z_back = carve([2, D])

        at[0] = here + (2 * 16 * (P + NW)) // 2
        at[0] += 2 * 16
        grp_far = carve([GROUPS])

        at[0] = 0
        w1_sb = carve([2, KD, F])
        w2_sb = carve([2, FT, D])
        b2_rows = carve([NE, D])
        gnnw_sb = carve([KD, D])
        gatew_sb = carve([KD, NE])
        b1_cols = carve([NE * FT])
        turn = at[0]
        x_tile = carve([U, D])
        agg_stat = carve([U, KD, P])
        at[0] = turn
        h_tile = carve([U, KD, P])
        h_feat = carve([U, KD, P])
        bn = carve([NW, 6])
        gate_l = carve([NW, NE])
        gate_e = carve([NW, NE])
        gate_t = carve([NW, NE])
        pick = carve([NW, NE])
        b1_rows = carve([P])
        at[0] = turn
        h_send = carve([ZC, XW])
        send_idx = carve([2, ZC // 2], I32)
        at[0] = turn
        xs_rows = carve([XSLOTS, 2, XW])
        xs_feat = carve([2, KD, CR])
        hid = carve([FT, CR])
        y_row = carve([D])
        y_low = carve([D])
        y_high = carve([D])
        y_fin = carve([D], I32)
        o_tile = carve([4, D])
        out_f = carve([4])
        out_miss = carve([4])
        out_idx = carve([4], I32)
        b1_pair = carve([2 * FT])

        tile_lim = sb("tile_lim", [P, 2, EB])
        grp_base = sb("grp_base", [1, GROUPS])
        grp_bad = sb("grp_bad", [1, GROUPS])
        grp_cmp = sb("grp_cmp", [1, GROUPS])
        base_i = sb("base_i", [1, GROUPS], I32)
        bad_sum = sb("bad_sum", [1, 1])
        bad_i = sb("bad_i", [1, 1], I32)
        mine_y = sb("mine_y", [P, 1])
        r_y = sb("r_y", [P, D])
        EDGE_TURNS = [(i, b, min(4, EB - b)) for i in range(2) for b in range(0, EB, 4)]

        neg_mean = sb("neg_mean", [P, NW])
        rstd = sb("rstd", [P, NW])
        shift = sb("shift", [P, NW])
        dist = sb("dist", [P, NW])
        deg = sb("deg", [P, NW])
        last_hist = sb("last_hist", [P, NW])
        first_f = sb("first_f", [P, NW])
        first_i = sb("first_i", [P, NW], I32)
        n_less = sb("n_less", [P, NW])
        row_start = sb("row_start", [P, NW + 1])
        disorder = sb("disorder", [P, 1])
        cross_sum = sb("cross_sum", [1, 1])
        unsorted_i = sb("unsorted_i", [1, 1], I32)
        dinv = sb("dinv", [P, NW])

        near = sb("near", [P, NW])
        near8 = sb("near8", [P, 8])
        top8 = sb("top8", [1, 8])
        thr = sb("thr", [P, 1])
        above = sb("above", [P, NW])
        tied = sb("tied", [P, NW])
        n_above = sb("n_above", [P, 1])
        room = sb("room", [P, 1])
        tie_scan = sb("tie_scan", [P, NW])
        tie_rank = sb("tie_rank", [P, NW])
        chosen = sb("chosen", [P, NW])

        col_fix = sb("col_fix", [P, KD])

        mean2 = sb("mean2", [P, NW])
        var2 = sb("var2", [P, NW])
        gap2 = sb("gap2", [P, NW])
        rstd2 = sb("rstd2", [P, NW])
        shift2 = sb("shift2", [P, NW])
        best = sb("best", [P, NW])
        norm = sb("norm", [P, NW])
        expert = sb("expert", [P, NW])
        place = sb("place", [P, NW])
        kept = sb("kept", [P, NW])
        weight = sb("weight", [P, NW])
        slot_f = sb("slot_f", [P, NW])
        put_idx = sb("put_idx", [P, NW], I32)
        tok_id = sb("tok_id", [P, NW])
        rank_e = sb("rank_e", [P, NE])
        iota_f = sb("iota_f", [P, NE])
        gateb_sb = sb("gateb_sb", [P, NE])
        taken_f = sb("taken_f", [1, NE])
        taken_i = sb("taken_i", [1, NE + 1], I32)

        S = {}
        for name in ("""edges_cleared edges_in r_in y_in consts edges_float edge_psum edges_out lims limps lim_rows bases
                     cmp_ps hist_built hist_used hist_ps mean_sum square_ok ssum dst_rows_out last_built first_ok
                     first_idx first_in0 first_in1 first_used starts_ok starts_ps hist_start less_ok bn1_ok shift_ok
                     mem_ok mem_patched diff_ok dist_ok deg_ok z_ok tick near_ok near_ps chosen_ok zstat_ok zT_ps
                     agg_init selps idx_ok sel_ok agg_ps agg_added fixed xt_in2 xt_in3 xt_in4 xt_in5 xt_in6 out_done2
                     out_done3 out_done4 out_done5 out_done6 zb_in0 zb_in1 zb_used rep_idx rep_got rep_free rep_relok
                     rep_sel rep_ps rep_added rep_bad rep_dst bn_ok zeroed rows_zero w_small w_in0 w_in1 xt_in0 xt_in1
                     aggst_ok conv_ps x1_ok var_ok lnb_ok h_ok h_dve hT_ps hT_ok logit_ps gate_taken gate_in gate_out
                     pick_ok rank_ps routed send_h pair_sent no_token send_x send_ids ids_ok res_ok row_step out_x1
                     sidx sent0 sent1 xs_in0 xs_in2 xs_in3 xs_in1 xT_ps xT_ok l1_ps hid_ok l2_ps y_ok b1_now out_done0
                     out_done1 b1_ps b1_ok dve_ch pool_ch""").split():
            S[name] = sem(name)
        x_chunk = [sem(f"x_chunk{c}") for c in range(NZC)]
        table_out = [sem(f"table_out{c}") for c in range(NZC)]
        gathered = [sem(f"gathered{i}") for i in range(GS)]

        block = ctx.enter_context(nc.Block())

        x_win = x[0:(NW - 1) * P, :].rearrange("(w p) (k c) -> p k w c", p=P, k=KD)
        x_last = x[(NW - 1) * P:N, :].rearrange("p (k c) -> p k c", k=KD)
        z_win = z_table.rearrange("(w p) (k c) -> p k w c", p=P, k=KD)

        @block.sync
        def _(sp):
            for i, e in enumerate((dst, src)):
                sp.dma_start(stage_i[:, i, 0:FB, :],
                             e[0:FB * P * P].rearrange("(b r e) -> r b e", r=P, e=P)).then_inc(S["edges_in"], 16)
            sp.wait_ge(S["edges_cleared"], 2)
            for i, e in enumerate((dst, src)):
                rows = FULL - FB * P
                sp.dma_start(stage_i[0:rows, i, FB, :],
                             e[FB * P * P:FULL * P].rearrange("(r e) -> r e", e=P)).then_inc(S["edges_in"], 16)
                sp.dma_start(stage_i[rows:rows + 1, i, FB, 0:E - FULL * P],
                             e[FULL * P:E].rearrange("(r e) -> r e", r=1)).then_inc(S["edges_in"], 16)
            sp.dma_start(y_i[:, :], yidx.rearrange("(a b) -> a b", a=1).to_broadcast([P, 1])).then_inc(S["y_in"], 16)
            sp.dma_start(r_rows[:, :], gnn_r.to_broadcast([P, D])).then_inc(S["r_in"], 16)
            def load_nodes(c):
                a, b = c * ZC, min((c + 1) * ZC, NW - 1)
                for k in range(KD):
                    sp.dma_start(nodes[:, k, a:b, :], x_win[:, k, a:b, :]).then_inc(x_chunk[c], 16)
            sp.wait_ge(S["edges_float"], 1)
            sp.dma_start(dst_rows.rearrange("(b r) e -> r b e", r=P), stage_f[:, 0, :, :]).then_inc(S["dst_rows_out"], 16)
            for c in range(NZC):
                load_nodes(c)
            sp.wait_ge(S["edges_cleared"], 3)
            sp.dma_start(nodes[0:LAST, :, NW - 1, :], x_last).then_inc(x_chunk[NZC - 1], 16)

            for c in range(NZC):
                sp.wait_ge(S["z_ok"], c + 1)
                for k in range(KD):
                    sp.dma_start(z_win[:, k, c * ZC:(c + 1) * ZC, :],
                                 nodes[:, k, c * ZC:(c + 1) * ZC, :]).then_inc(table_out[c], 16)

            def load_weights(e, j, small=False):
                sp.dma_start(w1_sb[:, j, :, :], w1[bass.ds(e, 1), :, :].rearrange("o (k p) f -> p (o k) f", p=P)).then_inc(S[f"w_in{j}"], 16)
                sp.dma_start(w2_sb[:, j, :, :], w2[bass.ds(e, 1), :, :].rearrange("o (t p) d -> p (o t) d", p=P)).then_inc(S[f"w_in{j}"], 16)

            for j in range(2):
                sp.wait_ge(S["agg_init"], NW)
                sp.dma_start(z_back[:, j, :], z_table[j * P:(j + 1) * P, :]).then_inc(S[f"zb_in{j}"], 16)
            with sp.Fori(1, PAIRS) as q:
                for j in range(2):
                    sp.wait_ge(S["zb_used"], q * 2 + (j - 1))
                    sp.dma_start(z_back[:, j, :], z_table[bass.ds((q * 2 + j) * P, P), :]).then_inc(S[f"zb_in{j}"], 16)

            sp.wait_ge(S["fixed"], 1)
            sp.dma_start(gnnw_sb, gnn_w.rearrange("(k p) d -> p k d", p=P)).then_inc(S["w_small"], 16)
            sp.dma_start(gatew_sb, gate_w.rearrange("(k p) e -> p k e", p=P)).then_inc(S["w_small"], 16)
            sp.dma_start(gateb_sb[:, :], gate_b.rearrange("(o e) -> o e", o=1).to_broadcast([P, NE])).then_inc(S["w_small"], 16)
            sp.dma_start(b1_rows[0:NE * FT, :], b1.rearrange("e (t c) -> (e t) c", c=P)).then_inc(S["w_small"], 16)
            sp.dma_start(b2_rows, b2.rearrange("(o e) d -> o e d", o=1).to_broadcast([P, NE, D])).then_inc(S["w_small"], 16)

            def load_x(w, j):
                sp.dma_start(x_tile[:, j, :], x[bass.ds(w * P, P), :]).then_inc(S[f"xt_in{j}"], 16)
            for j in range(U):
                load_x(j, j)
            with sp.Fori(1, NU - 1) as q:
                for j in range(U):
                    sp.wait_ge(S["x1_ok"], q * U + (j - U + 1))
                    load_x(q * U + j, j)
            for j in range(U):
                w = NW - U + j
                n = P if w < NW - 1 else LAST
                sp.wait_ge(S["x1_ok"], w - U + 1)
                sp.dma_start(x_tile[0:n, j, :], x[w * P:w * P + n, :]).then_inc(S[f"xt_in{j}"], 16)
            load_weights(0, 0)
            load_weights(1, 1)
            for c in range(NZC):
                a, b = c * ZC, min((c + 1) * ZC, NW - 1)
                sp.wait_ge(S["x1_ok"], b + (c == NZC - 1))
                for k in range(KD):
                    sp.dma_start(out[0:(NW - 1) * P, :].rearrange("(w p) (k c) -> p k w c", p=P, k=KD)[:, k, a:b, :],
                                 nodes[:, k, a:b, :]).then_inc(S["out_x1"], 16)
            sp.dma_start(out[(NW - 1) * P:N, :].rearrange("p (k c) -> p k c", k=KD), nodes[0:LAST, :, NW - 1, :]).then_inc(S["out_x1"], 16)

            def load_chunk(e, c, slot):
                c0, n = CHUNKS[c]
                full = n // P
                sp.dma_start(xs_rows[:, slot, 0:full, :],
                             xs[bass.ds(e * CAP + c0, full * P), :].rearrange("(t p) d -> p t d", p=P)).then_inc(S[f"xs_in{slot}"], 16)
                if n % P:
                    sp.dma_start(xs_rows[0:n % P, slot, full:full + 1, :],
                                 xs[bass.ds(e * CAP + (c0 + full * P), n % P), :].rearrange("(t p) d -> p t d", t=1)).then_inc(S[f"xs_in{slot}"], 16)
                else:
                    sp.sem_inc(S[f"xs_in{slot}"], 16)

            def load_or_skip(e, c, slot, took):
                with sp.If(took > CHUNKS[c][0]):
                    load_chunk(e, c, slot)
                with sp.Else():
                    sp.sem_inc(S[f"xs_in{slot}"], 32)

            def expert_pair(q, last):
                took = [sp.value_load(taken_i[0:1, bass.ds(q * 2 + i, 1)], min_val=0, max_val=N) for i in range(3)]
                for j in range(2):
                    for c in range(NCH):
                        s = j * NCH + c
                        more = s + XSLOTS
                        if not (last and more >= PC):
                            sp.wait_ge(S["res_ok"], q * (2 * PC) + (2 * s + 4))
                            sp.sem_inc(S["tick"], 1)
                            load_or_skip(q * 2 + more // NCH, more % NCH, s % XSLOTS, took[more // NCH])
                    if not last:
                        sp.wait_ge(S["y_ok"], q * (2 * PC) + (2 * (j + 1) * NCH + 2))
                        load_weights(q * 2 + (j + 2), j)
            sp.wait_ge(S["rows_zero"], 16 * (SLOTS // P + 1))
            sp.wait_ge(S["sent0"], 16 * ZC // 2 * NZC)
            sp.wait_ge(S["sent1"], 16 * ZC // 2 * NZC)
            for c in range(XSLOTS):
                load_or_skip(0, c, c, sp.value_load(taken_i[0:1, 0:1], min_val=0, max_val=N))
            with sp.Fori(0, NE // 2 - 1) as q:
                expert_pair(q, False)
            expert_pair(NE // 2 - 1, True)

            for j in range(2):
                sp.wait_ge(S[f"w_in{j}"], 32 * (NE // 2))
            for slot in range(4):
                sp.wait_ge(S[f"out_done{slot}"], 16 * (NE * NCH // 2))

        @block.gpsimd
        def _(pool):
            nc.gpsimd.memset(stage_i[:, 0, FB, :], PAD_DST).then_inc(S["edges_cleared"], 1)
            nc.gpsimd.memset(stage_i[:, 1, FB:EB, :], 0).then_inc(S["edges_cleared"], 1)
            pool.wait_ge(S["edges_cleared"], 2)
            nc.gpsimd.memset(nodes[64:P, :, NW - 1, :], 0.0).then_inc(S["edges_cleared"], 1)
            pool.wait_ge(S["edges_cleared"], 3)
            nc.gpsimd.iota(iota_i[:, :], [[1, P]], base=0, channel_multiplier=0).then_inc(S["pool_ch"], 1)
            nc.gpsimd.iota(node_i[:, :], [[P, NW]], base=0, channel_multiplier=1).then_inc(S["pool_ch"], 1)
            nc.gpsimd.iota(win_i[:, :], [[P, NW]], base=0, channel_multiplier=0).then_inc(S["pool_ch"], 1)
            nc.gpsimd.memset(zeros[:, :], 0.0).then_inc(S["pool_ch"], 1)
            nc.gpsimd.memset(ones[:, :], 1.0).then_inc(S["pool_ch"], 1)
            nc.gpsimd.memset(neg_half[:, :], -0.5).then_inc(S["pool_ch"], 1)
            pool.wait_ge(S["pool_ch"], 6)
            pool.sem_inc(S["zeroed"], 1)
            nc.gpsimd.tensor_copy(iota_b[:, :], iota_i[:, :]).then_inc(S["consts"], 1)
            nc.gpsimd.tensor_copy(node_id[:, :], node_i[:, :]).then_inc(S["consts"], 1)
            nc.gpsimd.tensor_copy(win_f[:, :], win_i[:, :]).then_inc(S["consts"], 1)
            for m, shifted in ((ident, 0), (down_one, -1), (corner, P - 1)):
                nc.gpsimd.affine_select(out=m[:, :], in_=zeros[:, 0:P], compare_op=ALU.not_equal, fill=1.0,
                                        base=shifted, pattern=[[-1, P]], channel_multiplier=1).then_inc(S["consts"], 1)
            nc.gpsimd.affine_select(out=tri[:, :], in_=ones[:, :], compare_op=ALU.is_ge, fill=0.0,
                                    base=0, pattern=[[1, P]], channel_multiplier=-1).then_inc(S["consts"], 1)

            pool.wait_ge(S["first_ok"], 1)
            pool.wait_ge(S["dst_rows_out"], 16)

            def fetch_first(q, half, first):
                if not first:
                    pool.wait_ge(S["first_used"], q * 2 + (half - 1))
                    pool.sem_inc(S["tick"], 1)
                nc.gpsimd.tensor_copy(first_ring[:, half, :], first_i[:, bass.ds(q * ZC + half * U, U)]).then_inc(S["first_idx"], 1)
                pool.wait_ge(S["first_idx"], q * 2 + (half + 1))
                pool.sem_inc(S["tick"], 1)
                for i in range(U):
                    nc.gpsimd.indirect_dma_start(
                        first_rows[:, half, i, :], None, dst_rows,
                        bass.IndirectOffsetOnAxis(ap=first_ring[:, half, i:i + 1], axis=0)).then_inc(S[f"first_in{half}"], 16)
            fetch_first(0, 0, True)
            fetch_first(0, 1, True)
            with pool.Fori(1, NZC // 2 + 1) as q:
                fetch_first(q, 0, False)
                fetch_first(q, 1, False)

            pool.wait_ge(S["ssum"], 1)
            nc.gpsimd.tensor_tensor(rstd[:, :], var2[:, :], neg_half[:, :], ALU.pow).then_inc(S["pool_ch"], 1)
            pool.wait_ge(S["pool_ch"], 7)
            nc.gpsimd.tensor_tensor(rstd[:, :], rstd[:, :], not_y[:, :], ALU.mult).then_inc(S["pool_ch"], 1)
            pool.wait_ge(S["pool_ch"], 8)
            nc.gpsimd.tensor_tensor(shift[:, :], rstd[:, :], neg_mean[:, :], ALU.mult).then_inc(S["shift_ok"], 1)
            with pool.Fori(NZC // 2 + 1, NZC) as q:
                fetch_first(q, 0, False)
                fetch_first(q, 1, False)

            pool.wait_ge(S["deg_ok"], 1)
            nc.gpsimd.tensor_tensor(dinv[:, :], deg[:, :], neg_half[:, :], ALU.pow).then_inc(S["deg_ok"], 1)

            for c in range(NZC):
                pool.wait_ge(table_out[c], 16 * KD)
            pool.wait_ge(S["dist_ok"], 2 * NZC)
            STEPS = TILES // 32
            def take_indices(t0, half):
                nc.gpsimd.tensor_copy(idx_ring[:, half, :], src_idx[:, bass.ds(t0, 16)]).then_inc(S["idx_ok"], 1)

            def gather_body(q, first):
                for half in range(2):
                    if not first:
                        for s in range(4):
                            pool.wait_ge(gathered[half * 4 + s], q * 64)
                        pool.sem_inc(S["tick"], 1)
                    take_indices(q * 32 + half * 16, half)
                    pool.wait_ge(S["idx_ok"], q * 2 + half + 1)
                    pool.sem_inc(S["tick"], 1)
                    for s in range(4):
                        slot = half * 4 + s
                        if not first:
                            pool.wait_ge(S["agg_ps"], (q - 1) * 8 + slot + 1)
                            pool.sem_inc(S["tick"], 1)
                        for t in range(GT):
                            nc.gpsimd.indirect_dma_start(
                                gath[:, slot, t, :], None, z_table,
                                bass.IndirectOffsetOnAxis(ap=idx_ring[:, half, s * GT + t:s * GT + t + 1], axis=0),
                            ).then_inc(gathered[slot], 16)

            gather_body(0, True)
            with pool.Fori(1, STEPS) as q:
                gather_body(q, False)

            pool.wait_ge(S["bases"], 1)
            n_bad = pool.value_load(bad_i[0:1, 0:1], min_val=0, max_val=GROUPS)
            with pool.If(n_bad > 0):
                pool.wait_ge(S["agg_ps"], GROUPS)
                with pool.Fori(0, GROUPS) as g:
                    pool.wait_ge(S["rep_free"], g + 1)
                    pool.sem_inc(S["tick"], 1)
                    nc.gpsimd.tensor_copy(idx_ring[:, 0, 0:GT], src_idx[:, bass.ds(g * GT, GT)]).then_inc(S["rep_idx"], 1)
                    pool.wait_ge(S["rep_idx"], g + 1)
                    pool.sem_inc(S["tick"], 1)
                    for t in range(GT):
                        nc.gpsimd.indirect_dma_start(
                            gath[:, 0, t, :], None, z_table,
                            bass.IndirectOffsetOnAxis(ap=idx_ring[:, 0, t:t + 1], axis=0)).then_inc(S["rep_got"], 16)

            pool.wait_ge(S["var_ok"], 1)
            nc.gpsimd.tensor_tensor(rstd2[:, :], var2[:, :], neg_half[:, :], ALU.pow).then_inc(S["var_ok"], 1)

            pool.wait_ge(S["routed"], 1)
            pool.wait_ge(S["rows_zero"], 16 * (SLOTS // P + 1))
            last_row = pool.to_reg(SLOTS - 1)
            HZ = ZC // 2

            def index_half(to, frm, q, half, s_idx):
                nc.gpsimd.tensor_copy(to[:, half, :], frm[:, bass.ds(q * ZC + half * HZ, HZ)]).then_inc(S[s_idx], 1)
                pool.wait_ge(S[s_idx], q * 2 + half + 1)
                pool.sem_inc(S["tick"], 1)

            def send(q, first):
                for half in range(2):
                    if not first:
                        pool.wait_ge(S[f"sent{half}"], q * (16 * HZ))
                        pool.sem_inc(S["tick"], 1)
                    index_half(send_idx, put_idx, q, half, "sidx")
                    for s in range(HZ):
                        pool.wait_ge(S["send_h"], q * ZC + (half * HZ + s + 1))
                        pool.sem_inc(S["tick"], 1)
                        if s == 0:
                            pool.wait_ge(S["send_ids"], q * 2 + (half + 1))
                            pool.sem_inc(S["tick"], 1)
                        pool.wait_ge(S["send_x"], q * ZC + (half * HZ + s + 1))
                        pool.sem_inc(S["tick"], 1)
                        nc.gpsimd.indirect_dma_start(
                            xs, bass.IndirectOffsetOnAxis(ap=send_idx[:, half, s:s + 1], axis=0), h_send[:, half * HZ + s, :], None,
                            bounds_check=last_row, oob_is_err=False).then_inc(S[f"sent{half}"], 16)
            send(0, True)
            with pool.Fori(1, NZC) as q:
                send(q, False)

            pool.wait_ge(S["out_x1"], 16 * (KD * NZC + 1))
            last_node = pool.to_reg(N - 1)
            pool.sem_inc(S["pair_sent"], 1)
            with pool.Fori(0, NE // 2) as q:
                for s in range(PC):
                    for t in range(2):
                        n, slot = min(P, CHUNKS[s % NCH][1] - t * P), s % 2 * 2 + t
                        pool.wait_ge(S["res_ok"], q * (2 * PC) + (2 * s + t + 3))
                        pool.sem_inc(S["tick"], 1)
                        nc.gpsimd.indirect_dma_start(
                            out, bass.IndirectOffsetOnAxis(ap=out_idx[0:n, slot:slot + 1], axis=0), o_tile[0:n, slot, :], None,
                            bounds_check=last_node, oob_is_err=False).then_inc(S[f"out_done{slot}"], 16)
                for slot in range(4):
                    pool.wait_ge(S[f"out_done{slot}"], q * (16 * NCH) + 16 * NCH)
                pool.sem_inc(S["pair_sent"], 1)

        @block.scalar
        def _(act):
            def node_row(w):
                return nodes[:, :, w, :]

            act.wait_ge(S["shift_ok"], 1)
            with act.Fori(0, ACT_WIN // 2) as q:
                for j in range(2):
                    nc.scalar.activation(node_row(q * 2 + j), node_row(q * 2 + j), ACT.Identity,
                                         bias=shift[:, bass.ds(q * 2 + j, 1)],
                                         scale=rstd[:, bass.ds(q * 2 + j, 1)]).then_inc(S["mean_sum"], 1)
            act.wait_ge(S["mean_sum"], ACT_WIN)
            act.sem_inc(S["mem_ok"], 1)
            for b in range(2 * NZC):
                act.wait_ge(S["diff_ok"], KD * (b + 1))
                nc.scalar.activation(diff[:, b % 2, :, :, :], diff[:, b % 2, :, :, :], ACT.Square).then_inc(S["square_ok"], 1)

            def z_tile(w, j):
                nc.scalar.activation(z_stat[:, j, :, :], node_row(w), ACT.Copy).then_inc(S["zstat_ok"], 1)
            act.wait_ge(S["z_ok"], 1)
            for i in range(ZC):
                if i >= U:
                    act.wait_ge(S["zT_ps"], i - U + 1)
                z_tile(i, i % U)
            with act.Fori(1, NZC) as q:
                act.wait_ge(S["z_ok"], q + 1)
                act.sem_inc(S["tick"], 1)
                for i in range(ZC):
                    act.wait_ge(S["zT_ps"], q * ZC + (i - U + 1))
                    z_tile(q * ZC + i, i % U)

            act.wait_ge(S["zeroed"], 1)
            ROW_WIN = SLOTS // P
            with act.Fori(0, ROW_WIN) as i:
                act.wait_ge(S["agg_ps"], i * (GROUPS // ROW_WIN) + 1)
                act.dma_start(xs[bass.ds(i * P, P), :], zeros[:, :]).then_inc(S["rows_zero"], 16)
            act.dma_start(xs[ROW_WIN * P:SLOTS, :], zeros[0:SLOTS - ROW_WIN * P, :]).then_inc(S["rows_zero"], 16)

            act.wait_ge(S["fixed"], 1)
            def agg_tile(w, j):
                nc.scalar.activation(agg_stat[:, j, :, :], node_row(w), ACT.Copy).then_inc(S["aggst_ok"], 1)
            for j in range(U):
                agg_tile(j, j)
            with act.Fori(1, NU) as q:
                for j in range(U):
                    act.wait_ge(S["conv_ps"], q * U + (j - U + 1))
                    agg_tile(q * U + j, j)
            act.wait_ge(S["lnb_ok"], 1)
            def norm_tile(to, w, sm):
                nc.scalar.activation(to, node_row(w), ACT.Identity, bias=shift2[:, bass.ds(w, 1)],
                                     scale=rstd2[:, bass.ds(w, 1)]).then_inc(S[sm], 1)
            for i in ACT_NORM:
                if i >= U:
                    act.wait_ge(S["hT_ps"], i - U + 1)
                    act.sem_inc(S["tick"], 1)
                norm_tile(h_tile[:, i % U, :, :], i, "h_ok")
            with act.Fori(1, NZC) as q:
                for i in ACT_NORM:
                    act.wait_ge(S["hT_ps"], q * ZC + (i - U + 1))
                    act.sem_inc(S["tick"], 1)
                    norm_tile(h_tile[:, i % U, :, :], q * ZC + i, "h_ok")
            act.wait_ge(S["gate_in"], 1)
            nc.scalar.activation(gate_e, gate_l, ACT.Exp).then_inc(S["gate_out"], 1)
            act.wait_ge(S["routed"], 1)
            def send_tile(w, s):
                norm_tile(h_send[:, s, 0:D].rearrange("p (k c) -> p k c", k=KD), w, "send_h")
            for s in range(ZC):
                send_tile(s, s)
            with act.Fori(1, NZC) as q:
                for half in range(2):
                    act.wait_ge(S[f"sent{half}"], q * (16 * ZC // 2))
                    act.sem_inc(S["tick"], 1)
                    for s in range(half * ZC // 2, (half + 1) * ZC // 2):
                        send_tile(q * ZC + s, s)

            for half in range(2):
                act.wait_ge(S[f"sent{half}"], 16 * U * NZC)
            act.sem_inc(S["hid_ok"], FT)
            with act.Fori(0, NE // 2) as q:
                took = [act.value_load(taken_i[0:1, bass.ds(q * 2 + i, 1)], min_val=0, max_val=N) for i in range(2)]
                act.wait_ge(S["hid_ok"], q * (PC * FT) + FT)
                nc.scalar.activation(b1_pair, b1_cols[:, bass.ds(q * (2 * FT), 2 * FT)], ACT.Copy).then_inc(S["b1_now"], 1)
                act.wait_ge(S["b1_now"], q + 1)
                act.sem_inc(S["tick"], 1)
                for j in range(2):
                    for c in range(NCH):
                        n, s = CHUNKS[c][1], j * NCH + c
                        with act.If(took[j] > CHUNKS[c][0]):
                            act.wait_ge(S["l2_ps"], q * (2 * PC) + (2 * s + 2))
                            for f in range(FT):
                                act.wait_ge(S["l1_ps"], q * (PC * FB2) + ((s + 2) * FB2 + f // 2 + 1))
                                nc.scalar.activation(hid[:, f, 0:n], up_bank[f // 2][:, f % 2 * CR:f % 2 * CR + n], ACT.Relu,
                                                     bias=b1_pair[:, j * FT + f:j * FT + f + 1]).then_inc(S["hid_ok"], 1)
                        with act.Else():
                            act.wait_ge(S["hid_ok"], q * (PC * FT) + (s + 1) * FT)
                            act.sem_inc(S["hid_ok"], FT)

        @block.vector
        def _(dve):
            ch = [0]

            def then(ins):
                ch[0] += 1
                ins.then_inc(S["dve_ch"], 1)
                dve.wait_ge(S["dve_ch"], ch[0])

            dve.wait_ge(S["edges_in"], 6 * 16)
            nc.vector.tensor_copy(stage_f[:, 0, :, :], stage_i[:, 0, :, :]).then_inc(S["edges_float"], 1)
            nc.vector.tensor_copy(stage_f[:, 1, :, :], stage_i[:, 1, :, :]).then_inc(S["edges_float"], 1)
            dve.wait_ge(S["edges_float"], 1)
            then(nc.vector.tensor_tensor(stage_f2[:, :, 0:P - 1], stage_f[:, 0, :, 0:P - 1], stage_f[:, 0, :, 1:P], ALU.is_gt))
            then(nc.vector.tensor_reduce(disorder[:, :], stage_f2[:, :, 0:P - 1], AX.XY, ALU.add))
            then(nc.vector.tensor_copy(last_i, stage_f[:, 0, :, P - 1]))
            then(nc.vector.tensor_single_scalar(last_low, last_i, 127, ALU.bitwise_and))
            then(nc.vector.tensor_copy(last_lo[:, 0:EB], last_low))
            then(nc.vector.tensor_single_scalar(last_low, last_i, 7, ALU.arith_shift_right))
            then(nc.vector.tensor_copy(last_hi[:, 0:EB], last_low))
            then(nc.vector.tensor_reduce(tile_lim[:, 0, :], stage_f[:, 0, :, :], AX.X, ALU.min))
            then(nc.vector.scalar_tensor_tensor(stage_f2[:, :, :], stage_f[:, 0, :, :], float(PAD_DST), stage_f[:, 0, :, :],
                                                ALU.is_lt, ALU.mult))
            nc.vector.tensor_reduce(tile_lim[:, 1, :], stage_f2[:, :, :], AX.X, ALU.max).then_inc(S["lims"], 1)
            for n, (i, b0, nb) in enumerate(EDGE_TURNS):
                dve.wait_ge(S["edge_psum"], n + 1)
                to = (dst_f if i == 0 else src_idx)[:, b0 * P:(b0 + nb) * P]
                nc.vector.tensor_copy(to, bank[n % 2][:, 0:nb * P]).then_inc(S["edges_out"], 1)
            dve.wait_ge(S["edges_out"], len(EDGE_TURNS))
            dve.wait_ge(S["dst_rows_out"], 16)
            for n in range(len(EDGE_TURNS)):
                i, b0, nb = EDGE_TURNS[n]
                dve.wait_ge(S["limps"], n + 1)
                then(nc.vector.tensor_copy(lim_row[0:1, i, b0 * P:(b0 + nb) * P], bank[2 + n % 2][0:1, 0:nb * P]))
                dve.sem_inc(S["lim_rows"], 1)
            lim_grp = lim_row[0:1, :, 0:TILES].rearrange("p i (g t) -> p i g t", t=GT)
            then(nc.vector.tensor_reduce(grp_min[:, :], lim_grp[:, 0, :, :], AX.X, ALU.min))
            then(nc.vector.tensor_reduce(grp_max[:, :], lim_grp[:, 1, :, :], AX.X, ALU.max))
            then(nc.vector.tensor_scalar(grp_base[:, :], grp_min[:, :], TOP_BASE, None, ALU.min))
            then(nc.vector.tensor_tensor(grp_max[:, :], grp_max[:, :], grp_base[:, :], ALU.subtract))
            then(nc.vector.tensor_scalar(grp_bad[:, :], grp_max[:, :], float(P), None, ALU.is_ge))
            then(nc.vector.tensor_reduce(bad_sum[:, :], grp_bad[:, :], AX.X, ALU.add))
            then(nc.vector.tensor_copy(bad_i[:, :], bad_sum[:, :]))
            then(nc.vector.tensor_copy(base_i[:, :], grp_base[:, :]))
            then(nc.vector.scalar_tensor_tensor(grp_cmp[:, :], grp_bad[:, :], -FAR, grp_base[:, :], ALU.mult, ALU.add))
            dve.sem_inc(S["bases"], 1)
            dve.wait_ge(S["cmp_ps"], 1)
            then(nc.vector.tensor_tensor(rel_b[:, 0:TILES].rearrange("p (g t) -> p g t", t=GT),
                                         dst_f[:, 0:TILES].rearrange("p (g t) -> p g t", t=GT),
                                         bank[4][:, 0:GROUPS].unsqueeze(2).to_broadcast([P, GROUPS, GT]), ALU.subtract))
            then(nc.vector.tensor_tensor(cross_row[0:1, 0:TILES - 1], lim_row[0:1, 0, 1:TILES], lim_row[0:1, 1, 0:TILES - 1], ALU.is_lt))
            then(nc.vector.tensor_reduce(cross_sum[:, :], cross_row[0:1, 0:TILES - 1], AX.X, ALU.add))
            then(nc.vector.tensor_tensor(cross_sum[:, :], cross_sum[:, :], bank[4][0:1, GROUPS:GROUPS + 1], ALU.add))
            then(nc.vector.tensor_copy(unsorted_i[:, :], cross_sum[:, :]))
            nc.vector.tensor_tensor(oh_lo[:, 0, 0:EB, :], iota_b[:, :].unsqueeze(1).to_broadcast([P, EB, P]),
                                    last_lo[:, 0:EB].unsqueeze(2).to_broadcast([P, EB, P]), ALU.is_equal).then_inc(S["last_built"], 1)
            nc.vector.tensor_tensor(oh_hi[:, 0, 0:EB, :], iota_b[:, 0:NW].unsqueeze(1).to_broadcast([P, EB, NW]),
                                    last_hi[:, 0:EB].unsqueeze(2).to_broadcast([P, EB, NW]), ALU.is_equal).then_inc(S["last_built"], 1)
            dve.wait_ge(S["starts_ps"], 1)
            then(nc.vector.tensor_copy(last_hist[:, :], bank[5][:, 0:NW]))
            dve.sem_inc(S["starts_ok"], 1)
            dve.wait_ge(S["starts_ps"], 2)
            then(nc.vector.tensor_tensor_scan(first_f[:, :], ones[:, 0:NW], bank[0][:, NW:2 * NW], 0.0, ALU.mult, ALU.add))
            then(nc.vector.tensor_tensor(first_f[:, :], first_f[:, :], bank[0][:, NW:2 * NW], ALU.subtract))
            then(nc.vector.tensor_tensor(first_f[:, :], first_f[:, :], bank[0][:, 0:NW], ALU.add))
            then(nc.vector.tensor_tensor(first_f[:, :], first_f[:, :], last_hist[:, :], ALU.subtract))
            then(nc.vector.tensor_copy(first_i[:, :], first_f[:, :]))
            dve.sem_inc(S["first_ok"], 1)
            dve.wait_ge(S["y_in"], 16)
            dve.wait_ge(S["r_in"], 16)
            then(nc.vector.memset(rel_b[:, TILES:EB * P], -1.0))
            then(nc.vector.tensor_copy(y_f[:, :], y_i[:, :]))
            then(nc.vector.tensor_single_scalar(wy_i[:, :], y_i[:, :], 7, ALU.arith_shift_right))
            then(nc.vector.tensor_scalar(is_y[:, :], node_id[:, :], y_f[:, 0:1], None, ALU.is_equal))
            then(nc.vector.tensor_scalar(not_y[:, :], is_y[:, :], -1.0, 1.0, ALU.mult, ALU.add))
            then(nc.vector.tensor_reduce(mine_y[:, :], is_y[:, :], AX.X, ALU.add))
            then(nc.vector.tensor_scalar(r_y[:, :], r_rows[:, :], mine_y[:, 0:1], None, ALU.mult))
            then(nc.vector.tensor_scalar(invalid[:, :], node_id[:, :], float(N), -3.0e38, ALU.is_ge, ALU.mult))
            then(nc.vector.tensor_scalar(tok_id[:, :], node_id[:, :], 1.0, None, ALU.add))
            then(nc.vector.memset(taken_i[:, :], 0))

            def count_first(q, half):
                w = q * ZC + half * U
                dve.wait_ge(S[f"first_in{half}"], q * (16 * U) + 16 * U)
                nc.vector.tensor_tensor(is_less, first_rows[:, half, :, :],
                                        node_id[:, bass.ds(w, U)].unsqueeze(2).to_broadcast([P, U, P]), ALU.is_lt).then_inc(S["less_ok"], 1)
                dve.wait_ge(S["less_ok"], q * 2 + (half + 1))
                nc.vector.tensor_reduce(n_less[:, bass.ds(w, U)], is_less, AX.X, ALU.add).then_inc(S["first_used"], 1)
                dve.wait_ge(S["first_used"], q * 2 + (half + 1))

            for c in range(NZC):
                dve.wait_ge(x_chunk[c], 16 * (KD + (c == NZC - 1)))
                with dve.Fori(0, 2) as h:
                    for i in range(U):
                        w = h * U + (c * ZC + i)
                        nc.vector.bn_stats(bn1[:, bass.ds(w, 1), :].rearrange("p o s -> p (o s)"), nodes[:, :, w, :]).then_inc(S["bn1_ok"], 1)
                count_first(c // 2, c % 2)
            dve.wait_ge(S["bn1_ok"], NW)
            then(nc.vector.tensor_tensor(neg_mean[:, :], bn1[:, :, 1], bn1[:, :, 4], ALU.add))
            then(nc.vector.tensor_scalar(neg_mean[:, :], neg_mean[:, :], -0.5, None, ALU.mult))
            then(nc.vector.tensor_tensor(gap2[:, :], bn1[:, :, 1], bn1[:, :, 4], ALU.subtract))
            then(nc.vector.tensor_tensor(gap2[:, :], gap2[:, :], gap2[:, :], ALU.mult))
            then(nc.vector.tensor_tensor(var2[:, :], bn1[:, :, 2], bn1[:, :, 5], ALU.add))
            then(nc.vector.tensor_scalar(var2[:, :], var2[:, :], 1.0 / D, EPS, ALU.mult, ALU.add))
            then(nc.vector.scalar_tensor_tensor(var2[:, :], gap2[:, :], 0.25, var2[:, :], ALU.mult, ALU.add))
            dve.sem_inc(S["ssum"], 1)
            for b in range(NZC, 2 * NZC):
                count_first(b // 2, b % 2)
                if b > NZC:
                    dve.wait_ge(S["shift_ok"], 1)
                    wins = slice(ACT_WIN + (b - NZC - 1) * U, ACT_WIN + (b - NZC) * U)
                    for scale, op in ((rstd, ALU.mult), (shift, ALU.add)):
                        for k in range(KD):
                            ins = nc.vector.tensor_tensor(nodes[:, k, wins, :], nodes[:, k, wins, :],
                                                          scale[:, wins].unsqueeze(2).to_broadcast([P, U, P]), op)
                            if k == 0:
                                ins.then_inc(S["dve_ch"], 1)
                                ch[0] += 1
                        then(ins)
            then(nc.vector.scalar_tensor_tensor(row_start[:, 0:NW], first_f[:, :], float(P), n_less[:, :], ALU.mult, ALU.add))
            then(nc.vector.memset(row_start[:, NW:NW + 1], float(E)))
            dve.sem_inc(S["starts_ok"], 1)
            dve.wait_ge(S["starts_ps"], 3)
            then(nc.vector.tensor_tensor(deg[:, :], bank[1][:, 0:NW], row_start[:, 0:NW], ALU.subtract))

            def one_hots(s, j):
                t0 = s * 16
                nc.vector.tensor_tensor(oh_lo[:, j, :, :], iota_b[:, :].unsqueeze(1).to_broadcast([P, 16, P]),
                                        lo_b[:, bass.ds(t0, 16)].unsqueeze(2).to_broadcast([P, 16, P]),
                                        ALU.is_equal).then_inc(S["hist_built"], 1)
                nc.vector.tensor_tensor(oh_hi[:, j, :, :], iota_b[:, 0:NW].unsqueeze(1).to_broadcast([P, 16, NW]),
                                        hi_b[:, bass.ds(t0, 16)].unsqueeze(2).to_broadcast([P, 16, NW]),
                                        ALU.is_equal).then_inc(S["hist_built"], 1)
            n_unsorted = dve.value_load(unsorted_i[0:1, 0:1], min_val=0, max_val=2 * E)
            with dve.If(n_unsorted > 0):
                nc.vector.tensor_copy(dst_i[:, :], dst_f[:, :]).then_inc(S["hist_start"], 1)
                dve.wait_ge(S["hist_start"], 1)
                nc.vector.tensor_single_scalar(low_i[:, :], dst_i[:, :], 127, ALU.bitwise_and).then_inc(S["hist_start"], 1)
                dve.wait_ge(S["hist_start"], 2)
                nc.vector.tensor_copy(lo_b[:, :], low_i[:, :]).then_inc(S["hist_start"], 1)
                dve.wait_ge(S["hist_start"], 3)
                nc.vector.tensor_single_scalar(low_i[:, :], dst_i[:, :], 7, ALU.arith_shift_right).then_inc(S["hist_start"], 1)
                dve.wait_ge(S["hist_start"], 4)
                nc.vector.tensor_copy(hi_b[:, :], low_i[:, :]).then_inc(S["hist_start"], 1)
                dve.wait_ge(S["hist_start"], 5)
                one_hots(0, 0)
                one_hots(1, 1)
                with dve.Fori(1, HSTEPS // 2) as q:
                    for j in range(2):
                        dve.wait_ge(S["hist_used"], q * 2 + (j - 1))
                        one_hots(q * 2 + j, j)
                dve.wait_ge(S["hist_ps"], 1)
                nc.vector.tensor_copy(deg[:, :], bank[5][:, 0:NW]).then_inc(S["hist_start"], 1)
                dve.wait_ge(S["hist_start"], 6)
            then(nc.vector.tensor_tensor(deg[:, :], deg[:, :], not_y[:, :], ALU.mult))
            then(nc.vector.scalar_tensor_tensor(deg[:, :], is_y[:, :], float(TOPK), deg[:, :], ALU.mult, ALU.add))
            nc.vector.tensor_scalar(deg[:, :], deg[:, :], SELF_W, None, ALU.add).then_inc(S["deg_ok"], 1)
            wy = dve.value_load(wy_i[0:1, 0:1], min_val=0, max_val=NW - 1)
            dve.wait_ge(S["mem_ok"], 1)
            for k in range(KD):
                nc.vector.tensor_tensor(nodes[:, k, bass.ds(wy, 1), :], nodes[:, k, bass.ds(wy, 1), :],
                                        r_y[:, k * P:(k + 1) * P].unsqueeze(1), ALU.add).then_inc(S["mem_patched"], 1)
            dve.wait_ge(S["mem_patched"], KD)
            def differ(b):
                if b >= 2:
                    dve.wait_ge(S["dist_ok"], b - 1)
                for k in range(KD):
                    nc.vector.tensor_tensor(diff[:, b % 2, :, k, :], nodes[:, k, b * U:(b + 1) * U, :],
                                            r_rows[:, k * P:(k + 1) * P].unsqueeze(1).to_broadcast([P, U, P]),
                                            ALU.subtract).then_inc(S["diff_ok"], 1)
                if b >= 1:
                    sum_squares(b - 1)

            def sum_squares(b):
                dve.wait_ge(S["square_ok"], b + 1)
                nc.vector.tensor_reduce(dist[:, b * U:(b + 1) * U], diff[:, b % 2, :, :, :], AX.XY, ALU.add).then_inc(S["dist_ok"], 1)

            AHEAD = 3
            for b in range(2 * AHEAD):
                differ(b)
            dve.wait_ge(S["deg_ok"], 2)
            for c in range(NZC):
                dve.wait_ge(S["diff_ok"], 2 * KD * (c + 1))
                for k in range(KD):
                    rows = nodes[:, k, c * ZC:(c + 1) * ZC, :]
                    ins = nc.vector.tensor_tensor(rows, rows, dinv[:, c * ZC:(c + 1) * ZC].unsqueeze(2).to_broadcast([P, ZC, P]),
                                                  ALU.mult)
                ins.then_inc(S["z_ok"], 1)
                if c + AHEAD < NZC:
                    differ(2 * (c + AHEAD))
                    differ(2 * (c + AHEAD) + 1)
            sum_squares(2 * NZC - 1)

            for c in range(NZC):
                dve.wait_ge(table_out[c], 16 * KD)
                with dve.Fori(0, 2) as h:
                    for j in range(U):
                        dve.wait_ge(S["zT_ps"], h * U + (c * ZC + j + 1))
                        nc.vector.tensor_scalar(nodes[:, :, h * U + (c * ZC + j), :], bank[j][:, 0:D].rearrange("p (k c) -> p k c", k=KD),
                                                SELF_W, None, ALU.mult).then_inc(S["agg_init"], 1)
            dve.wait_ge(S["agg_init"], NW)
            ycol = dve.value_load(y_i[0:1, 0:1], min_val=0, max_val=N - 1)
            then(nc.vector.tensor_copy(col_fix[:, :], agg[:, :, bass.ds(ycol, 1)].rearrange("p k o -> p (k o)")))
            dve.wait_ge(S["dist_ok"], 2 * NZC)
            then(nc.vector.scalar_tensor_tensor(near[:, :], dist[:, :], -1.0, not_y[:, :], ALU.mult, ALU.mult))
            then(nc.vector.tensor_tensor(near[:, :], near[:, :], invalid[:, :], ALU.add))
            then(nc.vector.max(near8[:, :], near[:, :]))
            dve.sem_inc(S["near_ok"], 1)
            dve.wait_ge(S["near_ps"], 1)
            nc.vector.tensor_copy(near_row[0:1, 0:4 * P], bank[0][0:1, :])
            then(nc.vector.tensor_copy(near_row[0:1, 4 * P:8 * P], bank[1][0:1, :]))
            dve.drain()
            then(nc.vector.max(top8[:, :], near_row[:, :]))
            dve.sem_inc(S["near_ok"], 1)
            dve.wait_ge(S["near_ps"], 2)
            then(nc.vector.tensor_copy(thr[:, :], bank[2][:, 0:1]))
            then(nc.vector.tensor_scalar(above[:, :], near[:, :], thr[:, 0:1], None, ALU.is_gt))
            then(nc.vector.tensor_scalar(tied[:, :], near[:, :], thr[:, 0:1], None, ALU.is_equal))
            then(nc.vector.tensor_reduce(n_above[:, :], above[:, :], AX.X, ALU.add))
            dve.sem_inc(S["near_ok"], 1)
            dve.wait_ge(S["near_ps"], 3)
            then(nc.vector.tensor_scalar(room[:, :], bank[2][:, 1:2], -1.0, float(TOPK), ALU.mult, ALU.add))
            then(nc.vector.tensor_tensor_scan(tie_scan[:, :], ones[:, 0:NW], bank[3][:, NW:2 * NW], 0.0, ALU.mult, ALU.add))
            then(nc.vector.tensor_tensor(tie_rank[:, :], tie_scan[:, :], bank[3][:, NW:2 * NW], ALU.subtract))
            then(nc.vector.tensor_tensor(tie_rank[:, :], tie_rank[:, :], bank[3][:, 0:NW], ALU.add))
            then(nc.vector.tensor_scalar(tie_rank[:, :], tie_rank[:, :], room[:, 0:1], None, ALU.is_le))
            then(nc.vector.tensor_tensor(chosen[:, :], tied[:, :], tie_rank[:, :], ALU.mult))
            then(nc.vector.tensor_tensor(chosen[:, :], chosen[:, :], above[:, :], ALU.add))
            dve.sem_inc(S["chosen_ok"], 1)

            def select(g, j):
                nc.vector.tensor_tensor(sel[:, j, :, :], iota_b[:, :].unsqueeze(1).to_broadcast([P, GT, P]),
                                        rel_b[:, bass.ds(g * GT, GT)].unsqueeze(2).to_broadcast([P, GT, P]),
                                        ALU.is_equal).then_inc(S["sel_ok"], 1)

            def add_group(g, j, first):
                base = dve.value_load(base_i[0:1, bass.ds(g, 1)], min_val=0, max_val=(NW - 1) * P)
                if not first:
                    dve.wait_ge(S["agg_added"], g)
                dve.wait_ge(S["agg_ps"], g + 1)
                where = agg[:, :, bass.ds(base, P)]
                nc.vector.tensor_tensor(where, where, bank[j][:, 0:D].rearrange("p (k c) -> p k c", k=KD),
                                        ALU.add).then_inc(S["agg_added"], 1)

            select(0, 0)
            select(1, 1)
            add_group(0, 0, True)
            with dve.Fori(0, (GROUPS - 2) // 2) as q:
                for j in range(2):
                    dve.wait_ge(S["agg_ps"], q * 2 + j + 1)
                    select(q * 2 + (j + 2), j)
                    add_group(q * 2 + (j + 1), (j + 1) % 2, False)
            add_group(GROUPS - 1, 1, False)
            dve.wait_ge(S["agg_added"], GROUPS)
            n_bad = dve.value_load(bad_i[0:1, 0:1], min_val=0, max_val=GROUPS)
            with dve.If(n_bad > 0):
                dve.sem_inc(S["rep_bad"], 1)
                dve.wait_ge(S["rep_dst"], 1)
                nc.vector.tensor_scalar(grp_far, bank[4][:, 0:GROUPS], -FAR, FAR, ALU.mult, ALU.add).then_inc(S["rep_bad"], 1)
                dve.wait_ge(S["rep_bad"], 2)
                by_group = dst_f[:, 0:TILES].rearrange("p (g t) -> p g t", t=GT)
                nc.vector.tensor_tensor(by_group, by_group, grp_far.unsqueeze(2).to_broadcast([P, GROUPS, GT]),
                                        ALU.add).then_inc(S["rep_bad"], 1)
                dve.wait_ge(S["rep_bad"], 3)
                with dve.Fori(0, GROUPS) as g:
                    with dve.Fori(0, NW) as w:
                        nc.vector.tensor_scalar(rep_rel[:, :], dst_f[:, bass.ds(g * GT, GT)], win_f[:, bass.ds(w, 1)], None,
                                                ALU.subtract).then_inc(S["rep_relok"], 1)
                        dve.wait_ge(S["rep_relok"], g * NW + (w + 1))
                        nc.vector.tensor_tensor(sel[:, 0, :, :], iota_b[:, :].unsqueeze(1).to_broadcast([P, GT, P]),
                                                rep_rel[:, :].unsqueeze(2).to_broadcast([P, GT, P]),
                                                ALU.is_equal).then_inc(S["rep_sel"], 1)
                        where = agg[:, :, bass.ds(w * P, P)]
                        dve.wait_ge(S["rep_ps"], g * NW + (w + 1))
                        nc.vector.tensor_tensor(where, where, bank[0][:, 0:D].rearrange("p (k c) -> p k c", k=KD),
                                                ALU.add).then_inc(S["rep_added"], 1)
                        dve.wait_ge(S["rep_added"], g * NW + (w + 1))
            dve.wait_ge(S["selps"], 1)
            then(nc.vector.tensor_tensor(agg[:, :, bass.ds(ycol, 1)].rearrange("p k o -> p (k o)"), col_fix[:, :],
                                         bank[3][:, 0:KD], ALU.add))
            dve.sem_inc(S["fixed"], 1)

            dve.wait_ge(S["b1_ps"], 1)
            nc.vector.tensor_copy(b1_cols, bank[4][:, 0:NE * FT]).then_inc(S["b1_ok"], 1)
            dve.wait_ge(S["aggst_ok"], 1)
            def residual(q, j):
                w = q * U + j
                dve.wait_ge(S["conv_ps"], w + 1)
                dve.wait_ge(S[f"xt_in{j}"], q * 16 + 16)
                nc.vector.scalar_tensor_tensor(nodes[:, :, w, :], bank[j][:, 0:D].rearrange("p (k c) -> p k c", k=KD),
                                               dinv[:, bass.ds(w, 1)], x_tile[:, j, :].rearrange("p (k c) -> p k c", k=KD),
                                               ALU.mult, ALU.add).then_inc(S["x1_ok"], 1)

            def stats(q, j):
                dve.wait_ge(S["x1_ok"], q * U + j + 1)
                dve.sem_inc(S["tick"], 1)
                nc.vector.bn_stats(bn[:, bass.ds(q * U + j, 1), :].rearrange("p o s -> p (o s)"),
                                   nodes[:, :, q * U + j, :]).then_inc(S["bn_ok"], 1)
            with dve.Fori(0, NU) as q:
                for j in range(U + 1):
                    if j < U:
                        residual(q, j)
                    if j:
                        stats(q, j - 1)
            dve.wait_ge(S["bn_ok"], NW)
            then(nc.vector.tensor_tensor(mean2[:, :], bn[:, :, 1], bn[:, :, 4], ALU.add))
            then(nc.vector.tensor_tensor(gap2[:, :], bn[:, :, 1], bn[:, :, 4], ALU.subtract))
            then(nc.vector.tensor_tensor(gap2[:, :], gap2[:, :], gap2[:, :], ALU.mult))
            then(nc.vector.tensor_tensor(var2[:, :], bn[:, :, 2], bn[:, :, 5], ALU.add))
            then(nc.vector.tensor_scalar(var2[:, :], var2[:, :], 1.0 / D, EPS, ALU.mult, ALU.add))
            nc.vector.scalar_tensor_tensor(var2[:, :], gap2[:, :], 0.25, var2[:, :], ALU.mult, ALU.add).then_inc(S["var_ok"], 1)
            dve.wait_ge(S["var_ok"], 2)
            then(nc.vector.scalar_tensor_tensor(shift2[:, :], mean2[:, :], -0.5, rstd2[:, :], ALU.mult, ALU.mult))
            dve.sem_inc(S["lnb_ok"], 1)
            def feat(w, j, first):
                dve.wait_ge(S["hT_ps"], w + 1)
                if not first:
                    dve.wait_ge(S["logit_ps"], w - U + 1)
                nc.vector.tensor_copy(h_feat[:, j, :, :], bank[turn_bank(j)][:, 0:D].rearrange("p (k c) -> p k c", k=KD)).then_inc(S["hT_ok"], 1)
            def take_logits(step, half):
                dve.wait_ge(S["logit_ps"], step * U + U)
                nc.vector.tensor_copy(gate_l[:, bass.ds(step * U, U), :],
                                      bank[6 + half][:, 0:U * NE].rearrange("p (w e) -> p w e", e=NE)).then_inc(S["gate_taken"], 1)
            def norm_ahead(q, i):
                if i % ZC in DVE_NORM:
                    w = q * ZC + i
                    nc.vector.tensor_scalar(h_tile[:, i % U, :, :], nodes[:, :, w, :], rstd2[:, bass.ds(w, 1)],
                                            shift2[:, bass.ds(w, 1)], ALU.mult, ALU.add).then_inc(S["h_dve"], 1)

            def gate_windows(q, first, last):
                for half in range(2):
                    for j in range(U):
                        feat(q * ZC + (half * U + j), j, first and half == 0)
                        if not (last and half == 1):
                            norm_ahead(q, half * U + j + U)
                    if not (first and half == 0):
                        take_logits(q * 2 + (half - 1), 1 - half)
            for i in range(U):
                norm_ahead(0, i)
            gate_windows(0, True, False)
            with dve.Fori(1, NZC - 1) as q:
                gate_windows(q, False, False)
            gate_windows(NZC - 1, False, True)
            take_logits(NU - 1, 1)
            dve.wait_ge(S["gate_taken"], NU)

            def over(ap):
                return ap.unsqueeze(2).to_broadcast([P, NW, NE])
            def per_expert(ap):
                return ap.unsqueeze(1).to_broadcast([P, NW, NE])
            then(nc.vector.tensor_tensor(gate_l, gate_l, per_expert(gateb_sb[:, :]), ALU.add))
            then(nc.vector.tensor_reduce(best[:, :], gate_l, AX.X, ALU.max))
            then(nc.vector.tensor_tensor(gate_l, gate_l, over(best[:, :]), ALU.subtract))
            dve.sem_inc(S["gate_in"], 1)
            then(nc.vector.tensor_copy(iota_f[:, :], iota_i[:, 0:NE]))
            then(nc.vector.tensor_scalar(rank_e[:, :], iota_f[:, :], -1.0, float(NE), ALU.mult, ALU.add))
            dve.wait_ge(S["gate_out"], 1)
            then(nc.vector.tensor_reduce(norm[:, :], gate_e, AX.X, ALU.add))
            then(nc.vector.reciprocal(norm[:, :], norm[:, :]))
            then(nc.vector.tensor_tensor(gate_e, gate_e, over(norm[:, :]), ALU.mult))
            then(nc.vector.tensor_reduce(best[:, :], gate_e, AX.X, ALU.max))
            then(nc.vector.tensor_tensor(gate_t, gate_e, over(best[:, :]), ALU.is_equal))
            then(nc.vector.tensor_tensor(gate_t, gate_t, per_expert(rank_e[:, :]), ALU.mult))
            then(nc.vector.tensor_reduce(expert[:, :], gate_t, AX.X, ALU.max))
            then(nc.vector.tensor_tensor(pick, gate_t, over(expert[:, :]), ALU.is_equal))
            then(nc.vector.tensor_scalar(kept[:, :], invalid[:, :], 0.0, None, ALU.is_ge))
            then(nc.vector.tensor_tensor(pick, pick, over(kept[:, :]), ALU.mult))
            dve.sem_inc(S["pick_ok"], 1)
            dve.wait_ge(S["rank_ps"], 1)
            HW = NW // 2
            for i in range(2):
                rows = slice(i * HW, (i + 1) * HW)
                then(nc.vector.tensor_copy(gate_t[:, rows, :], bank[2 + i][:, 0:HW * NE].rearrange("p (w e) -> p w e", e=NE)))
            for e in range(NE):
                then(nc.vector.tensor_tensor_scan(gate_l[:, :, e], ones[:, 0:NW], gate_t[:, :, e], 0.0, ALU.mult, ALU.add))
            then(nc.vector.tensor_copy(taken_f[0:1, :], gate_l[0:1, NW - 1, :]))
            then(nc.vector.tensor_copy(taken_i[0:1, 0:NE], taken_f[0:1, :]))
            then(nc.vector.tensor_tensor(gate_l, gate_l, gate_t, ALU.subtract))
            for i in range(2):
                rows = slice(i * HW, (i + 1) * HW)
                then(nc.vector.tensor_tensor(gate_l[:, rows, :], gate_l[:, rows, :],
                                             bank[i][:, 0:HW * NE].rearrange("p (w e) -> p w e", e=NE), ALU.add))
            then(nc.vector.tensor_tensor(gate_l, gate_l, pick, ALU.mult))
            then(nc.vector.tensor_reduce(place[:, :], gate_l, AX.X, ALU.add))
            then(nc.vector.tensor_scalar(expert[:, :], expert[:, :], -1.0, float(NE), ALU.mult, ALU.add))
            then(nc.vector.tensor_scalar(norm[:, :], place[:, :], float(CAP), None, ALU.is_le))
            then(nc.vector.tensor_tensor(kept[:, :], kept[:, :], norm[:, :], ALU.mult))
            then(nc.vector.tensor_tensor(weight[:, :], best[:, :], kept[:, :], ALU.mult))
            then(nc.vector.tensor_scalar(place[:, :], place[:, :], float(CAP), -1.0, ALU.min, ALU.add))
            then(nc.vector.scalar_tensor_tensor(slot_f[:, :], expert[:, :], float(CAP), place[:, :], ALU.mult, ALU.add))
            then(nc.vector.tensor_scalar(kept[:, :], kept[:, :], -FAR, FAR, ALU.mult, ALU.add))
            then(nc.vector.tensor_tensor(slot_f[:, :], slot_f[:, :], kept[:, :], ALU.add))
            then(nc.vector.tensor_copy(put_idx[:, :], slot_f[:, :]))
            dve.sem_inc(S["routed"], 1)

            def send_parts(q, first):
                for half in range(2):
                    if not first:
                        dve.wait_ge(S[f"sent{half}"], q * (16 * U))
                    rows, wins = slice(half * U, (half + 1) * U), bass.ds(q * ZC + half * U, U)
                    nc.vector.tensor_copy(h_send[:, rows, TOK], tok_id[:, wins]).then_inc(S["ids_ok"], 1)
                    nc.vector.tensor_copy(h_send[:, rows, GATE], weight[:, wins]).then_inc(S["ids_ok"], 1)
                    dve.wait_ge(S["ids_ok"], q * 4 + 2 * (half + 1))
                    dve.sem_inc(S["send_ids"], 1)
                    for s in range(half * U, (half + 1) * U):
                        nc.vector.tensor_copy(h_send[:, s, D:2 * D].rearrange("p (k c) -> p k c", k=KD),
                                              nodes[:, :, q * ZC + s, :]).then_inc(S["send_x"], 1)
            send_parts(0, True)
            with dve.Fori(1, NZC) as q:
                send_parts(q, False)

            def feats(q, s, took):
                n = CHUNKS[s % NCH][1]
                with dve.If(took > CHUNKS[s % NCH][0]):
                    dve.wait_ge(S["xT_ps"], q * PC + (s + 2))
                    dve.wait_ge(S["l1_ps"], q * (PC * FB2) + (s + 1) * FB2)
                    nc.vector.tensor_copy(xs_feat[:, s % 2, :, 0:n],
                                          bank[s % 2].rearrange("p (k c) -> p k c", k=KD)[:, :, 0:n]).then_inc(S["xT_ok"], 1)
                with dve.Else():
                    dve.wait_ge(S["xT_ok"], q * PC + (s + 2))
                    dve.sem_inc(S["xT_ok"], 1)

            BIG = 3.4028234e38
            STEPS_ROW = 10

            def slot_free(q, s, slot):
                if s < 2:
                    dve.wait_ge(S["pair_sent"], q + 1)
                else:
                    dve.wait_ge(S[f"out_done{slot}"], q * (16 * NCH) + 16 * (s // 2))

            def results(q, s, took):
                j, c = s // NCH, s % NCH
                with dve.If(took > CHUNKS[c][0]):
                    for t in range(2):
                        n, slot = min(P, CHUNKS[c][1] - t * P), s % 2 * 2 + t
                        token = xs_rows[0:n, s % XSLOTS, t, :]
                        at_step = [0]

                        def step(ins):
                            at_step[0] += 1
                            ins.then_inc(S["row_step"], 1)

                        def done():
                            dve.wait_ge(S["row_step"], q * (2 * PC * STEPS_ROW) + ((2 * s + t) * STEPS_ROW + at_step[0]))
                        dve.wait_ge(S["l2_ps"], q * (2 * PC) + (2 * s + t + 3))
                        nc.vector.tensor_tensor(y_row[0:n, :], bank[4 + t][0:n, 0:D],
                                                b2_rows[0:n, bass.ds(q * 2 + j, 1), :].rearrange("p o d -> p (o d)"),
                                                ALU.add).then_inc(S["y_ok"], 1)
                        dve.wait_ge(S["y_ok"], q * (2 * PC) + (2 * s + t + 3))
                        step(nc.vector.tensor_scalar(y_row[0:n, :], y_row[0:n, :], token[:, GATE:GATE + 1], None, ALU.mult))
                        slot_free(q, s, slot)
                        step(nc.vector.tensor_scalar(out_miss[0:n, slot:slot + 1], token[:, TOK:TOK + 1], 0.0, FAR, ALU.is_equal, ALU.mult))
                        step(nc.vector.tensor_scalar(out_f[0:n, slot:slot + 1], token[:, TOK:TOK + 1], -1.0, None, ALU.add))
                        done()
                        step(nc.vector.tensor_tensor(out_f[0:n, slot:slot + 1], out_f[0:n, slot:slot + 1], out_miss[0:n, slot:slot + 1], ALU.add))
                        step(nc.vector.tensor_scalar(y_low[0:n, :], y_row[0:n, :], -BIG, -1.0e4, ALU.is_lt, ALU.mult))
                        step(nc.vector.tensor_scalar(y_high[0:n, :], y_row[0:n, :], BIG, 1.0e4, ALU.is_gt, ALU.mult))
                        step(nc.vector.tensor_scalar(y_fin[0:n, :], y_row[0:n, :], 0.0, 0.0, ALU.mult, ALU.is_equal))
                        done()
                        step(nc.vector.tensor_copy(out_idx[0:n, slot:slot + 1], out_f[0:n, slot:slot + 1]))
                        step(nc.vector.tensor_tensor(y_high[0:n, :], y_high[0:n, :], y_low[0:n, :], ALU.add))
                        done()
                        dve.sem_inc(S["tick"], 1)
                        step(nc.vector.copy_predicated(y_high[0:n, :], y_fin[0:n, :], y_row[0:n, :]))
                        done()
                        nc.vector.tensor_tensor(o_tile[0:n, slot, :], token[:, D:2 * D], y_high[0:n, :], ALU.add).then_inc(S["res_ok"], 1)
                    dve.sem_inc(S["no_token"], 2)
                with dve.Else():
                    dve.wait_ge(S["res_ok"], q * (2 * PC) + (2 * s + 2))
                    for slot in (s % 2 * 2, s % 2 * 2 + 1):
                        slot_free(q, s, slot)
                        nc.vector.memset(out_idx[:, slot:slot + 1], int(FAR)).then_inc(S["no_token"], 1)
                    dve.wait_ge(S["no_token"], q * (2 * PC) + (2 * s + 2))
                    dve.sem_inc(S["row_step"], 2 * STEPS_ROW)
                    dve.sem_inc(S["y_ok"], 2)
                    dve.sem_inc(S["res_ok"], 2)

            for half in range(2):
                dve.wait_ge(S[f"sent{half}"], 16 * U * NZC)
            then(nc.vector.memset(o_tile, 0.0))
            dve.sem_inc(S["res_ok"], 2)
            dve.sem_inc(S["xT_ok"], 2)
            dve.sem_inc(S["y_ok"], 2)
            feats(0, 0, dve.value_load(taken_i[0:1, 0:1], min_val=0, max_val=N))
            with dve.Fori(0, NE // 2) as q:
                took = [dve.value_load(taken_i[0:1, bass.ds(q * 2 + i, 1)], min_val=0, max_val=N) for i in range(3)]
                for s in range(PC):
                    feats(q, s + 1, took[(s + 1) // NCH])
                    results(q, s, took[s // NCH])


        @block.tensor
        def _(pe):
            pe.wait_ge(S["consts"], 7)
            for n, (i, b0, nb) in enumerate(EDGE_TURNS):
                pe.wait_ge(S["edges_float"], i + 1)
                if n >= 2:
                    pe.wait_ge(S["edges_out"], n - 1)
                for b in range(nb):
                    last = nc.tensor.transpose(bank[n % 2][:, b * P:(b + 1) * P], stage_f[:, i, b0 + b, :], ident[:, :])
                last.then_inc(S["edge_psum"], 1)
            pe.wait_ge(S["lims"], 1)
            for n, (i, b0, nb) in enumerate(EDGE_TURNS):
                if n >= 2:
                    pe.wait_ge(S["lim_rows"], n - 1)
                for b in range(nb):
                    last = nc.tensor.matmul(bank[2 + n % 2][0:1, b * P:(b + 1) * P], tile_lim[:, i, b0 + b:b0 + b + 1],
                                            ident[:, :], start=True, stop=True)
                last.then_inc(S["limps"], 1)
            pe.wait_ge(S["bases"], 1)
            nc.tensor.matmul(bank[4][:, 0:GROUPS], ones[0:1, :], grp_cmp[0:1, :], start=True, stop=True)
            nc.tensor.matmul(bank[4][0:1, GROUPS:GROUPS + 1], disorder[:, :], ones[:, 0:1], start=True, stop=True).then_inc(S["cmp_ps"], 1)

            pe.wait_ge(S["last_built"], 2)
            for b in range(EB):
                last = nc.tensor.matmul(bank[5][:, 0:NW], oh_lo[:, 0, b, :], oh_hi[:, 0, b, :], start=(b == 0), stop=(b == EB - 1))
            last.then_inc(S["starts_ps"], 1)
            pe.wait_ge(S["starts_ok"], 1)
            nc.tensor.matmul(bank[0][:, 0:NW], tri[:, :], last_hist[:, :], start=True, stop=True)
            nc.tensor.matmul(bank[0][:, NW:2 * NW], ones[:, :], last_hist[:, :], start=True, stop=True).then_inc(S["starts_ps"], 1)
            pe.wait_ge(S["starts_ok"], 2)
            nc.tensor.matmul(bank[1][:, 0:NW], down_one[:, :], row_start[:, 0:NW], start=True, stop=False)
            nc.tensor.matmul(bank[1][:, 0:NW], corner[:, :], row_start[:, 1:NW + 1], start=False, stop=True).then_inc(S["starts_ps"], 1)

            n_unsorted = pe.value_load(unsorted_i[0:1, 0:1], min_val=0, max_val=2 * E)
            with pe.If(n_unsorted > 0):
                nc.tensor.matmul(bank[5][:, 0:NW], zeros[:, 0:P], zeros[:, 0:NW], start=True, stop=False)
                with pe.Fori(0, HSTEPS // 2) as q:
                    for j in range(2):
                        pe.wait_ge(S["hist_built"], q * 4 + 2 * (j + 1))
                        for t in range(16):
                            last = nc.tensor.matmul(bank[5][:, 0:NW], oh_lo[:, j, t, :], oh_hi[:, j, t, :], start=False, stop=False)
                        last.then_inc(S["hist_used"], 1)
                nc.tensor.matmul(bank[5][:, 0:NW], zeros[:, 0:P], zeros[:, 0:NW], start=False, stop=True).then_inc(S["hist_ps"], 1)

            def start_window(w, j):
                for k in range(KD):
                    last = nc.tensor.transpose(bank[j][:, k * P:(k + 1) * P], z_stat[:, j, k, :], ident[:, :])
                last.then_inc(S["zT_ps"], 1)
            for j in range(U):
                pe.wait_ge(S["zstat_ok"], j + 1)
                start_window(j, j)
            with pe.Fori(1, NU) as q:
                for j in range(U):
                    pe.wait_ge(S["zstat_ok"], q * U + j + 1)
                    pe.wait_ge(S["agg_init"], q * U + (j - U + 1))
                    start_window(q * U + j, j)

            pe.wait_ge(S["near_ok"], 1)
            for i in range(8):
                last = nc.tensor.matmul(bank[i // 4][0:1, (i % 4) * P:(i % 4 + 1) * P], near8[:, i:i + 1], ident[:, :],
                                        start=True, stop=True)
            last.then_inc(S["near_ps"], 1)
            pe.wait_ge(S["near_ok"], 2)
            nc.tensor.matmul(bank[2][:, 0:1], ones[0:1, :], top8[0:1, TOPK - 1:TOPK], start=True, stop=True).then_inc(S["near_ps"], 1)
            pe.wait_ge(S["near_ok"], 3)
            nc.tensor.matmul(bank[2][:, 1:2], ones[:, :], n_above[:, :], start=True, stop=True)
            nc.tensor.matmul(bank[3][:, 0:NW], tri[:, :], tied[:, :], start=True, stop=True)
            nc.tensor.matmul(bank[3][:, NW:2 * NW], ones[:, :], tied[:, :], start=True, stop=True).then_inc(S["near_ps"], 1)

            pe.wait_ge(S["chosen_ok"], 1)
            nc.tensor.matmul(bank[3][:, 0:KD], zeros[:, 0:P], zeros[:, 0:KD], start=True, stop=False)

            def chosen_rows(q):
                for j in range(2):
                    pe.wait_ge(S[f"zb_in{j}"], q * 16 + 16)
                    for k in range(KD):
                        last = nc.tensor.matmul(bank[3][:, k:k + 1], z_back[:, j, k * P:(k + 1) * P], chosen[:, bass.ds(q * 2 + j, 1)],
                                                start=False, stop=False)
                    last.then_inc(S["zb_used"], 1)

            def group(g, q, slot, first):
                j = slot % 2
                pe.wait_ge(S["sel_ok"], g + 1)
                pe.wait_ge(gathered[slot], q * 64 + 64)
                if not first:
                    pe.wait_ge(S["agg_added"], g - 1)
                for k in range(KD):
                    for t in range(GT):
                        last = nc.tensor.matmul(bank[j][:, k * P:(k + 1) * P], gath[:, slot, t, k * P:(k + 1) * P],
                                                sel[:, j, t, :], start=(t == 0), stop=(t == GT - 1))
                last.then_inc(S["agg_ps"], 1)
            for slot in range(GS):
                group(slot, 0, slot, slot < 2)
            chosen_rows(0)
            with pe.Fori(1, GROUPS // GS) as q:
                for slot in range(GS):
                    group(q * GS + slot, q, slot, False)
                chosen_rows(q)
            nc.tensor.matmul(bank[3][:, 0:KD], zeros[:, 0:P], zeros[:, 0:KD], start=False, stop=True).then_inc(S["selps"], 1)

            n_bad = pe.value_load(bad_i[0:1, 0:1], min_val=0, max_val=GROUPS)
            with pe.If(n_bad > 0):
                pe.wait_ge(S["rep_bad"], 1)
                nc.tensor.matmul(bank[4][:, 0:GROUPS], ones[0:1, :], grp_bad[0:1, :], start=True, stop=True).then_inc(S["rep_dst"], 1)
                pe.sem_inc(S["rep_free"], 1)
                with pe.Fori(0, GROUPS) as g:
                    pe.wait_ge(S["rep_got"], g * (16 * GT) + 16 * GT)
                    pe.sem_inc(S["tick"], 1)
                    with pe.Fori(0, NW) as w:
                        pe.wait_ge(S["rep_sel"], g * NW + (w + 1))
                        for k in range(KD):
                            for t in range(GT):
                                last = nc.tensor.matmul(bank[0][:, k * P:(k + 1) * P], gath[:, 0, t, k * P:(k + 1) * P],
                                                        sel[:, 0, t, :], start=(t == 0), stop=(t == GT - 1))
                        last.then_inc(S["rep_ps"], 1)
                    pe.wait_ge(S["rep_ps"], g * NW + NW)
                    pe.sem_inc(S["rep_free"], 1)

            pe.wait_ge(S["w_small"], 5 * 16)
            nc.tensor.transpose(bank[4][:, 0:NE * FT], b1_rows[0:NE * FT, :], ident[0:NE * FT, 0:NE * FT]).then_inc(S["b1_ps"], 1)
            pe.wait_ge(S["b1_ok"], 1)
            def convolve(w, j, first):
                pe.wait_ge(S["aggst_ok"], w + 1)
                if not first:
                    pe.wait_ge(S["x1_ok"], w - U + 1)
                for k in range(KD):
                    last = nc.tensor.matmul(bank[j][:, 0:D], agg_stat[:, j, k, :], gnnw_sb[:, k, :], start=(k == 0), stop=(k == KD - 1))
                last.then_inc(S["conv_ps"], 1)
            for j in range(U):
                convolve(j, j, True)
            with pe.Fori(1, NU) as q:
                for j in range(U):
                    convolve(q * U + j, j, False)

            def turn_rows(q, i, first):
                w, j = q * ZC + i, i % U
                by, mine = ("h_dve", DVE_NORM) if i % ZC in DVE_NORM else ("h_ok", ACT_NORM)
                pe.wait_ge(S[by], q * len(mine) + (i // ZC * len(mine) + mine.index(i % ZC) + 1))
                if turn_bank(j) == 2:
                    if not (first and j == 2):
                        pe.wait_ge(S["hT_ok"], w - (3 if j == 6 else 2))
                elif not first:
                    pe.wait_ge(S["hT_ok"], w - U + 1)
                for k in range(KD):
                    last = nc.tensor.transpose(bank[turn_bank(j)][:, k * P:(k + 1) * P], h_tile[:, j, k, :], ident[:, :])
                last.then_inc(S["hT_ps"], 1)

            def logits(q, half, j, first):
                pe.wait_ge(S["hT_ok"], q * ZC + (half * U + j + 1))
                if j == 0 and not first:
                    pe.wait_ge(S["gate_taken"], q * 2 + (half - 1))
                for k in range(KD):
                    last = nc.tensor.matmul(bank[6 + half][:, j * NE:(j + 1) * NE], h_feat[:, j, k, :], gatew_sb[:, k, :],
                                            start=(k == 0), stop=(k == KD - 1))
                last.then_inc(S["logit_ps"], 1)

            def gate_step(q, half, first, last):
                for j in range(U):
                    logits(q, half, j, first)
                    if not last:
                        turn_rows(q, half * U + U + j, False)
            for j in range(U):
                turn_rows(0, j, True)
            gate_step(0, 0, True, False)
            gate_step(0, 1, True, False)
            with pe.Fori(1, NZC - 1) as q:
                gate_step(q, 0, False, False)
                gate_step(q, 1, False, False)
            gate_step(NZC - 1, 0, False, False)
            gate_step(NZC - 1, 1, False, True)

            pe.wait_ge(S["pick_ok"], 1)
            HW = NW // 2
            for i in range(2):
                rows = pick[:, i * HW:(i + 1) * HW, :].rearrange("p w e -> p (w e)")
                nc.tensor.matmul(bank[i][:, 0:HW * NE], tri[:, :], rows, start=True, stop=True)
                last = nc.tensor.matmul(bank[2 + i][:, 0:HW * NE], ones[:, :], rows, start=True, stop=True)
            last.then_inc(S["rank_ps"], 1)

            def turn_chunk(q, s):
                n = CHUNKS[s % NCH][1]
                pe.wait_ge(S[f"xs_in{s % XSLOTS}"], q * (32 * PC // XSLOTS) + (32 * (s // XSLOTS) + 32))
                pe.wait_ge(S["xT_ok"], q * PC + (s + 1))
                for k in range(KD):
                    for t in range(-(-n // P)):
                        m = min(P, n - t * P)
                        last = nc.tensor.transpose(bank[s % 2][:, k * CR + t * P:k * CR + t * P + m],
                                                   xs_rows[0:m, s % XSLOTS, t, k * P:(k + 1) * P], ident[0:m, 0:m])
                last.then_inc(S["xT_ps"], 1)

            def skip_turn(q, s):
                pe.wait_ge(S["xT_ps"], q * PC + (s + 1))
                pe.sem_inc(S["xT_ps"], 1)

            def up(q, s):
                j, n = s // NCH, CHUNKS[s % NCH][1]
                pe.wait_ge(S["xT_ok"], q * PC + (s + 3))
                if s % NCH == 0:
                    pe.wait_ge(S[f"w_in{j}"], q * 32 + 32)
                for b in range(FB2):
                    pe.wait_ge(S["hid_ok"], q * (PC * FT) + (s * FT + 2 * b + 2))
                    for i in range(2):
                        f = 2 * b + i
                        for k in range(KD):
                            last = nc.tensor.matmul(up_bank[b][:, i * CR:i * CR + n], w1_sb[:, j, k, f * P:(f + 1) * P],
                                                    xs_feat[:, s % 2, k, 0:n], start=(k == 0), stop=(k == KD - 1))
                    last.then_inc(S["l1_ps"], 1)

            def down(q, s):
                j, n = s // NCH, CHUNKS[s % NCH][1]
                for t in range(2):
                    m = min(P, n - t * P)
                    pe.wait_ge(S["y_ok"], q * (2 * PC) + (2 * s + t + 1))
                    for f in range(FT):
                        if t == 0 and f % 2 == 0:
                            pe.wait_ge(S["hid_ok"], q * (PC * FT) + ((s + 1) * FT + f + 2))
                        last = nc.tensor.matmul(bank[4 + t][0:m, 0:D], hid[:, f, t * P:t * P + m], w2_sb[:, j, f, :],
                                                start=(f == 0), stop=(f == FT - 1))
                    last.then_inc(S["l2_ps"], 1)

            pe.wait_ge(S["routed"], 1)
            pe.sem_inc(S["xT_ps"], 1)
            pe.sem_inc(S["l1_ps"], 2 * FB2)
            pe.sem_inc(S["l2_ps"], 2)

            def turn_or_skip(q, s, took):
                with pe.If(took > CHUNKS[s % NCH][0]):
                    turn_chunk(q, s)
                with pe.Else():
                    skip_turn(q, s)

            turn_or_skip(0, 0, pe.value_load(taken_i[0:1, 0:1], min_val=0, max_val=N))
            with pe.Fori(0, NE // 2) as q:
                took = [pe.value_load(taken_i[0:1, bass.ds(q * 2 + i, 1)], min_val=0, max_val=N) for i in range(3)]
                for s in range(PC):
                    inside = s % NCH < NCH - 1
                    with pe.If(took[s // NCH] > CHUNKS[s % NCH][0]):
                        up(q, s)
                        if inside:
                            turn_or_skip(q, s + 1, took[s // NCH])
                        down(q, s)
                    with pe.Else():
                        pe.wait_ge(S["l2_ps"], q * (2 * PC) + (2 * s + 2))
                        pe.sem_inc(S["l1_ps"], FB2)
                        pe.sem_inc(S["l2_ps"], 2)
                        if inside:
                            skip_turn(q, s + 1)
                    if not inside:
                        turn_or_skip(q, s + 1, took[(s + 1) // NCH])


_INS = ["x", "src", "dst", "L0_gnn_r", "L0_gnn_W", "L0_gnn_y", "L0_ffn_gate_w", "L0_ffn_gate_b",
        "L0_ffn_w1", "L0_ffn_b1", "L0_ffn_w2", "L0_ffn_b2"]


def kernel(**inputs):
    import numpy as np
    import concourse.bacc as bacc
    from concourse.bass_utils import run_bass_kernel_spmd as run

    nc = bacc.Bacc("TRN2", target_bir_lowering=False, num_devices=1)
    arrays, args = {}, []
    for name in _INS:
        v = np.ascontiguousarray(inputs[name])
        arrays[f"in_{name}"] = v
        args.append(nc.dram_tensor(f"in_{name}", v.shape, mybir.dt.from_np(v.dtype), kind="ExternalInput").ap())
    out = nc.dram_tensor("out", arrays["in_x"].shape, F32, kind="ExternalOutput").ap()
    build(nc, *args, out)
    r = run(nc, [arrays], core_ids=[0])
    return r.results[0]["out"]
```
